# Optimizing a Trainium2 kernel written in Bass

```python
import numpy as np
import jax
import jax.numpy as jnp

def _softmax(x, axis=-1):
    return jax.nn.softmax(x, axis=axis)

def _gelu(x):
    return jax.nn.gelu(x, approximate=True)

def _silu(x):
    return jax.nn.silu(x)

def _sigmoid(x):
    return jax.nn.sigmoid(x)

def _layernorm(x, axis=-1, eps=1e-05):
    m = jnp.mean(x, axis=axis, keepdims=True)
    v = jnp.var(x, axis=axis, keepdims=True)
    return (x - m) / jnp.sqrt(v + eps)

def _scatter_add(tgt, idx, src, axis=0):
    return tgt.at[idx].add(src)

def _segment_sum(src, seg, n):
    return jax.ops.segment_sum(src, seg, n)
kernel_name = 'mk_macaron_d1_jaxref_r4_24a286'

def setup_inputs(seed: int=0):
    np.random.seed(seed)
    _w = jnp.asarray

    def _L0_attn_setup():
        import jax, jax.numpy as jnp
        import numpy as np
        import math
        B, T, D, H = (4, 512, 256, 16)
        HD = D // H
        ROPE_BASE = 10000.0

        def apply_rope(x):
            t, hd = (x.shape[2], x.shape[3])
            half = hd // 2
            theta = 1.0 / ROPE_BASE ** (jnp.arange(0, hd, 2, dtype=jnp.float32) / hd)
            pos = jnp.arange(1, t + 1, dtype=jnp.float32)
            ang = pos[:, None] * theta[None, :]
            ang = jnp.concatenate([ang, ang], axis=-1)
            sin, cos = (jnp.sin(ang), jnp.cos(ang))
            rot = jnp.concatenate([-x[..., half:], x[..., :half]], axis=-1)
            return x * cos[None, None, :, :] + rot * sin[None, None, :, :]
        key = jax.random.key(seed)
        ks = jax.random.split(key, 9)
        s = 1.0 / math.sqrt(D)
        return {'x': jax.random.normal(ks[0], (B, T, D), dtype=jnp.float32), 'Wq': jax.random.normal(ks[1], (D, D), dtype=jnp.float32) * s, 'bq': jax.random.normal(ks[2], (D,), dtype=jnp.float32) * 0.01, 'Wk': jax.random.normal(ks[3], (D, D), dtype=jnp.float32) * s, 'bk': jax.random.normal(ks[4], (D,), dtype=jnp.float32) * 0.01, 'Wv': jax.random.normal(ks[5], (D, D), dtype=jnp.float32) * s, 'bv': jax.random.normal(ks[6], (D,), dtype=jnp.float32) * 0.01, 'Wo': jax.random.normal(ks[7], (D, D), dtype=jnp.float32) * s, 'bo': jax.random.normal(ks[8], (D,), dtype=jnp.float32) * 0.01}
    _L0_attn_in = _L0_attn_setup()

    def _L0_ffn_setup():
        import jax, jax.numpy as jnp
        import numpy as np
        B, S, D = (4, 1024, 256)
        E, F_EXP = (16, 512)
        F_C = 2.0
        F_SH = 512
        key = jax.random.key(seed)
        ks = jax.random.split(key, 8)
        s = 0.02
        return {'hidden_states': jax.random.normal(ks[0], (B, S, D), jnp.float32), 'gate_w': jax.random.normal(ks[1], (E, D), jnp.float32) * s, 'Wg': jax.random.normal(ks[2], (E, F_EXP, D), jnp.float32) * s, 'Wu': jax.random.normal(ks[3], (E, F_EXP, D), jnp.float32) * s, 'Wd': jax.random.normal(ks[4], (E, D, F_EXP), jnp.float32) * s, 'Ws_g': jax.random.normal(ks[5], (F_SH, D), jnp.float32) * s, 'Ws_u': jax.random.normal(ks[6], (F_SH, D), jnp.float32) * s, 'Ws_d': jax.random.normal(ks[7], (D, F_SH), jnp.float32) * s}
    _L0_ffn_in = _L0_ffn_setup()
    _d = {'L0_attn_x': _L0_attn_in['x'], 'L0_attn_Wq': _L0_attn_in['Wq'], 'L0_attn_bq': _L0_attn_in['bq'], 'L0_attn_Wk': _L0_attn_in['Wk'], 'L0_attn_bk': _L0_attn_in['bk'], 'L0_attn_Wv': _L0_attn_in['Wv'], 'L0_attn_bv': _L0_attn_in['bv'], 'L0_attn_Wo': _L0_attn_in['Wo'], 'L0_attn_bo': _L0_attn_in['bo'], 'L0_ffn_gate_w': _L0_ffn_in['gate_w'], 'L0_ffn_Wg': _L0_ffn_in['Wg'], 'L0_ffn_Wu': _L0_ffn_in['Wu'], 'L0_ffn_Wd': _L0_ffn_in['Wd'], 'L0_ffn_Ws_g': _L0_ffn_in['Ws_g'], 'L0_ffn_Ws_u': _L0_ffn_in['Ws_u'], 'L0_ffn_Ws_d': _L0_ffn_in['Ws_d']}
    _x0 = _d['L0_attn_x']
    _d['L0_attn_x'] = jax.random.normal(jax.random.fold_in(jax.random.key(seed), 1), (2, 2048, 256), dtype=_x0.dtype)
    del _x0
    return _d

def reference(L0_attn_x, L0_attn_Wq, L0_attn_bq, L0_attn_Wk, L0_attn_bk, L0_attn_Wv, L0_attn_bv, L0_attn_Wo, L0_attn_bo, L0_ffn_gate_w, L0_ffn_Wg, L0_ffn_Wu, L0_ffn_Wd, L0_ffn_Ws_g, L0_ffn_Ws_u, L0_ffn_Ws_d):

    def _L0_attn_ref(x, Wq, bq, Wk, bk, Wv, bv, Wo, bo):
        import jax, jax.numpy as jnp
        import numpy as np
        import math
        B, T, D, H = (4, 512, 256, 16)
        HD = D // H
        ROPE_BASE = 10000.0

        def apply_rope(x):
            t, hd = (x.shape[2], x.shape[3])
            half = hd // 2
            theta = 1.0 / ROPE_BASE ** (jnp.arange(0, hd, 2, dtype=jnp.float32) / hd)
            pos = jnp.arange(1, t + 1, dtype=jnp.float32)
            ang = pos[:, None] * theta[None, :]
            ang = jnp.concatenate([ang, ang], axis=-1)
            sin, cos = (jnp.sin(ang), jnp.cos(ang))
            rot = jnp.concatenate([-x[..., half:], x[..., :half]], axis=-1)
            return x * cos[None, None, :, :] + rot * sin[None, None, :, :]
        b, t, d = x.shape
        h, hd = (H, HD)
        q = x @ Wq.T + bq
        k = x @ Wk.T + bk
        v = x @ Wv.T + bv
        split = lambda z: z.reshape(b, t, h, hd).transpose(0, 2, 1, 3)
        q, k, v = (split(q), split(k), split(v))
        q = apply_rope(q)
        k = apply_rope(k)
        scale = math.sqrt(hd)
        att = jnp.einsum('bhqd,bhkd->bhqk', q, k) / scale
        mask = jnp.tril(jnp.ones((t, t), dtype=bool))
        att = jnp.where(mask[None, None, :, :], att, -jnp.inf)
        att = jax.nn.softmax(att, axis=-1)
        y = jnp.einsum('bhqk,bhkd->bhqd', att, v)
        y = y.transpose(0, 2, 1, 3).reshape(b, t, d)
        y = y @ Wo.T + bo
        return y

    def _L0_ffn_ref(hidden_states, gate_w, Wg, Wu, Wd, Ws_g, Ws_u, Ws_d):
        import jax, jax.numpy as jnp
        import numpy as np
        B, S, D = (4, 1024, 256)
        E, F_EXP = (16, 512)
        F_C = 2.0
        F_SH = 512
        b, s, d = hidden_states.shape
        e = gate_w.shape[0]
        cap = int(s * F_C / e)
        logits = jnp.einsum('bsd,ed->bse', hidden_states, gate_w)
        scores = jax.nn.softmax(logits, axis=-1).transpose(0, 2, 1)
        topk_w, topk_idx = jax.lax.top_k(scores, cap)
        x_tok = jnp.take_along_axis(hidden_states[:, None, :, :], topk_idx[..., None], axis=2)
        g = jnp.einsum('becd,efd->becf', x_tok, Wg)
        u = jnp.einsum('becd,efd->becf', x_tok, Wu)
        h = jax.nn.gelu(g, approximate=False) * u
        eo = jnp.einsum('becf,edf->becd', h, Wd) * topk_w[..., None]
        offs = (jnp.arange(b) * s)[:, None, None]
        flat_idx = (topk_idx + offs).reshape(-1)
        flat = jnp.zeros((b * s, d), hidden_states.dtype)
        flat = flat.at[flat_idx].add(eo.reshape(-1, d))
        out = flat.reshape(b, s, d)
        gs = jnp.einsum('bsd,fd->bsf', hidden_states, Ws_g)
        us = jnp.einsum('bsd,fd->bsf', hidden_states, Ws_u)
        shared = jnp.einsum('bsf,df->bsd', jax.nn.gelu(gs, approximate=False) * us, Ws_d)
        return out + shared
    x = L0_attn_x
    x = x + 0.5 * _L0_ffn_ref(_layernorm(x, axis=-1), L0_ffn_gate_w, L0_ffn_Wg, L0_ffn_Wu, L0_ffn_Wd, L0_ffn_Ws_g, L0_ffn_Ws_u, L0_ffn_Ws_d)
    x = x + _L0_attn_ref(_layernorm(x, axis=-1), L0_attn_Wq, L0_attn_bq, L0_attn_Wk, L0_attn_bk, L0_attn_Wv, L0_attn_bv, L0_attn_Wo, L0_attn_bo)
    x = x + 0.5 * _L0_ffn_ref(_layernorm(x, axis=-1), L0_ffn_gate_w, L0_ffn_Wg, L0_ffn_Wu, L0_ffn_Wd, L0_ffn_Ws_g, L0_ffn_Ws_u, L0_ffn_Ws_d)
    return x

_drawn_inputs = setup_inputs


def setup_inputs(seed=0):
    import zlib

    import numpy as np

    out = dict(_drawn_inputs(seed))
    spreads = {}
    factors = {'L0_attn_bq': 58.644,
     'L0_attn_bk': 64.0,
     'L0_attn_bv': 5.7,
     'L0_attn_bo': 16.242,
     'L0_ffn_gate_w': 8.0,
     'L0_ffn_Wg': 8.0,
     'L0_ffn_Wu': 8.0,
     'L0_ffn_Wd': 8.0,
     'L0_ffn_Ws_g': 4.386,
     'L0_ffn_Ws_u': 5.078,
     'L0_ffn_Ws_d': 4.747}
    for name, (base, spread) in spreads.items():
        noise = np.random.default_rng([zlib.crc32(name.encode()), seed]).standard_normal(out[name].shape)
        drawn = base * np.exp(spread * noise) if base else spread * noise
        out[name] = jnp.asarray(drawn.astype(out[name].dtype))
    for name, factor in factors.items():
        out[name] = (out[name] * factor).astype(out[name].dtype)
    return out
```

```python
from contextlib import ExitStack

import numpy as np

B, S, D = 2, 2048, 256
N = B * S
P = 128
NT = N // P
TPB = S // P
NQ = NT // 4
E, F = 16, 512
CAP = S * 2 // E
H, HD = 16, 16
DC = D // P
FC = F // P
ROW = D + E
VW = 32
EPS = 1e-5
TRIPLE = ((0, 1, 0), (0, 0, 1))
SAFE_NORMS = 14000.0
NBITS = 30


class Steps:

    def __init__(self, sem, names):
        self.sem, self.names, self.K = sem, names, len(names)
        self.at = {n: k for k, n in enumerate(names)}
        assert len(self.at) == self.K
        self.next = 0

    def value(self, name, i, d=0):
        c = self.at[name] + 1 + d * self.K
        return i * self.K + c

    def wait(self, eng, name, i, d=0):
        v = self.value(name, i, d)
        if isinstance(v, int) and v <= 0:
            return
        eng.wait_ge(self.sem, v)

    def done(self, ins, name):
        assert self.names[self.next] == name, (self.names[self.next], name)
        self.next = (self.next + 1) % self.K
        ins.then_inc(self.sem, 1)

    def skip(self, eng, i, names):
        first = self.at[names[0]]
        v = i * self.K + first
        if v > 0:
            eng.wait_ge(self.sem, v)
        for n in names:
            assert self.names[self.next] == n, (self.names[self.next], n)
            self.next = (self.next + 1) % self.K
        eng.sem_inc(self.sem, len(names))


def passes(eng, n, body):
    body(0)
    if n > 2:
        with eng.Fori(1, n - 1) as i:
            body(i)
    if n > 1:
        body(n - 1)


class Program:
    def __init__(self, nc, ins, out):
        import concourse.bass as bass
        from concourse import mybir
        self.nc, self.bass, self.ins, self.out = nc, bass, ins, out
        self.f32, self.f32r = mybir.dt.float32, mybir.dt.float32r
        self.bf16, self.i32 = mybir.dt.bfloat16, mybir.dt.int32
        self.ACT, self.ALU, self.AX = mybir.ActivationFunctionType, mybir.AluOpType, mybir.AxisListType

        def dram(name, shape):
            return nc.dram_tensor(name, shape, self.f32, kind="Internal").ap()

        self.x1 = dram("x_after_ffn1", [N, D])
        self.x2 = dram("x_after_attn", [N, D])
        self.table = dram("token_table", [N, ROW])
        self.qk = [dram(n, [B * D * 3, S]) for n in ("q_rows", "k_rows")]
        self.shift = dram("shift", [B * H, 2, S])
        self.vals = dram("values", [N, H * VW])
        self.y = dram("attn_heads", [N, D])

    def settle(self, eng):
        eng.sem_inc(self.settled, 1)

    def scope(self):
        st = ExitStack()
        nc = self.nc
        tag = f"{nc.next_id()}_"
        st.sb = lambda name, shape, dt=self.f32: st.enter_context(nc.sbuf_tensor(tag + name, shape, dt))
        st.ps = lambda name, shape, dt=self.f32: st.enter_context(nc.psum_tensor(tag + name, shape, dt))
        st.sem = lambda name: st.enter_context(nc.semaphore(tag + name))
        st.steps = lambda name, names: Steps(st.sem(name), names)
        return st

    def product3(self, pe, out, w_hi, w_lo, x_hi, x_lo, start, stop):
        pe.matmul(out, w_hi, x_hi, start=start, stop=False)
        pe.matmul(out, w_hi, x_lo, start=False, stop=False)
        return pe.matmul(out, w_lo, x_hi, start=False, stop=stop)

    def load_constants(self, st):
        nc, ALU = self.nc, self.ALU
        self.ident = st.sb("ident", [P, P])
        self.tri = st.sb("tri", [P, P], self.bf16)
        self.ones = st.sb("ones", [P, P], self.bf16)
        self.same_expert = st.sb("same_expert", [P, P], self.bf16)
        self.slots = st.sb("slots", [P, CAP], self.bf16)
        self.bits = st.sb("bits", [P, NBITS], self.i32)
        self.ones32 = st.sb("ones32", [E, P])
        self.gate = st.sb("gate", [P, DC, E])
        self.eps = st.sb("eps", [P, 1])
        self.settled = st.sem("settled")
        with self.scope() as t, nc.Block() as blk:
            raw = t.sb("raw", [P, 3 * P + CAP])
            s_in, s_id, s_cast = t.sem("in"), t.sem("ident"), t.sem("cast")

            @blk.sync
            def _(sp):
                sp.dma_start(self.ident[:, :], self.ins["c_ident"]).then_inc(s_id, 16)
                sp.dma_start(raw[:, :], self.ins["c_masks"]).then_inc(s_in, 16)
                sp.dma_start(self.bits[:, :], self.ins["c_bits"]).then_inc(s_id, 16)
                sp.dma_start(self.gate[:, :, :], self.ins["gate_wT"].rearrange("(c p) e -> p c e", p=P)).then_inc(s_id, 16)
                sp.wait_ge(s_id, 48)

            @blk.vector
            def _(dve):
                dve.memset(self.ones32[:, :], 1.0)
                dve.memset(self.eps[:, :], EPS)
                dve.wait_ge(s_in, 16)
                for k, m in enumerate((self.tri, self.ones, self.same_expert)):
                    dve.tensor_copy(m[:, :], raw[:, k * P:(k + 1) * P])
                dve.tensor_copy(self.slots[:, :], raw[:, 3 * P:]).then_inc(s_cast, 1)
                dve.wait_ge(s_cast, 1)

    def ln_router(self, x):
        nc, ALU, ACT, AX = self.nc, self.ALU, self.ACT, self.AX
        scores = self.scores
        with self.scope() as t, nc.Block() as blk:
            xq = t.sb("xq", [P, 2, 4, D])
            xn = t.sb("xn", [P, 2, 4, D])
            st6 = t.sb("st6", [P, 2, 4, 6])
            mv = t.sb("mv", [P, 2, 4, 2])
            std = t.sb("std", [P, 2, 4])
            rstd = t.sb("rstd", [P, 2, 4])
            shift = t.sb("shift", [P, 2, 4])
            xT = t.sb("xT", [P, 2, DC, 4 * P])
            mx = t.sb("mx", [P, NT])
            dif = t.sb("dif", [P, NT, E])
            ex = t.sb("ex", [P, NT, E])
            pT = t.ps("pT", [P, 2, DC, 4 * P])
            pL = t.ps("pL", [P, NT * E])
            s_x = [t.sem(f"x{k}") for k in range(2)]
            s_w = [t.sem(f"w{k}") for k in range(2)]
            s_sc = t.sem("sc")
            per = lambda *names: [(n, k) for k in range(2) for n in names]
            dve = t.steps("dve", per("stats", "mv", "rstd", "shift", "xn", "xT1"))
            act = t.steps("act", per("std", "xT0"))
            pe = t.steps("pe", per("T", "L"))
            s_sm = t.sem("softmax_dve")
            s_ex = t.sem("softmax_act")
            xv = x.rearrange("(q t p) d -> q p t d", t=4, p=P)
            tv = self.table[:, 0:D].rearrange("(q t p) d -> q p t d", t=4, p=P)

            @blk.sync
            def _(sp):
                def body(i):
                    for k in range(2):
                        dve.wait(sp, ("xn", k), i, -1)
                        sp.dma_start(xq[:, k, :, :], xv[2 * i + k]).then_inc(s_x[k], 16)
                passes(sp, NQ // 2, body)

            @blk.gpsimd
            def _(pool):
                def body(i):
                    for k in range(2):
                        dve.wait(pool, ("xn", k), i)
                        pool.dma_start(tv[2 * i + k], xn[:, k, :, :]).then_inc(s_w[k], 16)
                passes(pool, NQ // 2, body)
                for k in range(2):
                    pool.wait_ge(s_w[k], 16 * (NQ // 2))
                pool.wait_ge(s_sm, 6)
                with nc.allow_non_contiguous_dma(reason="64-byte rows"):
                    pool.dma_start(self.table[:, D:ROW].rearrange("(t p) e -> p t e", p=P),
                                   scores[:, :, :]).then_inc(s_sc, 16)
                pool.wait_ge(s_sc, 16)

            @blk.vector
            def _(v):
                def body(i):
                    for k in range(2):
                        v.wait_ge(s_x[k], 16 * (i + 1))
                        for j in range(4):
                            m = v.bn_stats(st6[:, k, j, :], xq[:, k, j, :])
                        dve.done(m, ("stats", k))
                        dve.wait(v, ("stats", k), i)
                        self.settle(v)
                        for j in range(4):
                            m = v.bn_aggr(mv[:, k, j, :], st6[:, k, j, :])
                        dve.done(m, ("mv", k))
                        act.wait(v, ("std", k), i)
                        dve.done(v.reciprocal(rstd[:, k, :], std[:, k, :]), ("rstd", k))
                        dve.wait(v, ("rstd", k), i)
                        dve.done(v.scalar_tensor_tensor(shift[:, k, :], mv[:, k, :, 0], -1.0, rstd[:, k, :],
                                                        ALU.mult, ALU.mult), ("shift", k))
                        dve.wait(v, ("shift", k), i)
                        pe.wait(v, ("T", k), i, -1)
                        if not (isinstance(i, int) and i == 0):
                            v.wait_ge(s_w[k], 16 * i)
                        for j in range(4):
                            m = v.tensor_scalar(xn[:, k, j, :], xq[:, k, j, :], rstd[:, k, j:j + 1],
                                                shift[:, k, j:j + 1], ALU.mult, ALU.add)
                        dve.done(m, ("xn", k))
                        pe.wait(v, ("T", k), i)
                        pe.wait(v, ("L", k), i, -1)
                        dve.done(v.tensor_copy(xT[:, k, 1, :], pT[:, k, 1, :]), ("xT1", k))
                passes(v, NQ // 2, body)
                pe.wait(v, ("L", 1), NQ // 2 - 1)
                lg = pL[:, :].rearrange("p (t e) -> p t e", e=E)
                bc = lambda a: a[:, :].unsqueeze(2).to_broadcast([P, NT, E])
                v.tensor_reduce(mx[:, :], lg, AX.X, ALU.max).then_inc(s_sm, 1)
                v.wait_ge(s_sm, 1)
                v.tensor_tensor(dif[:, :, :], lg, bc(mx), ALU.subtract).then_inc(s_sm, 1)
                v.wait_ge(s_ex, 1)
                v.wait_ge(s_sm, 2)
                v.tensor_reduce(mx[:, :], ex[:, :, :], AX.X, ALU.add).then_inc(s_sm, 1)
                v.wait_ge(s_sm, 3)
                v.reciprocal(mx[:, :], mx[:, :]).then_inc(s_sm, 1)
                v.wait_ge(s_sm, 4)
                v.tensor_tensor(scores[:, :, :], ex[:, :, :], bc(mx), ALU.mult).then_inc(s_sm, 2)

            @blk.scalar
            def _(a):
                def body(i):
                    for k in range(2):
                        dve.wait(a, ("mv", k), i)
                        dve.wait(a, ("rstd", k), i, -1)
                        act.done(a.activation(std[:, k, :], mv[:, k, :, 1], ACT.Sqrt, bias=self.eps[:, :]), ("std", k))
                        pe.wait(a, ("T", k), i)
                        pe.wait(a, ("L", k), i, -1)
                        act.done(a.activation(xT[:, k, 0, :], pT[:, k, 0, :], ACT.Copy), ("xT0", k))
                passes(a, NQ // 2, body)
                a.wait_ge(s_sm, 2)
                a.activation(ex[:, :, :], dif[:, :, :], ACT.Exp).then_inc(s_ex, 1)

            @blk.tensor
            def _(t_):
                def body(i):
                    for k in range(2):
                        dve.wait(t_, ("xn", k), i)
                        dve.wait(t_, ("xT1", k), i, -1)
                        act.wait(t_, ("xT0", k), i, -1)
                        for j in range(4):
                            for c in range(DC):
                                m = t_.transpose(pT[:, k, c, j * P:(j + 1) * P], xn[:, k, j, c * P:(c + 1) * P],
                                                 self.ident[:, :])
                        pe.done(m, ("T", k))
                        dve.wait(t_, ("xT1", k), i)
                        act.wait(t_, ("xT0", k), i)
                        for j in range(4):
                            o = pL[:, self.bass.ds((2 * i + k) * 4 * E + j * E, E)]
                            for c in range(DC):
                                m = t_.matmul(o, xT[:, k, c, j * P:(j + 1) * P], self.gate[:, c, :],
                                              start=c == 0, stop=c == DC - 1)
                        pe.done(m, ("L", k))
                passes(t_, NQ // 2, body)

    def route(self):
        nc, ALU, ACT, AX, f32, bf16, i32 = self.nc, self.ALU, self.ACT, self.AX, self.f32, self.bf16, self.i32
        scores, idx = self.scores, self.idx
        G = NT // 8
        HC = CAP // P
        with self.scope() as t, nc.Block() as blk:
            rows = t.sb("rows", [P, G, P])
            best = t.sb("best", [P, B])
            cand = t.sb("cand", [P, B])
            keep = t.sb("keep", [P, B])
            ge = t.sb("ge", [P, S // 8], bf16)
            cnt = t.sb("cnt", [P, B], bf16)
            diag = t.sb("diag", [E, B, E])
            thr = t.sb("thr", [P, B, E])
            gt = t.sb("gt", [P, B, TPB, E], bf16)
            eq = t.sb("eq", [P, B, TPB, E], bf16)
            sel = t.sb("sel", [P, B, TPB, E], bf16)
            before = t.sb("before", [P, 3, B, TPB, E], bf16)
            need = t.sb("need", [P, B, E])
            fits = t.sb("fits", [P, B, TPB, E])
            rank = t.sb("rank", [P, B, TPB, E])
            L = t.sb("L", [P, 2, TPB, CAP], bf16)
            p_rows = t.ps("p_rows", [P, G, P])
            p_cnt = t.ps("p_cnt", [P, 512])
            p_thr = t.ps("p_thr", [P, 512])
            p_rank = t.ps("p_rank", [P, B * TPB * E])
            p_idx = t.ps("p_idx", [P, E, B, HC])
            s_pe, s_v = t.sem("pe"), t.sem("dve")
            s_bit = t.steps("bit", ["cand", "cnt0", "cnt1", "keep", "best"])
            s_tot = t.steps("tot", ["tot"])
            s_L = t.steps("L", ["L0", "L1"])
            s_M = t.steps("M", ["M0", "M1"])
            over = lambda a: a.unsqueeze(2).to_broadcast([P, B, TPB, E])

            @blk.vector
            def _(v):
                n = [0]

                def link(m):
                    n[0] += 1
                    m.then_inc(s_v, 1)
                    v.wait_ge(s_v, n[0])

                v.wait_ge(s_pe, 1)
                link(v.tensor_copy(rows[:, :, :], p_rows[:, :, :]))
                link(v.memset(best[:, :], 0.0))

                def search(i):
                    bit = self.bits[:, self.bass.ds(i, 1)].to_broadcast([P, B])
                    s_bit.wait(v, "best", i, -1)
                    s_bit.done(v.tensor_tensor(cand[:, :].bitcast(i32), best[:, :].bitcast(i32), bit,
                                               ALU.bitwise_or), "cand")
                    s_bit.wait(v, "cand", i)
                    for b in range(B):
                        if b:
                            s_bit.wait(v, "cnt0", i)
                        m = v.tensor_scalar(ge[:, :], rows[:, b * G // B:(b + 1) * G // B, :].rearrange("p g k -> p (g k)"),
                                            cand[:, b:b + 1], None, ALU.is_ge, ALU.add, accum_out=cnt[:, b:b + 1])
                        s_bit.done(m, f"cnt{b}")
                    s_tot.wait(v, "tot", i)
                    s_bit.done(v.scalar_tensor_tensor(keep[:, :], p_cnt[:, 0:B], float(CAP), cand[:, :],
                                                      ALU.is_ge, ALU.mult), "keep")
                    s_bit.wait(v, "keep", i)
                    s_bit.done(v.tensor_tensor(best[:, :], best[:, :], keep[:, :], ALU.max), "best")
                passes(v, NBITS, search)
                s_bit.wait(v, "best", NBITS - 1)
                for b in range(B):
                    m = v.tensor_scalar(diag[:, b, :], self.ident[0:E, 0:E], best[0:E, b:b + 1], None, ALU.mult)
                link(m)
                v.wait_ge(s_pe, 2)
                link(v.tensor_copy(thr[:, :, :], p_thr[:, 0:B * E].rearrange("p (b e) -> p b e", e=E)))
                sc = scores[:, :, :].rearrange("p (b t) e -> p b t e", b=B)
                for b in range(B):
                    tb = thr[:, b, :].unsqueeze(1).to_broadcast([P, TPB, E])
                    v.tensor_tensor(gt[:, b, :, :], sc[:, b, :, :], tb, ALU.is_gt)
                    m = v.tensor_tensor(eq[:, b, :, :], sc[:, b, :, :], tb, ALU.is_equal)
                link(m)

                def running(k, mask):
                    link(v.memset(before[:, k, :, 0, :], 0.0))
                    for tt in range(1, TPB):
                        link(v.tensor_tensor(before[:, k, :, tt, :], before[:, k, :, tt - 1, :],
                                             mask[:, :, tt - 1, :], ALU.add))

                running(0, gt)
                running(1, eq)
                self.after_eq = n[0]
                v.wait_ge(s_pe, 3)
                link(v.tensor_scalar(need[:, :, :], p_thr[:, 0:B * E].rearrange("p (b e) -> p b e", e=E),
                                     -1.0, float(CAP), ALU.mult, ALU.add))
                pr = p_rank[:, :].rearrange("p (b t e) -> p b t e", b=B, e=E)
                for b in range(B):
                    nb = need[:, b, :].unsqueeze(1).to_broadcast([P, TPB, E])
                    m = v.tensor_tensor(fits[:, b, :, :], pr[:, b, :, :], nb, ALU.is_le)
                link(m)
                flat = lambda a: a[:, :, :, :].rearrange("p b t e -> p (b t e)")
                link(v.tensor_tensor(flat(fits), flat(fits), flat(eq), ALU.mult))
                link(v.tensor_tensor(flat(sel), flat(fits), flat(gt), ALU.add))
                running(2, sel)
                self.after_sel = n[0]
                v.wait_ge(s_pe, 4)
                link(v.tensor_copy(flat(rank), p_rank[:, :]))
                def columns(i):
                    for b in range(B):
                        s_M.wait(v, f"M{b}", i, -1)
                        for tt in range(TPB):
                            r = flat(rank)[:, self.bass.ds(i + (b * TPB + tt) * E, 1)]
                            m = v.tensor_scalar(L[:, b, tt, :], self.slots[:, :], r, None, ALU.is_ge)
                        s_L.done(m, f"L{b}")
                passes(v, E, columns)
                s_M.wait(v, "M1", E - 1)
                for b in range(B):
                    m = v.tensor_scalar(idx[:, :, b, :], p_idx[:, :, b, :], float(b * S), None, ALU.add)
                link(m)

            @blk.tensor
            def _(t_):
                for g in range(G):
                    m = t_.transpose(p_rows[:, g, :], scores[:, 8 * g:8 * g + 8, :].rearrange("p t e -> p (t e)"),
                                     self.ident[:, :])
                m.then_inc(s_pe, 1)
                def total(i):
                    s_bit.wait(t_, "cnt1", i)
                    s_tot.done(t_.matmul(p_cnt[:, 0:B], self.same_expert[:, :], cnt[:, :], start=True, stop=True), "tot")
                passes(t_, NBITS, total)
                t_.wait_ge(s_v, 3)
                t_.matmul(p_thr[:, 0:B * E], self.ones32[:, :], diag[:, :, :].rearrange("p b e -> p (b e)"),
                          start=True, stop=True).then_inc(s_pe, 1)
                t_.wait_ge(s_v, self.after_eq)

                def ranks(k, mask):
                    f = lambda a: a.rearrange("p b t e -> p (b t e)")
                    t_.matmul(p_rank[:, :], self.tri[:, :], f(mask[:, :, :, :]), start=True, stop=False)
                    return t_.matmul(p_rank[:, :], self.ones[:, :], f(before[:, k, :, :, :]), start=False, stop=True)
                ranks(1, eq)
                o = p_thr[:, 0:B * E].rearrange("p (b e) -> p b e", e=E)
                t_.matmul(o, self.ones[:, :], before[:, 0, :, TPB - 1, :], start=True, stop=False)
                t_.matmul(o, self.ones[:, :], gt[:, :, TPB - 1, :], start=False, stop=True).then_inc(s_pe, 1)
                t_.wait_ge(s_v, self.after_sel)
                ranks(2, sel).then_inc(s_pe, 1)
                cols = p_idx[:, :, :, :].rearrange("p e b h -> p (e b h)")
                def tokens_of(i):
                    for b in range(B):
                        s_L.wait(t_, f"L{b}", i)
                        for h in range(HC):
                            o = cols[:, self.bass.ds(i * (B * HC) + b * HC + h, 1)]
                            for tt in range(TPB):
                                m = t_.matmul(o, L[:, b, tt, h * P:(h + 1) * P], self.ones[:, 0:1],
                                              start=tt == 0, stop=tt == TPB - 1)
                        s_M.done(m, f"M{b}")
                passes(t_, E, tokens_of)

    def experts(self, x, out, shared):
        nc, ALU, ACT, bass = self.nc, self.ALU, self.ACT, self.bass
        J = NQ if shared else E
        W = 4 * P
        with self.scope() as t, nc.Block() as blk:
            raw_g, raw_u = t.sb("raw_g", [P, DC, F]), t.sb("raw_u", [P, DC, F])
            raw_d = t.sb("raw_d", [P, FC, D])
            nw = 1 if shared else 2
            wg = [t.sb(f"wg{h}", [P, nw, DC, F], self.f32r) for h in range(2)]
            wu = [t.sb(f"wu{h}", [P, nw, DC, F], self.f32r) for h in range(2)]
            wd = [t.sb(f"wd{h}", [P, nw, FC, D], self.f32r) for h in range(2)]
            xr = t.sb("xr", [P, 2, 4, ROW])
            xT = [t.sb(f"xT{h}", [P, 2, DC, W], self.f32r) for h in range(2)]
            gl = t.sb("gl", [P, 2, W])
            hf = t.sb("hf", [P, 2, W])
            hT = [t.sb(f"hT{h}", [P, 2, FC, W], self.f32r) for h in range(2)]
            eo = t.sb("eo", [P, 2, 4, D])
            xres = t.sb("xres", [P, 2, 4, D]) if shared else None
            wt = t.sb("wt", [P, 2, 4])
            gidx = t.sb("gidx", [P, 2, 4], self.i32)
            sidx = t.sb("sidx", [P, 2, 4], self.i32)
            pG, pU = t.ps("pG", [P, 2, W]), t.ps("pU", [P, 2, W])
            pD = t.ps("pD", [P, 2, 2, D])
            pX = t.ps("pX", [P, DC, W])

            per = lambda *names: [(n, k) for k in range(2) for n in names]
            pe = t.steps("pe", per("G0", "U0", "G1", "U1", "D0", "D1", "T0", "T1", "G2", "U2", "G3", "U3"))
            a_own = () if shared else ("wgh", "wuh")
            act = t.steps("act", per("gelu0", "hh0", "gelu1", "hh1", "xh0", "xh1", *a_own, "gelu2", "hh2", "gelu3", "hh3",
                                     *(() if shared else ("wdh",))))
            dve = t.steps("dve", per("mul0", "mul1", "hl0", "hl1", "ev0", "ev1", "xl0", "xl1", "wt",
                                     "mul2", "mul3", "hl2", "hl3"))
            pool = t.steps("pool", per(*(() if shared else ("gi", "wgl", "wul", "si", "wdl"))) or ["none"])
            s_rows = [t.sem(f"rows{k}") for k in range(2)]
            s_res = [t.sem(f"res{k}") for k in range(2)] if shared else None
            s_raw = [t.sem(n) for n in ("raw_g", "raw_u", "raw_d")]
            s_out = [t.sem(f"out{k}") for k in range(2)]
            s_wh, s_wl = (t.sem("wh"), t.sem("wl")) if shared else (None, None)
            rows_inc = 16 if shared else 64
            out_inc = 16 if shared else 64
            ob = lambda k: 0 if shared else k

            tv = self.table[:, 0:D].rearrange("(q t p) d -> q p t d", t=4, p=P)
            xv = x.rearrange("(q t p) d -> q p t d", t=4, p=P)
            ov = out.rearrange("(q t p) d -> q p t d", t=4, p=P)
            src = [self.ins[n] for n in (("WsgT", "WsuT", "WsdT") if shared else ("WgT", "WuT", "WdT"))]

            def other(k, d):
                return (k + d) % 2, (k + d) // 2

            class Pass:
                def __init__(p, i, k):
                    p.i, p.k, p.n = i, k, 1 - k
                    s = 2 * i + k if isinstance(i, int) else None
                    p.rows = s is None or s < J
                    p.up = s is None or 1 <= s <= J
                    p.down = s is None or s >= 2

            def stream(eng, body):
                def both(i):
                    for k in range(2):
                        body(Pass(i, k))
                passes(eng, J // 2 + 1, both)

            def split_weights(eng_op, eng, which, slot):
                raw = (raw_g, raw_u, raw_d)[which]
                hi, lo = (wg, wu, wd)[which]
                if eng_op == "hi":
                    return eng.activation(hi[:, slot, :, :], raw[:, :, :], ACT.Copy)
                return eng.tensor_tensor(lo[:, slot, :, :], raw[:, :, :], hi[:, slot, :, :].bitcast(self.f32), ALU.subtract)

            @blk.sync
            def _(sp):
                if shared:
                    for w, (dst, ch) in enumerate(((raw_g, P), (raw_u, P), (raw_d, P))):
                        sp.dma_start(dst[:, :, :], src[w].rearrange("(c p) f -> p c f", p=P)).then_inc(s_raw[w], 16)

                def body(p):
                    i, k = p.i, p.k
                    k1, d1 = other(k, 1)
                    if shared:
                        if p.rows:
                            pe.wait(sp, ("T1", k), i, -1)
                            sp.dma_start(xr[:, k, :, 0:D], tv[2 * i + k]).then_inc(s_rows[k], 16)
                        if p.down:
                            dve.wait(sp, ("ev1", k), i, -1)
                            sp.dma_start(xres[:, k, :, :], xv[2 * (i - 1) + k]).then_inc(s_res[k], 16)
                    elif p.rows:
                        for w, (dst, st) in enumerate(((raw_g, "wgl"), (raw_u, "wul"), (raw_d, "wdl"))):
                            kb, db = other(k, -1)
                            pool.wait(sp, (st, kb), i, db)
                            wsrc = src[w].rearrange("e (c p) f -> e p c f", p=P)
                            sp.dma_start(dst[:, :, :], wsrc[2 * i + k]).then_inc(s_raw[w], 16)
                stream(sp, body)

            @blk.tensor
            def _(t_):
                def gu(p, f):
                    i, k, n = p.i, p.k, p.n
                    b = f % 2
                    kb, db = (k, 0) if f >= 2 else other(k, -1)
                    fb = (f + 2) % 4
                    for name, ps, w, user, eng_u in (("G", pG, wg, "mul", dve), ("U", pU, wu, "mul", dve)):
                        if name == "G":
                            act.wait(t_, (f"gelu{fb}", kb), i, db)
                        dve.wait(t_, (f"mul{fb}", kb), i, db)
                        for c in range(DC):
                            m = self.product3(t_, ps[:, b, :], w[0][:, ob(n), c, f * P:(f + 1) * P],
                                              w[1][:, ob(n), c, f * P:(f + 1) * P],
                                              xT[0][:, n, c, :], xT[1][:, n, c, :], c == 0, c == DC - 1)
                        pe.done(m, (f"{name}{f}", k))

                def body(p):
                    i, k, n = p.i, p.k, p.n
                    kb, db = other(k, -1)
                    if p.up:
                        dve.wait(t_, ("xl1", kb), i, db)
                        if not shared:
                            pool.wait(t_, ("wul", kb), i, db)
                        else:
                            t_.wait_ge(s_wl, 3)
                        gu(p, 0)
                        gu(p, 1)
                    else:
                        pe.skip(t_, i, [(x_, k) for x_ in ("G0", "U0", "G1", "U1")])
                    if p.down:
                        dve.wait(t_, ("hl3", kb), i, db)
                        if not shared:
                            pool.wait(t_, ("wdl", k), i, -1)
                        for h in range(2):
                            dve.wait(t_, (f"ev{h}", kb), i, db)
                            for r in range(2):
                                for c in range(FC):
                                    q = 2 * h + r
                                    m = self.product3(t_, pD[:, h, r, :], hT[0][:, k, c, q * P:(q + 1) * P],
                                                      hT[1][:, k, c, q * P:(q + 1) * P], wd[0][:, ob(k), c, :],
                                                      wd[1][:, ob(k), c, :], c == 0, c == FC - 1)
                            pe.done(m, (f"D{h}", k))
                    else:
                        pe.skip(t_, i, [("D0", k), ("D1", k)])
                    if p.rows:
                        t_.wait_ge(s_rows[k], rows_inc * (i + 1))
                        for c in range(DC):
                            dve.wait(t_, (f"xl{c}", kb), i, db)
                            for q in range(4):
                                m = t_.transpose(pX[:, c, q * P:(q + 1) * P], xr[:, k, q, c * P:(c + 1) * P], self.ident[:, :])
                            pe.done(m, (f"T{c}", k))
                    else:
                        pe.skip(t_, i, [("T0", k), ("T1", k)])
                    if p.up:
                        gu(p, 2)
                        gu(p, 3)
                    else:
                        pe.skip(t_, i, [(x_, k) for x_ in ("G2", "U2", "G3", "U3")])
                stream(t_, body)

            @blk.scalar
            def _(a):
                if shared:
                    for w in range(3):
                        a.wait_ge(s_raw[w], 16)
                        split_weights("hi", a, w, 0).then_inc(s_wh, 1)

                def hidden(p, f):
                    i, k, n = p.i, p.k, p.n
                    if not p.up:
                        act.skip(a, i, [(f"gelu{f}", k), (f"hh{f}", k)])
                        return
                    kb, db = (k, 0) if f >= 2 else other(k, -1)
                    pe.wait(a, (f"G{f}", k), i)
                    dve.wait(a, (f"mul{(f + 2) % 4}", kb), i, db)
                    act.done(a.activation(gl[:, f % 2, :], pG[:, f % 2, :], ACT.Gelu), (f"gelu{f}", k))
                    dve.wait(a, (f"mul{f}", k), i)
                    if f == 0:
                        kc, dc = other(k, -1)
                        pe.wait(a, ("D1", kc), i, dc)
                    act.done(a.activation(hT[0][:, n, f, :], hf[:, f % 2, :], ACT.Copy), (f"hh{f}", k))

                def body(p):
                    i, k = p.i, p.k
                    hidden(p, 0)
                    hidden(p, 1)
                    if p.rows:
                        kb, db = other(k, -1)
                        pe.wait(a, ("U3", kb), i, db)
                        for c in range(DC):
                            pe.wait(a, (f"T{c}", k), i)
                            act.done(a.activation(xT[0][:, k, c, :], pX[:, c, :], ACT.Copy), (f"xh{c}", k))
                        if not shared:
                            for w, nm in enumerate(("wgh", "wuh")):
                                a.wait_ge(s_raw[w], 16 * (2 * i + k + 1))
                                act.done(split_weights("hi", a, w, k), (nm, k))
                    else:
                        act.skip(a, i, [(x_, k) for x_ in ("xh0", "xh1", *a_own)])
                    hidden(p, 2)
                    hidden(p, 3)
                    if not shared:
                        if p.rows:
                            a.wait_ge(s_raw[2], 16 * (2 * i + k + 1))
                            pe.wait(a, ("D1", k), i)
                            act.done(split_weights("hi", a, 2, k), ("wdh", k))
                        else:
                            act.skip(a, i, [("wdh", k)])
                stream(a, body)

            @blk.vector
            def _(v):
                if shared:
                    for w in range(3):
                        v.wait_ge(s_wh, w + 1)
                        split_weights("lo", v, w, 0).then_inc(s_wl, 1)

                def mul(p, f):
                    i, k = p.i, p.k
                    act.wait(v, (f"gelu{f}", k), i)
                    pe.wait(v, (f"U{f}", k), i)
                    kb, db = (k, 0) if f >= 2 else other(k, -1)
                    act.wait(v, (f"hh{(f + 2) % 4}", kb), i, db)
                    dve.wait(v, (f"hl{(f + 2) % 4}", kb), i, db)
                    dve.done(v.tensor_tensor(hf[:, f % 2, :], gl[:, f % 2, :], pU[:, f % 2, :], ALU.mult), (f"mul{f}", k))

                def low(p, f):
                    i, k, n = p.i, p.k, p.n
                    act.wait(v, (f"hh{f}", k), i)
                    dve.done(v.tensor_tensor(hT[1][:, n, f, :], hf[:, f % 2, :], hT[0][:, n, f, :].bitcast(self.f32),
                                             ALU.subtract), (f"hl{f}", k))

                def body(p):
                    i, k = p.i, p.k
                    if p.up:
                        mul(p, 0)
                        mul(p, 1)
                        low(p, 0)
                        low(p, 1)
                    else:
                        dve.skip(v, i, [(x_, k) for x_ in ("mul0", "mul1", "hl0", "hl1")])
                    if p.down:
                        if not isinstance(i, int) or 2 * i + k >= 4:
                            v.wait_ge(s_out[k], out_inc * (i - 1))
                        if shared:
                            v.wait_ge(s_res[k], 16 * i)
                        for h in range(2):
                            pe.wait(v, (f"D{h}", k), i)
                            for r in range(2):
                                q = 2 * h + r
                                if shared:
                                    m = v.scalar_tensor_tensor(eo[:, k, q, :], pD[:, h, r, :], 0.5, xres[:, k, q, :],
                                                               ALU.mult, ALU.add)
                                else:
                                    m = v.tensor_scalar(eo[:, k, q, :], pD[:, h, r, :], wt[:, k, q:q + 1], 0.5,
                                                        ALU.mult, ALU.mult)
                            dve.done(m, (f"ev{h}", k))
                    else:
                        dve.skip(v, i, [("ev0", k), ("ev1", k)])
                    if p.rows:
                        for c in range(DC):
                            act.wait(v, (f"xh{c}", k), i)
                            dve.done(v.tensor_tensor(xT[1][:, k, c, :], pX[:, c, :], xT[0][:, k, c, :].bitcast(self.f32),
                                                     ALU.subtract), (f"xl{c}", k))
                    else:
                        dve.skip(v, i, [("xl0", k), ("xl1", k)])
                    if p.rows and not shared:
                        dve.wait(v, ("ev1", k), i)
                        col = xr[:, k, :, :].rearrange("p q w -> p w q")[:, bass.ds(2 * i + (D + k), 1), :]
                        dve.done(v.tensor_copy(wt[:, k, :].unsqueeze(1), col), ("wt", k))
                    else:
                        dve.skip(v, i, [("wt", k)])
                    if p.up:
                        mul(p, 2)
                        mul(p, 3)
                        low(p, 2)
                        low(p, 3)
                    else:
                        dve.skip(v, i, [(x_, k) for x_ in ("mul2", "mul3", "hl2", "hl3")])
                stream(v, body)

            @blk.gpsimd
            def _(g):
                idx = self.idx

                def take_rows(i, k):
                    flat = idx[:, :, :, :].rearrange("p e b h -> p (e b h)")
                    m = g.tensor_copy(gidx[:, k, :], flat[:, bass.ds((2 * i + k) * 4, 4)])
                    return m

                def gather(k):
                    for q in range(4):
                        g.indirect_dma_start(xr[:, k, q, :], None, self.table[:, :],
                                             bass.IndirectOffsetOnAxis(gidx[:, k, q:q + 1], 0)).then_inc(s_rows[k], 16)

                if shared:
                    def body(p):
                        i, k = p.i, p.k
                        if p.down:
                            dve.wait(g, ("ev1", k), i)
                            g.dma_start(ov[2 * (i - 1) + k], eo[:, k, :, :]).then_inc(s_out[k], 16)
                    stream(g, body)
                    for k in range(2):
                        g.wait_ge(s_out[k], 16 * (J // 2))
                    return

                def body(p):
                    i, k = p.i, p.k
                    if p.rows:
                        if not (isinstance(i, int) and i == 0):
                            g.wait_ge(s_rows[k], 64 * i)
                        pool.done(take_rows(i, k), ("gi", k))
                        pool.wait(g, ("gi", k), i)
                        pe.wait(g, ("T1", k), i, -1)
                        dve.wait(g, ("wt", k), i, -1)
                        self.settle(g)
                        gather(k)
                    else:
                        pool.skip(g, i, [("gi", k)])
                    if p.rows:
                        for w, nm in enumerate(("wg", "wu")):
                            act.wait(g, (nm + "h", k), i)
                            pool.done(split_weights("lo", g, w, k), (nm + "l", k))
                    else:
                        pool.skip(g, i, [("wgl", k), ("wul", k)])
                    if p.down:
                        if not isinstance(i, int) or 2 * i + k >= 3:
                            g.wait_ge(s_out[1 - k], 64 * (i - 1 + k))
                        flat = idx[:, :, :, :].rearrange("p e b h -> p (e b h)")
                        if not isinstance(i, int) or 2 * i + k >= 4:
                            g.wait_ge(s_out[k], 64 * (i - 1))
                        m = g.tensor_copy(sidx[:, k, :], flat[:, bass.ds((2 * i + k - 2) * 4, 4)])
                        pool.done(m, ("si", k))
                        pool.wait(g, ("si", k), i)
                        dve.wait(g, ("ev1", k), i)
                        self.settle(g)
                        for q in range(4):
                            g.indirect_dma_start(out, bass.IndirectOffsetOnAxis(sidx[:, k, q:q + 1], 0),
                                                 eo[:, k, q, :], None, compute_op=ALU.add).then_inc(s_out[k], 16)
                    else:
                        pool.skip(g, i, [("si", k)])
                    if p.rows:
                        act.wait(g, ("wdh", k), i)
                        pool.done(split_weights("lo", g, 2, k), ("wdl", k))
                    else:
                        pool.skip(g, i, [("wdl", k)])
                stream(g, body)
                for k in range(2):
                    g.wait_ge(s_out[k], 64 * (J // 2))

    def ffn(self, x, out):
        with self.scope() as st:
            self.scores = st.sb("scores", [P, NT, E])
            self.idx = st.sb("idx", [P, E, B, CAP // P], self.i32)
            self.ln_router(x)
            self.route()
            self.experts(x, out, True)
            self.experts(x, out, False)


    def projections(self, x):
        nc, ALU, ACT, bass, AX = self.nc, self.ALU, self.ACT, self.bass, self.AX
        HF = HD // 2
        LO = 32
        with self.scope() as t, nc.Block() as blk:
            raw = t.sb("raw", [P, DC, 3 * D])
            w = [t.sb(f"w{h}", [P, DC, 3 * D], self.f32r) for h in range(2)]
            bias_raw, bias_hi = t.sb("bias_raw", [LO + 1, 3 * D]), t.sb("bias_hi", [LO + 1, 3 * D], self.f32r)
            bias = t.sb("bias", [LO + 1, 3 * D], self.f32r)
            ones = t.sb("ones", [LO + 1, P], self.f32r)
            head_of = t.sb("head_of", [P, 32], self.bf16)
            rope = t.sb("rope", [P, NT, 2, HD])
            xq = t.sb("xq", [P, 2, 4, D])
            xn = t.sb("xn", [P, 2, 4, D])
            st6, mv = t.sb("st6", [P, 4, 6]), t.sb("mv", [P, 4, 2])
            std, rstd, shift = t.sb("std", [P, 4]), t.sb("rstd", [P, 4]), t.sb("shift", [P, 4])
            xT = [t.sb(f"xT{h}", [P, 2, DC, 4 * P], self.f32r) for h in range(2)]
            turned = t.sb("turned", [P, 2, 2 * D])
            scaled = t.sb("scaled", [P, 2, 2 * D])
            roped = t.sb("roped", [P, 2, 2 * D])
            half = [t.sb(f"half{h}", [P, 2, 4, 4 * P], self.f32r) for h in range(2)]
            squares = t.sb("squares", [P, 4, 4 * P], self.bf16)
            vt = t.sb("vt", [P, 2, 4, H, VW])
            norm, top = t.sb("norm", [P, 1]), t.sb("top", [P, 1])
            best, prod = t.sb("best", [1, 2]), t.sb("prod", [1, 1])
            zero = t.sb("zero", [B * H, 2 * S])
            pX = t.ps("pX", [P, DC, 4 * P])
            pQ = t.ps("pQ", [P, 2, 2 * D])
            pV = t.ps("pV", [P, 512])
            pR = t.ps("pR", [P, 2, 4, P])
            pN = t.ps("pN", [P, 4 * P])

            per = lambda *names: [(n, k) for k in range(2) for n in names]
            pe = t.steps("pe", per("A0", "V0", "N", "A1", "V1", "R0", "A2", "V2", "R1", "A3", "V3", "R2", "T0", "T1", "R3"))
            act = t.steps("act", per("v0", "v1", "rh0", "std", "v2", "rh1", "v3", "rh2", "xh0", "xh1", "rh3", "sq"))
            dve = t.steps("dve", per("cs0", "sn0", "cs1", "sn1", "rl0", "norm", "top",
                                     "stats", "mv", "rstd", "shift", "xn",
                                     "cs2", "sn2", "rl1", "cs3", "sn3", "rl2", "xl0", "xl1", "rl3"))
            pool = t.steps("pool", per(*(f"ad{j}" for j in range(4))))
            s_w, s_wh, s_wl, s_c, s_b = (t.sem(n) for n in ("w", "wh", "wl", "const", "bias"))
            s_x = [t.sem(f"x{k}") for k in range(2)]
            s_out = [t.sem(f"out{k}") for k in range(2)]
            s_zero, s_one, s_flag, s_tt = t.sem("zero"), t.sem("one"), t.sem("flag"), t.sem("top_t")
            J = NQ
            NOUT = 16 * 7
            xv = x.rearrange("(q t p) d -> q p t d", t=4, p=P)

            def stream(eng, body):
                def both(i):
                    for k in range(2):
                        s_ = 2 * i + k if isinstance(i, int) else None
                        body(i, k, s_ is None or s_ < J, s_ is None or 1 <= s_ <= J, s_ is None or s_ >= 2)
                passes(eng, J // 2 + 1, both)

            def back(k, d=1):
                return (k - d) % 2, (k - d) // 2

            def two_before(k, j):
                return (j - 2, k, 0) if j >= 2 else (j + 2, *back(k))

            @blk.sync
            def _(sp):
                sp.dma_start(raw[:, :, 0:2 * D], self.ins["WqkT"].rearrange("(c p) f -> p c f", p=P)).then_inc(s_w, 16)
                sp.dma_start(raw[:, :, 2 * D:], self.ins["WvT"].rearrange("(c p) f -> p c f", p=P)).then_inc(s_w, 16)
                for row in (0, LO):
                    sp.dma_start(bias_raw[row:row + 1, :], self.ins["b_qkvo"][0:1, 0:3 * D]).then_inc(s_b, 16)
                sp.dma_start(rope[:, :, :, :], self.ins["c_rope"]).then_inc(s_c, 16)
                sp.wait_ge(s_one, 3)
                sp.dma_start(self.shift.rearrange("h c s -> h (c s)"), zero[:, :]).then_inc(s_zero, 16)

                def body(i, k, rows, up, norms):
                    kb, db = back(k)
                    if rows:
                        dve.wait(sp, ("xn", k), i, -1)
                        sp.dma_start(xq[:, k, :, :], xv[2 * i + k]).then_inc(s_x[k], 16)
                    if up:
                        q = 2 * (i + db) + kb
                        dve.wait(sp, ("rl3", k), i)
                        bb, cc = q // (NQ // B), q % (NQ // B)
                        for a_ in range(2):
                            for r, part in enumerate(TRIPLE[a_]):
                                dst = self.qk[a_].rearrange("(b c p r) s -> b r p c s", b=B, p=P, r=3)[bb][r]
                                sp.dma_start(dst[:, :, bass.ds(cc * 4 * P, 4 * P)],
                                             half[part][:, kb, 2 * a_:2 * a_ + 2, :].bitcast(self.f32)).then_inc(s_out[kb], 16)
                        sp.dma_start(self.vals.rearrange("(q t p) w -> q p t w", t=4, p=P)[q],
                                     vt[:, kb, :, :, :].rearrange("p t h w -> p t (h w)")).then_inc(s_out[kb], 16)
                stream(sp, body)
                for k in range(2):
                    sp.wait_ge(s_out[k], NOUT * (J // 2))
                sp.wait_ge(s_zero, 16)

            @blk.tensor
            def _(t_):
                def product(o, kb, j, lo, hi):
                    t_.matmul(o, ones[:, :], bias[:, lo:hi], start=True, stop=False)
                    for c in range(DC):
                        x_hi, x_lo = (xT[h][:, kb, c, j * P:(j + 1) * P] for h in range(2))
                        t_.matmul(o, x_hi, w[0][:, c, lo:hi], start=False, stop=False)
                        t_.matmul(o, x_hi, w[1][:, c, lo:hi], start=False, stop=False)
                        m = t_.matmul(o, x_lo, w[0][:, c, lo:hi], start=False, stop=c == DC - 1)
                    return m

                def tile(i, k, j):
                    kb, db = back(k)
                    jb, kj, dj = two_before(k, j)
                    dve.wait(t_, (f"sn{jb}", kj), i, dj)
                    pe.done(product(pQ[:, j % 2, :], kb, j, 0, 2 * D), (f"A{j}", k))
                    act.wait(t_, (f"v{j - 1}", k) if j else ("v3", kb), i, 0 if j else db)
                    pe.done(product(pV[:, 0:D], kb, j, 2 * D, 3 * D), (f"V{j}", k))

                def turn(i, k, j):
                    jb, kj, dj = two_before(k, j)
                    pool.wait(t_, (f"ad{j}", k), i)
                    dve.wait(t_, (f"rl{jb}", kj), i, dj)
                    for c in range(4):
                        m = t_.transpose(pR[:, j % 2, c, :], roped[:, j % 2, c * P:(c + 1) * P], self.ident[:, :])
                    pe.done(m, (f"R{j}", k))

                def body(i, k, rows, up, norms):
                    kb, db = back(k)
                    if up:
                        dve.wait(t_, ("xl1", kb), i, db)
                        t_.wait_ge(s_wl, 2)
                        tile(i, k, 0)
                    else:
                        pe.skip(t_, i, [("A0", k), ("V0", k)])
                    if norms:
                        act.wait(t_, ("sq", kb), i, db)
                        dve.wait(t_, ("norm", kb), i, db)
                        for c in range(4):
                            m = t_.matmul(pN[32 * c:32 * c + 32, :], head_of[:, :], squares[:, c, :], start=True, stop=True)
                        pe.done(m, ("N", k))
                    else:
                        pe.skip(t_, i, [("N", k)])
                    if up:
                        tile(i, k, 1)
                        turn(i, k, 0)
                        tile(i, k, 2)
                        turn(i, k, 1)
                        tile(i, k, 3)
                        turn(i, k, 2)
                    else:
                        pe.skip(t_, i, [(n_, k) for n_ in ("A1", "V1", "R0", "A2", "V2", "R1", "A3", "V3", "R2")])
                    if rows:
                        dve.wait(t_, ("xn", k), i)
                        for c in range(DC):
                            dve.wait(t_, (f"xl{c}", kb), i, db)
                            for j in range(4):
                                m = t_.transpose(pX[:, c, j * P:(j + 1) * P], xn[:, k, j, c * P:(c + 1) * P], self.ident[:, :])
                            pe.done(m, (f"T{c}", k))
                    else:
                        pe.skip(t_, i, [("T0", k), ("T1", k)])
                    if up:
                        turn(i, k, 3)
                    else:
                        pe.skip(t_, i, [("R3", k)])
                stream(t_, body)
                t_.wait_ge(s_flag, 1)
                t_.transpose(pN[0:1, 0:P], top[:, :], self.ident[:, :]).then_inc(s_tt, 1)

            @blk.scalar
            def _(a):
                a.wait_ge(s_w, 32)
                a.activation(w[0][:, :, :], raw[:, :, :], ACT.Copy).then_inc(s_wh, 1)
                a.wait_ge(s_b, 32)
                a.wait_ge(s_one, 8)
                for row in (0, LO):
                    m = a.activation(bias_hi[row:row + 1, :], bias_raw[row:row + 1, :], ACT.Copy)
                a.activation(bias[0:1, :], bias_raw[0:1, :], ACT.Copy).then_inc(s_wh, 1)

                def value(i, k, j, up):
                    if not up:
                        return act.skip(a, i, [(f"v{j}", k)])
                    kb, db = back(k)
                    pe.wait(a, (f"V{j}", k), i)
                    a.wait_ge(s_one, 4)
                    if j == 0 and not (isinstance(i, int) and 2 * i + k < 3):
                        a.wait_ge(s_out[kb], NOUT * (i + db))
                    act.done(a.activation(vt[:, kb, j, :, 0:HD], pV[:, 0:D].rearrange("p (h w) -> p h w", w=HD), ACT.Copy),
                             (f"v{j}", k))

                def high(i, k, j, up):
                    if not up:
                        return act.skip(a, i, [(f"rh{j}", k)])
                    kb, db = back(k)
                    pe.wait(a, (f"R{j}", k), i)
                    if j == 0 and not (isinstance(i, int) and 2 * i + k < 3):
                        a.wait_ge(s_out[kb], NOUT * (i + db))
                        act.wait(a, ("sq", k), i, -1)
                    act.done(a.activation(half[0][:, kb, :, j * P:(j + 1) * P], pR[:, j % 2, :, :], ACT.Copy), (f"rh{j}", k))

                def body(i, k, rows, up, norms):
                    kb, db = back(k)
                    value(i, k, 0, up)
                    value(i, k, 1, up)
                    high(i, k, 0, up)
                    if rows:
                        dve.wait(a, ("mv", k), i)
                        act.done(a.activation(std[:, :], mv[:, :, 1], ACT.Sqrt, bias=self.eps[:, :]), ("std", k))
                    else:
                        act.skip(a, i, [("std", k)])
                    value(i, k, 2, up)
                    high(i, k, 1, up)
                    value(i, k, 3, up)
                    high(i, k, 2, up)
                    if rows:
                        for c in range(DC):
                            pe.wait(a, (f"T{c}", k), i)
                            pe.wait(a, ("V3", kb), i, db)
                            act.done(a.activation(xT[0][:, k, c, :], pX[:, c, :], ACT.Copy), (f"xh{c}", k))
                    else:
                        act.skip(a, i, [("xh0", k), ("xh1", k)])
                    high(i, k, 3, up)
                    if up:
                        act.wait(a, ("rh3", k), i)
                        pe.wait(a, ("N", k), i)
                        act.done(a.activation(squares[:, :, :], half[0][:, kb, :, :].bitcast(self.f32), ACT.Square), ("sq", k))
                    else:
                        act.skip(a, i, [("sq", k)])
                stream(a, body)

            @blk.vector
            def _(v):
                v.memset(top[:, :], 0.0).then_inc(s_one, 1)
                v.memset(zero[:, :], 0.0).then_inc(s_one, 1)
                v.memset(vt[:, :, :, :, :], 0.0).then_inc(s_one, 1)
                v.wait_ge(s_one, 3)
                v.memset(vt[:, :, :, :, HD:HD + 1], 1.0).then_inc(s_one, 1)
                v.memset(bias[:, :].bitcast(self.f32), 0.0).then_inc(s_one, 1)
                v.memset(ones[:, :].bitcast(self.f32), 1.0).then_inc(s_one, 1)
                v.memset(head_of[:, :], 0.0).then_inc(s_one, 1)
                v.wait_ge(s_one, 7)
                with nc.allow_low_precision(reason="zeros and ones"):
                    v.tensor_reduce(head_of[:, 0:P // HD], self.ident[:, :].rearrange("p (h w) -> p h w", w=HD),
                                    AX.X, ALU.add).then_inc(s_one, 1)
                v.wait_ge(s_one, 8)
                v.wait_ge(s_wh, 2)
                v.tensor_tensor(w[1][:, :, :], raw[:, :, :], w[0][:, :, :].bitcast(self.f32), ALU.subtract).then_inc(s_wl, 1)
                v.tensor_tensor(bias[LO:LO + 1, :], bias_raw[LO:LO + 1, :], bias_hi[LO:LO + 1, :].bitcast(self.f32),
                                ALU.subtract).then_inc(s_wl, 1)
                v.wait_ge(s_c, 16)

                def tile(i, k, j, up):
                    names = [(f"cs{j}", k), (f"sn{j}", k)]
                    if not up:
                        return dve.skip(v, i, names)
                    kb, db = back(k)
                    jb, kj, dj = two_before(k, j)
                    n = j % 2
                    tile_ = 4 * (2 * (i + db) + kb) + j
                    table = rope[:, :, :, :].rearrange("p t c w -> p (t c w)")
                    pe.wait(v, (f"A{j}", k), i)
                    pool.wait(v, (f"ad{jb}", kj), i, dj)
                    heads = lambda a_: a_.rearrange("p (h w) -> p h w", w=HD)
                    cs = table[:, bass.ds(tile_ * 2 * HD, HD)]
                    dve.done(v.tensor_tensor(heads(scaled[:, n, :]), heads(pQ[:, n, :]),
                                             cs.unsqueeze(1).to_broadcast([P, 2 * H, HD]), ALU.mult), names[0])
                    src = pQ[:, n, :].rearrange("p (h r w) -> p h r w", r=2, w=HF)
                    dst = turned[:, n, :].rearrange("p (h r w) -> p h r w", r=2, w=HF)
                    for r in range(2):
                        sn = table[:, bass.ds(tile_ * 2 * HD + HD + r * HF, HF)]
                        m = v.tensor_tensor(dst[:, :, r, :], src[:, :, 1 - r, :],
                                            sn.unsqueeze(1).to_broadcast([P, 2 * H, HF]), ALU.mult)
                    dve.done(m, names[1])

                def low(i, k, j, up):
                    if not up:
                        return dve.skip(v, i, [(f"rl{j}", k)])
                    kb, db = back(k)
                    act.wait(v, (f"rh{j}", k), i)
                    dve.done(v.tensor_tensor(half[1][:, kb, :, j * P:(j + 1) * P], pR[:, j % 2, :, :],
                                             half[0][:, kb, :, j * P:(j + 1) * P].bitcast(self.f32), ALU.subtract), (f"rl{j}", k))

                def body(i, k, rows, up, norms):
                    kb, db = back(k)
                    tile(i, k, 0, up)
                    tile(i, k, 1, up)
                    low(i, k, 0, up)
                    if norms:
                        pe.wait(v, ("N", k), i)
                        dve.wait(v, ("top", kb), i, db)
                        dve.done(v.tensor_reduce(norm[:, :], pN[:, :], AX.X, ALU.max), ("norm", k))
                        dve.wait(v, ("norm", k), i)
                        dve.done(v.tensor_tensor(top[:, :], top[:, :], norm[:, :], ALU.max), ("top", k))
                    else:
                        dve.skip(v, i, [("norm", k), ("top", k)])
                    if rows:
                        v.wait_ge(s_x[k], 16 * (i + 1))
                        dve.wait(v, ("mv", kb), i, db)
                        for j in range(4):
                            m = v.bn_stats(st6[:, j, :], xq[:, k, j, :])
                        dve.done(m, ("stats", k))
                        dve.wait(v, ("stats", k), i)
                        act.wait(v, ("std", kb), i, db)
                        dve.wait(v, ("shift", kb), i, db)
                        self.settle(v)
                        for j in range(4):
                            m = v.bn_aggr(mv[:, j, :], st6[:, j, :])
                        dve.done(m, ("mv", k))
                        act.wait(v, ("std", k), i)
                        dve.wait(v, ("xn", kb), i, db)
                        dve.done(v.reciprocal(rstd[:, :], std[:, :]), ("rstd", k))
                        dve.wait(v, ("rstd", k), i)
                        dve.done(v.scalar_tensor_tensor(shift[:, :], mv[:, :, 0], -1.0, rstd[:, :],
                                                        ALU.mult, ALU.mult), ("shift", k))
                        dve.wait(v, ("shift", k), i)
                        pe.wait(v, ("T1", k), i, -1)
                        for j in range(4):
                            m = v.tensor_scalar(xn[:, k, j, :], xq[:, k, j, :], rstd[:, j:j + 1],
                                                shift[:, j:j + 1], ALU.mult, ALU.add)
                        dve.done(m, ("xn", k))
                    else:
                        dve.skip(v, i, [(n_, k) for n_ in ("stats", "mv", "rstd", "shift", "xn")])
                    tile(i, k, 2, up)
                    low(i, k, 1, up)
                    tile(i, k, 3, up)
                    low(i, k, 2, up)
                    if rows:
                        for c in range(DC):
                            act.wait(v, (f"xh{c}", k), i)
                            dve.done(v.tensor_tensor(xT[1][:, k, c, :], pX[:, c, :], xT[0][:, k, c, :].bitcast(self.f32),
                                                     ALU.subtract), (f"xl{c}", k))
                    else:
                        dve.skip(v, i, [("xl0", k), ("xl1", k)])
                    low(i, k, 3, up)
                stream(v, body)
                dve.wait(v, ("top", 1), J // 2)
                v.engine_nop().then_inc(s_flag, 1)
                v.wait_ge(s_tt, 1)
                v.tensor_reduce(best[:, :], pN[0:1, 0:P].rearrange("p (a h) -> p a h", a=2), AX.X, ALU.max).then_inc(s_flag, 1)
                v.wait_ge(s_flag, 2)
                v.tensor_tensor(prod[:, :], best[:, 0:1], best[:, 1:2], ALU.mult).then_inc(s_flag, 1)
                v.wait_ge(s_flag, 3)
                v.tensor_scalar(self.unsafe[:, :], prod[:, :], SAFE_NORMS, None, ALU.is_gt).then_inc(s_flag, 1)
                v.wait_ge(s_flag, 4)

            @blk.gpsimd
            def _(g):
                def body(i, k, rows, up, norms):
                    if not up:
                        return pool.skip(g, i, [(f"ad{j}", k) for j in range(4)])
                    for j in range(4):
                        jb, kj, dj = two_before(k, j)
                        dve.wait(g, (f"sn{j}", k), i)
                        pe.wait(g, (f"R{jb}", kj), i, dj)
                        pool.done(g.tensor_tensor(roped[:, j % 2, :], scaled[:, j % 2, :], turned[:, j % 2, :], ALU.add),
                                  (f"ad{j}", k))
                stream(g, body)

    def exact_shift(self):
        nc, ALU, ACT, bass, AX = self.nc, self.ALU, self.ACT, self.bass, self.AX
        KR, NEG = 3 * HD, -1e30
        OFF = S - P
        with self.scope() as t, nc.Block() as blk:
            qa, ka = t.sb("qa", [KR, S], self.f32r), t.sb("ka", [KR, S], self.f32r)
            qc = t.sb("qc", [KR, P], self.f32r)
            mask = t.sb("mask", [P, OFF + S], self.bf16)
            ident = t.sb("ident", [P, P], self.bf16)
            mx = t.sb("mx", [P, TPB])
            halves = t.sb("halves", [TPB, 2, P], self.f32r)
            pS = t.ps("pS", [P, S])
            pM = t.ps("pM", [TPB, 512])
            dve_t = t.steps("dve_tile", ["query", "max"])
            pe_t = t.steps("pe_tile", ["scores"])
            dve_h = t.steps("dve_head", ["hi", "lo"])
            pe_h = t.steps("pe_head", ["turned"])
            s_ld, s_st, s_go = t.sem("load"), t.sem("store"), t.sem("go")
            s_mask, s_ident = t.sem("mask"), t.sem("ident")

            def guarded(eng, body):
                r = eng.value_load(self.unsafe[0:1, 0:1], min_val=0, max_val=1)
                with eng.If(r > 0):
                    body(eng)
                eng.end_ifs()

            def heads(eng, body):
                with eng.Fori(0, B * H) as h:
                    body(h)

            @blk.sync
            def _(sp):
                def run(sp):
                    def head(h):
                        sp.wait_ge(s_go, h + 1)
                        sp.dma_start(qa[:, :].bitcast(self.f32), self.qk[0][bass.ds(h * KR, KR), :]).then_inc(s_ld, 16)
                        sp.dma_start(ka[:, :].bitcast(self.f32), self.qk[1][bass.ds(h * KR, KR), :]).then_inc(s_ld, 16)
                        dve_h.wait(sp, "lo", h)
                        sp.dma_start(self.shift.rearrange("h c (t p) -> h t c p", p=P)[h],
                                     halves[:, :, :].bitcast(self.f32)).then_inc(s_st, 16)
                    heads(sp, head)
                    sp.wait_ge(s_st, 16 * B * H)
                guarded(sp, run)

            @blk.gpsimd
            def _(g):
                def run(g):
                    g.memset(mask[:, :], 0.0).then_inc(s_mask, 1)
                    g.wait_ge(s_mask, 1)
                    g.affine_select(out=mask[:, :], in_=mask[:, :], compare_op=ALU.is_ge, fill=NEG, base=OFF,
                                    pattern=[[-1, OFF + S]], channel_multiplier=1).then_inc(s_mask, 1)
                guarded(g, run)

            @blk.vector
            def _(v):
                def run(v):
                    v.tensor_copy(ident[:, :], self.ident[:, :]).then_inc(s_ident, 1)
                    v.sem_inc(s_go, 1)

                    def head(h):
                        v.wait_ge(s_ld, 32 * h + 32)

                        def tile(q):
                            n = h * TPB + q
                            dve_t.done(v.tensor_copy(qc[:, :], qa[:, bass.ds(q * P, P)].bitcast(self.f32)), "query")
                            pe_t.wait(v, "scores", n)
                            dve_t.done(v.tensor_reduce(mx[:, bass.ds(q, 1)], pS[:, :], AX.X, ALU.max), "max")
                            dve_t.wait(v, "max", n)
                        self.settle(v)
                        with v.Fori(0, TPB) as q:
                            tile(q)
                        pe_h.wait(v, "turned", h)
                        dve_h.done(v.tensor_scalar(halves[:, 0, :], pM[:, 0:P], -1.0, None, ALU.mult), "hi")
                        dve_h.wait(v, "hi", h)
                        dve_h.done(v.scalar_tensor_tensor(halves[:, 1, :], pM[:, 0:P], -1.0,
                                                          halves[:, 0, :].bitcast(self.f32), ALU.mult, ALU.subtract), "lo")
                        v.wait_ge(s_st, 16 * h + 16)
                        v.sem_inc(s_go, 1)
                    heads(v, head)
                guarded(v, run)

            @blk.tensor
            def _(t_):
                def run(t_):
                    t_.wait_ge(s_mask, 2)
                    t_.wait_ge(s_ident, 1)

                    def head(h):
                        with t_.Fori(0, TPB) as q:
                            dve_t.wait(t_, "query", h * TPB + q)
                            for c in range(S // 512):
                                o = pS[:, c * 512:(c + 1) * 512]
                                t_.matmul(o, qc[:, :], ka[:, c * 512:(c + 1) * 512], start=True, stop=False)
                                m = t_.matmul(o, ident[:, :], mask[:, bass.ds(q * -P + (OFF + c * 512), 512)],
                                              start=False, stop=True)
                            pe_t.done(m, "scores")
                        dve_t.wait(t_, "max", h * TPB + (TPB - 1))
                        pe_h.done(t_.transpose(pM[:, 0:P], mx[:, :], self.ident[:, :]), "turned")
                    heads(t_, head)
                guarded(t_, run)

    def attention(self):
        nc, ALU, ACT, bass = self.nc, self.ALU, self.ACT, self.bass
        NG, GH = B * H // 4, 4
        QB = S // 512
        KR = 3 * HD + 2
        with self.scope() as t, nc.Block() as blk:
            sq = t.sb("sq", [P, 2, GH, S], self.f32r)
            sk = t.sb("sk", [P, 2, 2, S], self.f32r)
            vg = t.sb("vg", [P, 2, TPB, GH * VW])
            pr = t.sb("pr", [P, 2, GH, 512])
            oT = t.sb("oT", [P, 2, 512])
            rs = t.sb("rs", [P, 2, 4, GH])
            yo = t.sb("yo", [P, 2, 4, GH, HD])
            pS = t.ps("pS", [P, 3, 2, 512])
            pO = t.ps("pO", [P, 512])
            pT = t.ps("pT", [P, 4, P])

            work = [(k, qb, kt) for k in range(2) for qb in range(QB) for kt in range(4 * qb + 4)]
            NS = len(work)
            last = [n for n, (k, qb, kt) in enumerate(work) if kt == 4 * qb + 3]
            diag = lambda n: work[n][2] - 4 * work[n][1] >= 0

            def span(n):
                k, qb, kt = work[n]
                lo = max(qb * 512, kt * P)
                return lo, (qb + 1) * 512 - lo

            pe_names = [("S", 0, 0), ("S", 0, 1)]
            for n in range(NS):
                if n + 1 < NS:
                    pe_names.append(("S", n + 1, 0))
                pe_names.append(("O", n))
                if n + 1 < NS:
                    pe_names.append(("S", n + 1, 1))
                if n - 1 in last:
                    pe_names.append(("T", n - 1))
            pe_names.append(("T", NS - 1))
            pe = t.steps("pe", pe_names)
            act = t.steps("act", [("exp", n, h) for n in range(NS) for h in range(2)])
            pool = t.steps("pool", [("mask", n) for n in range(NS) if diag(n)])
            dve = t.steps("dve", [(a_, n) for n in last for a_ in ("copy", "rs", "y")])
            s_ld = [t.sem(f"ld{k}") for k in range(2)]
            s_y = [t.sem(f"y{k}") for k in range(2)]
            s_init = t.sem("init")
            loads = 3 * GH + 1

            @blk.sync
            def _(sp):
                sp.wait_ge(s_init, 2)

                def body(i):
                    for k in range(2):
                        lastk = max(n for n in range(NS) if work[n][0] == k)
                        pe.wait(sp, ("O", lastk), i, -1)
                        g = 2 * i + k
                        for hh in range(GH):
                            pair, base = hh // 2, 64 * (hh % 2)
                            for dst, tab in ((sq[:, k, hh, :], 0), (sk[:, k, pair, :], 1)):
                                sp.dma_start(dst[base:base + 3 * HD, :].bitcast(self.f32),
                                             self.qk[tab][bass.ds((g * GH + hh) * 3 * HD, 3 * HD), :]).then_inc(s_ld[k], 16)
                            sp.dma_start(sq[base + 3 * HD:base + KR, k, hh, :].bitcast(self.f32),
                                         self.shift.rearrange("h c s -> (h c) s")[bass.ds((g * GH + hh) * 2, 2), :]
                                         ).then_inc(s_ld[k], 16)
                        vv = self.vals.rearrange("(b t p) w -> b p t w", b=B, p=P)[g // (NG // B)]
                        sp.dma_start(vg[:, k, :, :], vv[:, :, bass.ds((g % (NG // B)) * (GH * VW), GH * VW)]).then_inc(s_ld[k], 16)
                passes(sp, NG // 2, body)

            @blk.tensor
            def _(t_):
                def scores(i, n, h):
                    k, qb, kt = work[n]
                    u = 2 * n + h
                    if u >= 3:
                        act.wait(t_, ("exp", (u - 3) // 2, (u - 3) % 2), i)
                    else:
                        lb = max(x_ for x_ in range(2 * NS) if x_ % 3 == u % 3)
                        act.wait(t_, ("exp", lb // 2, lb % 2), i, -1)
                    lo, wd = span(n)
                    for e in range(2):
                        m = t_.matmul(pS[:, u % 3, e, 0:wd], sk[:, k, h, kt * P:(kt + 1) * P],
                                      sq[:, k, 2 * h + e, lo:lo + wd], start=True, stop=True)
                    pe.done(m, ("S", n, h))

                def values(i, n):
                    k, qb, kt = work[n]
                    act.wait(t_, ("exp", n, 1), i)
                    if diag(n):
                        pool.wait(t_, ("mask", n), i)
                    if kt == 0:
                        j = last.index(next(x_ for x_ in last if x_ >= n))
                        dve.wait(t_, ("copy", last[j - 1]), i, 0 if j else -1)
                    lo, wd = span(n)
                    off = lo - qb * 512
                    for e in range(GH):
                        m = t_.matmul(pO[e * VW:(e + 1) * VW, off:off + wd], vg[:, k, kt, e * VW:(e + 1) * VW],
                                      pr[:, n % 2, e, 0:wd], start=kt == 0, stop=kt == 4 * qb + 3)
                    pe.done(m, ("O", n))

                def turn(i, n):
                    j = last.index(n)
                    dve.wait(t_, ("copy", n), i)
                    dve.wait(t_, ("y", last[j - 1]), i, 0 if j else -1)
                    for q in range(4):
                        m = t_.transpose(pT[:, q, :], oT[:, j % 2, q * P:(q + 1) * P], self.ident[:, :])
                    pe.done(m, ("T", n))

                def body(i):
                    t_.wait_ge(s_ld[0], 16 * loads * (i + 1))
                    scores(i, 0, 0)
                    scores(i, 0, 1)
                    for n in range(NS):
                        if n + 1 < NS:
                            if work[n + 1][0] != work[n][0]:
                                t_.wait_ge(s_ld[1], 16 * loads * (i + 1))
                            scores(i, n + 1, 0)
                        values(i, n)
                        if n + 1 < NS:
                            scores(i, n + 1, 1)
                        if n - 1 in last:
                            turn(i, n - 1)
                    turn(i, NS - 1)
                passes(t_, NG // 2, body)

            @blk.scalar
            def _(a):
                def body(i):
                    for n in range(NS):
                        lo, wd = span(n)
                        for h in range(2):
                            u = 2 * n + h
                            pe.wait(a, ("S", n, h), i)
                            if h == 0:
                                pe.wait(a, ("O", (n - 2) % NS), i, 0 if n >= 2 else -1)
                            act.done(a.activation(pr[:, n % 2, 2 * h:2 * h + 2, 0:wd], pS[:, u % 3, :, 0:wd], ACT.Exp,
                                                  scale=HD ** -0.5), ("exp", n, h))
                passes(a, NG // 2, body)

            yv = self.y.rearrange("(b q t p) d -> b q p t d", b=B, q=QB, p=P)

            def store(eng, i, n):
                k, qb, kt = work[n]
                dve.wait(eng, ("y", n), i)
                g, jj = 2 * i + k, last.index(n) % 2
                dst = yv[g // (NG // B)][qb][:, :, bass.ds((g % (NG // B)) * GH * HD, GH * HD)]
                eng.dma_start(dst, yo[:, jj, :, :, :].rearrange("p t h w -> p t (h w)")).then_inc(s_y[jj], 16)

            @blk.gpsimd
            def _(g):
                def body(i):
                    for n in range(NS):
                        if n - 3 in last:
                            store(g, i, n - 3)
                        if diag(n):
                            act.wait(g, ("exp", n, 1), i)
                            self.settle(g)
                            blk_ = pr[:, n % 2, :, 0:P]
                            pool.done(g.affine_select(out=blk_, in_=blk_, compare_op=ALU.is_ge, fill=0.0, base=0,
                                                      pattern=[[0, GH], [1, P]], channel_multiplier=-1), ("mask", n))
                    store(g, i, NS - 1)
                passes(g, NG // 2, body)
                for k in range(2):
                    g.wait_ge(s_y[k], 16 * (NG // 2) * len(last) // 2)

            @blk.vector
            def _(v):
                v.memset(sq[:, :, :, :].bitcast(self.f32), 0.0).then_inc(s_init, 1)
                v.memset(sk[:, :, :, :].bitcast(self.f32), 1.0).then_inc(s_init, 1)

                def body(i):
                    for j, n in enumerate(last):
                        k, qb, kt = work[n]
                        jj = j % 2
                        pe.wait(v, ("O", n), i)
                        pe.wait(v, ("T", last[j - 2]), i, 0 if j >= 2 else -1)
                        dve.done(v.tensor_copy(oT[:, jj, :], pO[:, :]), ("copy", n))
                        pe.wait(v, ("T", n), i)
                        heads = pT[:, :, :].rearrange("p t (h w) -> p t h w", w=VW)
                        dve.wait(v, ("y", last[j - 2]), i, 0 if j >= 2 else -1)
                        dve.done(v.reciprocal(rs[:, jj, :, :], heads[:, :, :, HD]), ("rs", n))
                        dve.wait(v, ("rs", n), i)
                        cnt = i * (len(last) // 2) + j // 2
                        if not (isinstance(cnt, int) and cnt == 0):
                            v.wait_ge(s_y[jj], 16 * cnt)
                        dve.done(v.tensor_tensor(yo[:, jj, :, :, :], heads[:, :, :, 0:HD],
                                                 rs[:, jj, :, :].unsqueeze(3).to_broadcast([P, 4, GH, HD]), ALU.mult), ("y", n))
                passes(v, NG // 2, body)


    def output(self, x, out):
        nc, ALU, ACT = self.nc, self.ALU, self.ACT
        with self.scope() as t, nc.Block() as blk:
            raw = t.sb("raw", [P, DC, D])
            w = [t.sb(f"w{h}", [P, DC, D], self.f32r) for h in range(2)]
            bias = t.sb("bias", [P, D])
            yq, xq, xb, ob = (t.sb(n_, [P, 2, 4, D]) for n_ in ("yq", "xq", "xb", "ob"))
            yT = [t.sb(f"yT{h}", [P, 2, DC, 4 * P], self.f32r) for h in range(2)]
            pX = t.ps("pX", [P, DC, 4 * P])
            pO = t.ps("pO", [P, 4, 512])
            per = lambda *names: [(n, k) for k in range(2) for n in names]
            pe = t.steps("pe", per("T0", "T1", "O0", "O1", "O2", "O3"))
            act = t.steps("act", per("yh0", "yh1"))
            dve = t.steps("dve", per("yl0", "yl1", "o0", "o1", "o2", "o3"))
            pool = t.steps("pool", per("xb"))
            s_w, s_wh, s_wl = t.sem("w"), t.sem("wh"), t.sem("wl")
            s_y = [t.sem(f"y{k}") for k in range(2)]
            s_x = [t.sem(f"x{k}") for k in range(2)]
            s_out = [t.sem(f"out{k}") for k in range(2)]
            J = NQ
            quads = lambda a_: a_.rearrange("(q t p) d -> q p t d", t=4, p=P)

            @blk.sync
            def _(sp):
                sp.dma_start(raw[:, :, :], self.ins["WoT"].rearrange("(c p) f -> p c f", p=P)).then_inc(s_w, 16)
                sp.dma_start(bias[:, :], self.ins["b_qkvo"][0:1, 3 * D:4 * D].partition_broadcast(P)).then_inc(s_w, 16)

                def body(i):
                    for k in range(2):
                        pe.wait(sp, ("T1", k), i, -1)
                        sp.dma_start(yq[:, k, :, :], quads(self.y)[2 * i + k]).then_inc(s_y[k], 16)
                        pool.wait(sp, ("xb", k), i, -1)
                        sp.dma_start(xq[:, k, :, :], quads(x)[2 * i + k]).then_inc(s_x[k], 16)
                passes(sp, J // 2, body)

            @blk.tensor
            def _(t_):
                t_.wait_ge(s_wl, 1)

                def body(i):
                    for k in range(2):
                        kb, db = (k - 1) % 2, (k - 1) // 2
                        t_.wait_ge(s_y[k], 16 * (i + 1))
                        for c in range(DC):
                            dve.wait(t_, (f"yl{c}", kb), i, db)
                            for j in range(4):
                                m = t_.transpose(pX[:, c, j * P:(j + 1) * P], yq[:, k, j, c * P:(c + 1) * P], self.ident[:, :])
                            pe.done(m, (f"T{c}", k))
                        dve.wait(t_, ("yl1", k), i)
                        for j in range(4):
                            dve.wait(t_, (f"o{j}", kb), i, db)
                            o = pO[:, j, 0:D]
                            for c in range(DC):
                                y_hi, y_lo = (yT[h][:, k, c, j * P:(j + 1) * P] for h in range(2))
                                t_.matmul(o, y_hi, w[0][:, c, :], start=c == 0, stop=False)
                                t_.matmul(o, y_hi, w[1][:, c, :], start=False, stop=False)
                                m = t_.matmul(o, y_lo, w[0][:, c, :], start=False, stop=c == DC - 1)
                            pe.done(m, (f"O{j}", k))
                passes(t_, J // 2, body)

            @blk.scalar
            def _(a):
                a.wait_ge(s_w, 32)
                a.activation(w[0][:, :, :], raw[:, :, :], ACT.Copy).then_inc(s_wh, 1)

                def body(i):
                    for k in range(2):
                        for c in range(DC):
                            pe.wait(a, (f"T{c}", k), i)
                            pe.wait(a, ("O3", k), i, -1)
                            act.done(a.activation(yT[0][:, k, c, :], pX[:, c, :], ACT.Copy), (f"yh{c}", k))
                passes(a, J // 2, body)

            @blk.gpsimd
            def _(g):
                g.wait_ge(s_w, 32)

                def body(i):
                    for k in range(2):
                        g.wait_ge(s_x[k], 16 * (i + 1))
                        dve.wait(g, ("o3", k), i, -1)
                        pool.done(g.tensor_tensor(xb[:, k, :, :], xq[:, k, :, :],
                                                  bias[:, :].unsqueeze(1).to_broadcast([P, 4, D]), ALU.add), ("xb", k))
                        dve.wait(g, ("o3", k), i)
                        g.dma_start(quads(out)[2 * i + k], ob[:, k, :, :]).then_inc(s_out[k], 16)
                passes(g, J // 2, body)
                for k in range(2):
                    g.wait_ge(s_out[k], 16 * (J // 2))

            @blk.vector
            def _(v):
                v.wait_ge(s_wh, 1)
                v.tensor_tensor(w[1][:, :, :], raw[:, :, :], w[0][:, :, :].bitcast(self.f32), ALU.subtract).then_inc(s_wl, 1)

                def body(i):
                    for k in range(2):
                        for c in range(DC):
                            act.wait(v, (f"yh{c}", k), i)
                            dve.done(v.tensor_tensor(yT[1][:, k, c, :], pX[:, c, :], yT[0][:, k, c, :].bitcast(self.f32),
                                                     ALU.subtract), (f"yl{c}", k))
                        pool.wait(v, ("xb", k), i)
                        if not (isinstance(i, int) and i == 0):
                            v.wait_ge(s_out[k], 16 * i)
                        for j in range(4):
                            pe.wait(v, (f"O{j}", k), i)
                            dve.done(v.tensor_tensor(ob[:, k, j, :], pO[:, j, 0:D], xb[:, k, j, :], ALU.add), (f"o{j}", k))
                passes(v, J // 2, body)

    def attn(self, x, out):
        with self.scope() as st:
            self.unsafe = st.sb("unsafe", [1, 1], self.i32)
            self.projections(x)
            self.exact_shift()
            self.attention()
            self.output(x, out)


def build(nc, ins, out):
    prog = Program(nc, ins, out)
    with prog.scope() as st:
        prog.load_constants(st)
        prog.ffn(ins["x"], prog.x1)
        prog.attn(prog.x1, prog.x2)
        prog.ffn(prog.x2, out)


def layout(inputs):
    a = {k: np.asarray(v) for k, v in inputs.items()}
    p = np.arange(P)
    same = (p[:, None] % E == p[None, :] % E)
    masks = np.concatenate([p[:, None] <= p[None, :], np.ones((P, P)), same,
                            np.broadcast_to(np.arange(CAP), (P, CAP))], 1).astype(np.float32)
    theta = (np.float32(1.0) / np.power(np.float32(10000.0), np.arange(0, HD, 2, dtype=np.float32) / np.float32(HD))).astype(np.float32)
    ang = np.arange(1, S + 1, dtype=np.float32)[:, None] * theta[None, :]
    ang = np.concatenate([ang, ang], 1).astype(np.float64)
    sign = np.where(np.arange(HD) < HD // 2, -1.0, 1.0)
    rope = np.stack([np.cos(ang), np.sin(ang) * sign], 1).astype(np.float32)
    t = lambda w: np.ascontiguousarray(w.T)
    te = lambda w: np.ascontiguousarray(np.transpose(w, (0, 2, 1)))
    return {
        "x": a["L0_attn_x"].reshape(N, D),
        "WqkT": np.ascontiguousarray(np.concatenate([a["L0_attn_Wq"], a["L0_attn_Wk"]], 0).T),
        "WvT": t(a["L0_attn_Wv"]), "WoT": t(a["L0_attn_Wo"]),
        "b_qkvo": np.concatenate([a["L0_attn_bq"], a["L0_attn_bk"], a["L0_attn_bv"], a["L0_attn_bo"]]).reshape(1, 4 * D),
        "gate_wT": t(a["L0_ffn_gate_w"]),
        "WgT": te(a["L0_ffn_Wg"]), "WuT": te(a["L0_ffn_Wu"]), "WdT": te(a["L0_ffn_Wd"]),
        "WsgT": t(a["L0_ffn_Ws_g"]), "WsuT": t(a["L0_ffn_Ws_u"]), "WsdT": t(a["L0_ffn_Ws_d"]),
        "c_ident": np.eye(P, dtype=np.float32),
        "c_masks": masks,
        "c_bits": np.ascontiguousarray(np.broadcast_to(1 << np.arange(NBITS - 1, -1, -1), (P, NBITS))).astype(np.int32),
        "c_rope": np.ascontiguousarray(np.tile(rope.reshape(TPB, P, 2, HD).transpose(1, 0, 2, 3), (1, B, 1, 1))),
    }


def kernel(**inputs):
    import concourse.bacc as bacc
    from concourse import mybir
    from concourse.bass_utils import run_bass_kernel_spmd

    nc = bacc.Bacc("TRN2", target_bir_lowering=False, num_devices=1)
    arrays = layout(inputs)
    ins = {n: nc.dram_tensor(n, a.shape, mybir.dt.from_np(a.dtype), kind="ExternalInput").ap()
           for n, a in arrays.items()}
    out = nc.dram_tensor("out", [N, D], mybir.dt.float32, kind="ExternalOutput").ap()
    build(nc, ins, out)
    r = run_bass_kernel_spmd(nc, [arrays], core_ids=[0])
    return r.results[0]["out"].reshape(B, S, D)
```

```python
from contextlib import ExitStack

import numpy as np

B, S, D = 2, 2048, 256
N = B * S
P = 128
NT = N // P
TPB = S // P
NQ = NT // 4
E, F = 16, 512
CAP = S * 2 // E
H, HD = 16, 16
DC = D // P
FC = F // P
ROW = D + E
WQ = 16
VW = 32
EPS = 1e-5
TRIPLE = ((0, 1, 0), (0, 0, 1))
SAFE_NORMS = 14000.0
NBITS = 32


class Steps:

    def __init__(self, sem, names):
        self.sem, self.names, self.K = sem, names, len(names)
        self.at = {n: k for k, n in enumerate(names)}
        assert len(self.at) == self.K
        self.next = 0

    def value(self, name, i, d=0):
        c = self.at[name] + 1 + d * self.K
        return i * self.K + c

    def wait(self, eng, name, i, d=0):
        v = self.value(name, i, d)
        if isinstance(v, int) and v <= 0:
            return
        eng.wait_ge(self.sem, v)

    def done(self, ins, name):
        assert self.names[self.next] == name, (self.names[self.next], name)
        self.next = (self.next + 1) % self.K
        ins.then_inc(self.sem, 1)

    def skip(self, eng, i, names):
        first = self.at[names[0]]
        v = i * self.K + first
        if v > 0:
            eng.wait_ge(self.sem, v)
        for n in names:
            assert self.names[self.next] == n, (self.names[self.next], n)
            self.next = (self.next + 1) % self.K
        eng.sem_inc(self.sem, len(names))


def passes(eng, n, body, tail=1):
    body(0)
    if n > tail + 1:
        with eng.Fori(1, n - tail) as i:
            body(i)
    for i in range(max(1, n - tail), n):
        body(i)


class Program:
    def __init__(self, nc, ins, out):
        import concourse.bass as bass
        from concourse import mybir
        self.nc, self.bass, self.ins, self.out = nc, bass, ins, out
        self.f32, self.f32r = mybir.dt.float32, mybir.dt.float32r
        self.bf16, self.i32 = mybir.dt.bfloat16, mybir.dt.int32
        self.ACT, self.ALU, self.AX = mybir.ActivationFunctionType, mybir.AluOpType, mybir.AxisListType

        def dram(name, shape):
            return nc.dram_tensor(name, shape, self.f32, kind="Internal").ap()

        self.x1 = dram("x_after_ffn1", [N, D])
        self.x2 = dram("x_after_attn", [N, D])
        self.table = dram("token_table", [N, ROW])
        self.qk = [dram(n, [B * D * 3, S]) for n in ("q_rows", "k_rows")]
        self.shift = dram("shift", [B * H, 2, S])
        self.vals = dram("values", [N, H * VW])
        self.y = dram("attn_heads", [N, D])

    def settle(self, eng):
        eng.sem_inc(self.settled, 1)

    def scope(self):
        st = ExitStack()
        nc = self.nc
        tag = f"{nc.next_id()}_"
        st.sb = lambda name, shape, dt=self.f32: st.enter_context(nc.sbuf_tensor(tag + name, shape, dt))
        st.ps = lambda name, shape, dt=self.f32: st.enter_context(nc.psum_tensor(tag + name, shape, dt))
        st.sem = lambda name: st.enter_context(nc.semaphore(tag + name))
        st.steps = lambda name, names: Steps(st.sem(name), names)
        return st

    def product3(self, pe, out, w_hi, w_lo, x_hi, x_lo, start, stop):
        pe.matmul(out, w_hi, x_hi, start=start, stop=False)
        pe.matmul(out, w_hi, x_lo, start=False, stop=False)
        return pe.matmul(out, w_lo, x_hi, start=False, stop=stop)

    def load_constants(self, st):
        nc, ALU = self.nc, self.ALU
        self.ident = st.sb("ident", [P, P])
        self.tri = st.sb("tri", [P, P], self.bf16)
        self.ones = st.sb("ones", [P, P], self.bf16)
        self.same_expert = st.sb("same_expert", [P, P], self.bf16)
        self.iota = st.sb("iota", [P, WQ], self.bf16)
        route = st.sb("route", [P, P + P // WQ + 8 + 1])
        self.spread = route[:, 0:P]
        self.own_expert = route[:, P:P + P // WQ]
        self.own_column = route[:, P + P // WQ:P + P // WQ + 8]
        self.place = route[:, P + P // WQ + 8:]
        self.bits = st.sb("bits", [P, NBITS], self.i32)
        self.ones32 = st.sb("ones32", [E, P])
        self.gate = st.sb("gate", [P, DC, E])
        self.eps = st.sb("eps", [P, 1])
        self.settled = st.sem("settled")
        with self.scope() as t, nc.Block() as blk:
            raw = t.sb("raw", [P, 3 * P + WQ])
            s_in, s_id, s_cast = t.sem("in"), t.sem("ident"), t.sem("cast")

            @blk.sync
            def _(sp):
                sp.dma_start(self.ident[:, :], self.ins["c_ident"]).then_inc(s_id, 16)
                sp.dma_start(raw[:, :], self.ins["c_masks"]).then_inc(s_in, 16)
                sp.dma_start(self.bits[:, :], self.ins["c_bits"]).then_inc(s_id, 16)
                sp.dma_start(self.gate[:, :, :], self.ins["gate_wT"].rearrange("(c p) e -> p c e", p=P)).then_inc(s_id, 16)
                sp.dma_start(route[:, :], self.ins["c_route"]).then_inc(s_id, 16)
                sp.wait_ge(s_id, 64)

            @blk.vector
            def _(dve):
                dve.memset(self.ones32[:, :], 1.0)
                dve.memset(self.eps[:, :], EPS)
                dve.wait_ge(s_in, 16)
                for k, m in enumerate((self.tri, self.ones, self.same_expert)):
                    dve.tensor_copy(m[:, :], raw[:, k * P:(k + 1) * P])
                dve.tensor_copy(self.iota[:, :], raw[:, 3 * P:]).then_inc(s_cast, 1)
                dve.wait_ge(s_cast, 1)

    def ln_router(self, x):
        nc, ALU, ACT, AX = self.nc, self.ALU, self.ACT, self.AX
        scores = self.scores
        with self.scope() as t, nc.Block() as blk:
            xq = t.sb("xq", [P, 2, 4, D])
            xn = t.sb("xn", [P, 2, 4, D])
            st6 = t.sb("st6", [P, 2, 4, 6])
            mv = t.sb("mv", [P, 2, 4, 2])
            std = t.sb("std", [P, 2, 4])
            rstd = t.sb("rstd", [P, 2, 4])
            shift = t.sb("shift", [P, 2, 4])
            xT = t.sb("xT", [P, 2, DC, 4 * P])
            mx = t.sb("mx", [P, NT])
            dif = t.sb("dif", [P, NT, E])
            ex = t.sb("ex", [P, NT, E])
            pT = t.ps("pT", [P, 2, DC, 4 * P])
            pL = t.ps("pL", [P, NT * E])
            s_x = [t.sem(f"x{k}") for k in range(2)]
            s_w = [t.sem(f"w{k}") for k in range(2)]
            s_sc = t.sem("sc")
            per = lambda *names: [(n, k) for k in range(2) for n in names]
            dve = t.steps("dve", per("stats", "mv", "rstd", "shift", "xn", "xT1"))
            act = t.steps("act", per("std", "xT0"))
            pe = t.steps("pe", per("T", "L"))
            s_sm = t.sem("softmax_dve")
            s_ex = t.sem("softmax_act")
            s_rows, s_turned = t.sem("rows"), t.sem("turned")
            xv = x.rearrange("(q t p) d -> q p t d", t=4, p=P)
            tv = self.table[:, 0:D].rearrange("(q t p) d -> q p t d", t=4, p=P)

            @blk.sync
            def _(sp):
                def body(i):
                    for k in range(2):
                        dve.wait(sp, ("xn", k), i, -1)
                        sp.dma_start(xq[:, k, :, :], xv[2 * i + k]).then_inc(s_x[k], 16)
                passes(sp, NQ // 2, body)

            @blk.gpsimd
            def _(pool):
                def body(i):
                    for k in range(2):
                        dve.wait(pool, ("xn", k), i)
                        pool.dma_start(tv[2 * i + k], xn[:, k, :, :]).then_inc(s_w[k], 16)
                passes(pool, NQ // 2, body)
                for k in range(2):
                    pool.wait_ge(s_w[k], 16 * (NQ // 2))
                pool.wait_ge(s_sm, 6)
                with nc.allow_non_contiguous_dma(reason="64-byte rows"):
                    pool.dma_start(self.table[:, D:ROW].rearrange("(t p) e -> p t e", p=P),
                                   scores[:, :, :]).then_inc(s_sc, 16)
                pool.wait_ge(s_sc, 16)

            @blk.vector
            def _(v):
                def body(i):
                    for k in range(2):
                        v.wait_ge(s_x[k], 16 * (i + 1))
                        for j in range(4):
                            m = v.bn_stats(st6[:, k, j, :], xq[:, k, j, :])
                        dve.done(m, ("stats", k))
                        dve.wait(v, ("stats", k), i)
                        self.settle(v)
                        for j in range(4):
                            m = v.bn_aggr(mv[:, k, j, :], st6[:, k, j, :])
                        dve.done(m, ("mv", k))
                        act.wait(v, ("std", k), i)
                        dve.done(v.reciprocal(rstd[:, k, :], std[:, k, :]), ("rstd", k))
                        dve.wait(v, ("rstd", k), i)
                        dve.done(v.scalar_tensor_tensor(shift[:, k, :], mv[:, k, :, 0], -1.0, rstd[:, k, :],
                                                        ALU.mult, ALU.mult), ("shift", k))
                        dve.wait(v, ("shift", k), i)
                        pe.wait(v, ("T", k), i, -1)
                        if not (isinstance(i, int) and i == 0):
                            v.wait_ge(s_w[k], 16 * i)
                        for j in range(4):
                            m = v.tensor_scalar(xn[:, k, j, :], xq[:, k, j, :], rstd[:, k, j:j + 1],
                                                shift[:, k, j:j + 1], ALU.mult, ALU.add)
                        dve.done(m, ("xn", k))
                        pe.wait(v, ("T", k), i)
                        pe.wait(v, ("L", k), i, -1)
                        dve.done(v.tensor_copy(xT[:, k, 1, :], pT[:, k, 1, :]), ("xT1", k))
                passes(v, NQ // 2, body)
                pe.wait(v, ("L", 1), NQ // 2 - 1)
                lg = pL[:, :].rearrange("p (t e) -> p t e", e=E)
                bc = lambda a: a[:, :].unsqueeze(2).to_broadcast([P, NT, E])
                v.tensor_reduce(mx[:, :], lg, AX.X, ALU.max).then_inc(s_sm, 1)
                v.wait_ge(s_sm, 1)
                v.tensor_tensor(dif[:, :, :], lg, bc(mx), ALU.subtract).then_inc(s_sm, 1)
                v.wait_ge(s_ex, 1)
                v.wait_ge(s_sm, 2)
                v.tensor_reduce(mx[:, :], ex[:, :, :], AX.X, ALU.add).then_inc(s_sm, 1)
                v.wait_ge(s_sm, 3)
                v.reciprocal(mx[:, :], mx[:, :]).then_inc(s_sm, 1)
                v.wait_ge(s_sm, 4)
                v.tensor_tensor(scores[:, :, :], ex[:, :, :], bc(mx), ALU.mult).then_inc(s_sm, 2)
                v.memset(self.best[:, :], 0.0).then_inc(s_rows, 1)
                v.wait_ge(s_turned, 1)
                v.tensor_copy(self.rows[:, :, :], pT[:, 0, 0, :].rearrange("p (g k) -> p g k", k=P)).then_inc(s_rows, 1)
                v.wait_ge(s_rows, 2)

            @blk.scalar
            def _(a):
                def body(i):
                    for k in range(2):
                        dve.wait(a, ("mv", k), i)
                        dve.wait(a, ("rstd", k), i, -1)
                        act.done(a.activation(std[:, k, :], mv[:, k, :, 1], ACT.Sqrt, bias=self.eps[:, :]), ("std", k))
                        pe.wait(a, ("T", k), i)
                        pe.wait(a, ("L", k), i, -1)
                        act.done(a.activation(xT[:, k, 0, :], pT[:, k, 0, :], ACT.Copy), ("xT0", k))
                passes(a, NQ // 2, body)
                a.wait_ge(s_sm, 2)
                a.activation(ex[:, :, :], dif[:, :, :], ACT.Exp).then_inc(s_ex, 1)

            @blk.tensor
            def _(t_):
                def body(i):
                    for k in range(2):
                        dve.wait(t_, ("xn", k), i)
                        dve.wait(t_, ("xT1", k), i, -1)
                        act.wait(t_, ("xT0", k), i, -1)
                        for j in range(4):
                            for c in range(DC):
                                m = t_.transpose(pT[:, k, c, j * P:(j + 1) * P], xn[:, k, j, c * P:(c + 1) * P],
                                                 self.ident[:, :])
                        pe.done(m, ("T", k))
                        dve.wait(t_, ("xT1", k), i)
                        act.wait(t_, ("xT0", k), i)
                        for j in range(4):
                            o = pL[:, self.bass.ds((2 * i + k) * 4 * E + j * E, E)]
                            for c in range(DC):
                                m = t_.matmul(o, xT[:, k, c, j * P:(j + 1) * P], self.gate[:, c, :],
                                              start=c == 0, stop=c == DC - 1)
                        pe.done(m, ("L", k))
                passes(t_, NQ // 2, body)
                t_.wait_ge(s_sm, 6)
                for g in range(NT // 8):
                    m = t_.transpose(pT[:, 0, 0, g * P:(g + 1) * P],
                                     scores[:, 8 * g:8 * g + 8, :].rearrange("p t e -> p (t e)"), self.ident[:, :])
                m.then_inc(s_turned, 1)

    def route(self):
        nc, ALU, ACT, AX, f32, bf16 = self.nc, self.ALU, self.ACT, self.AX, self.f32, self.bf16
        scores, idx = self.scores, self.idx
        TE = TPB * E
        G, Q = P // WQ, CAP // WQ
        NG = E // G
        FAR = 4096.0
        ROUND = float(3 << 22)
        with self.scope() as t, nc.Block() as blk:
            diag = t.sb("diag", [E, B, E])
            thr = t.sb("thr", [P, B, E])
            gt, eq, sel = (t.sb(n, [P, B, TPB, E], bf16) for n in ("gt", "eq", "sel"))
            need = t.sb("need", [P, B, E])
            fits = t.sb("fits", [P, B, TPB, E])
            rank, quot = t.sb("rank", [P, B * TE]), t.sb("quot", [P, B * TE])
            hi, lo = t.sb("hi", [P, B * TE], bf16), t.sb("lo", [P, B * TE], bf16)
            hot_hi, hot_lo = (t.sb(n, [P, B, TE, WQ], bf16) for n in ("hot_hi", "hot_lo"))
            tok = t.sb("tok", [P, B, 2, TE * WQ], bf16)
            own, mine = t.sb("own", [P, B, NG, G, WQ]), t.sb("mine", [P, B, NG, G, WQ])
            found = t.sb("found", [P, B, E, 2])
            p_thr = t.ps("p_thr", [P, 512])
            p_rank = t.ps("p_rank", [P, B, TPB, E])
            p_tok = t.ps("p_tok", [P, B, NG, 2, G * WQ])
            p_own = t.ps("p_own", [P, B * NG * G * WQ])
            s_pe, s_v = t.sem("pe"), t.sem("dve")
            s_hot, s_tok = t.sem("hot"), t.sem("tok")
            marks = {}
            flat = lambda a: a[:, :, :, :].rearrange("p b t e -> p (b t e)")

            @blk.vector
            def _(v):
                n = [0]

                def link(m):
                    n[0] += 1
                    m.then_inc(s_v, 1)
                    v.wait_ge(s_v, n[0])

                for b in range(B):
                    m = v.tensor_scalar(diag[:, b, :], self.ident[0:E, 0:E], self.best[0:E, b:b + 1], None, ALU.mult)
                link(m)
                marks["diag"] = n[0]
                v.wait_ge(s_pe, 1)
                link(v.tensor_copy(thr[:, :, :], p_thr[:, 0:B * E].rearrange("p (b e) -> p b e", e=E)))
                sc = scores[:, :, :].rearrange("p (b t) e -> p b t e", b=B)
                for b in range(B):
                    tb = thr[:, b, :].unsqueeze(1).to_broadcast([P, TPB, E])
                    v.tensor_tensor(gt[:, b, :, :], sc[:, b, :, :], tb, ALU.is_gt)
                    m = v.tensor_tensor(eq[:, b, :, :], sc[:, b, :, :], tb, ALU.is_equal)
                link(m)
                marks["masks"] = n[0]
                v.wait_ge(s_pe, 2)
                link(v.tensor_scalar(need[:, :, :], p_thr[:, 0:B * E].rearrange("p (b e) -> p b e", e=E),
                                     -1.0, float(CAP), ALU.mult, ALU.add))
                for b in range(B):
                    nb = need[:, b, :].unsqueeze(1).to_broadcast([P, TPB, E])
                    m = v.tensor_tensor(fits[:, b, :, :], p_rank[:, b, :, :], nb, ALU.is_le)
                link(m)
                link(v.tensor_tensor(flat(fits), flat(fits), flat(eq), ALU.mult))
                link(v.tensor_tensor(flat(sel), flat(fits), flat(gt), ALU.add))
                marks["sel"] = n[0]
                v.wait_ge(s_pe, 3)
                link(v.scalar_tensor_tensor(rank[:, :], flat(sel), -FAR, flat(p_rank), ALU.mult, ALU.add))
                link(v.tensor_scalar(rank[:, :], rank[:, :], FAR - 1.0, None, ALU.add))
                link(v.tensor_scalar(quot[:, :], rank[:, :], 1.0 / WQ, 0.5 / WQ - 0.5, ALU.mult, ALU.add))
                link(v.tensor_scalar(quot[:, :], quot[:, :], ROUND, None, ALU.add))
                link(v.tensor_scalar(quot[:, :], quot[:, :], ROUND, None, ALU.subtract))
                v.tensor_copy(hi[:, :], quot[:, :])
                link(v.scalar_tensor_tensor(lo[:, :], quot[:, :], -float(WQ), rank[:, :], ALU.mult, ALU.add))
                for b in range(B):
                    for hot, part in ((hot_lo, lo), (hot_hi, hi)):
                        v.tensor_tensor(hot[:, b, :, :], part[:, b * TE:(b + 1) * TE].unsqueeze(2).to_broadcast([P, TE, WQ]),
                                        self.iota[:, :].unsqueeze(1).to_broadcast([P, TE, WQ]), ALU.is_equal
                                        ).then_inc(s_hot, 1)
                v.wait_ge(s_pe, 4)
                link(v.tensor_copy(own[:, :, :, :, :].rearrange("p b n g w -> p (b n) (g w)"),
                                   p_tok[:, :, :, 0, :].rearrange("p b n w -> p (b n) w")))
                link(v.scalar_tensor_tensor(own[:, :, :, :, :].rearrange("p b n g w -> p (b n) (g w)"),
                                            p_tok[:, :, :, 1, :].rearrange("p b n w -> p (b n) w"), float(P),
                                            own[:, :, :, :, :].rearrange("p b n g w -> p (b n) (g w)"), ALU.mult, ALU.add))
                link(v.tensor_tensor(own[:, :, :, :, :].rearrange("p b n g w -> p (b n) g w"),
                                     own[:, :, :, :, :].rearrange("p b n g w -> p (b n) g w"),
                                     self.own_expert.unsqueeze(1).unsqueeze(3).to_broadcast([P, B * NG, G, WQ]), ALU.mult))
                marks["own"] = n[0]
                v.wait_ge(s_pe, 5)
                cols = mine[:, :, :, :, :].rearrange("p b n g (h w) -> p (b n g h) w", w=8)
                link(v.tensor_tensor(cols, p_own[:, :].rearrange("p (c w) -> p c w", w=8),
                                     self.own_column.unsqueeze(1).to_broadcast([P, B * E * 2, 8]), ALU.mult))
                link(v.tensor_reduce(found[:, :, :, :].rearrange("p b e h -> p (b e h)"), cols, AX.X, ALU.add))
                for b in range(B):
                    m = v.tensor_scalar(idx[:, :, b, :], found[:, b, :, :], float(b * S), None, ALU.add)
                link(m)

            @blk.scalar
            def _(a):
                for b in range(B):
                    a.wait_ge(s_hot, 2 * b + 1)
                    low = hot_lo[:, b, :, :].rearrange("p c w -> p (c w)")
                    a.activation(tok[:, b, 0, :], low, ACT.Copy, scale=self.place)
                    for tt in range(TPB):
                        cols = slice(tt * E * WQ, (tt + 1) * E * WQ)
                        m = a.activation(tok[:, b, 1, cols], low[:, cols], ACT.Copy, scale=float(tt))
                    m.then_inc(s_tok, 1)

            @blk.tensor
            def _(t_):
                t_.wait_ge(s_v, marks["diag"])
                t_.matmul(p_thr[:, 0:B * E], self.ones32[:, :], diag[:, :, :].rearrange("p b e -> p (b e)"),
                          start=True, stop=True).then_inc(s_pe, 1)
                t_.wait_ge(s_v, marks["masks"])

                def ranks(mask):
                    m = t_.matmul(flat(p_rank), self.tri[:, :], flat(mask), start=True, stop=False)
                    for tt in range(TPB - 1):
                        later = TPB - 1 - tt
                        m = t_.matmul(p_rank[:, :, tt + 1:, :], self.ones[:, :],
                                      mask[:, :, tt, :].unsqueeze(2).to_broadcast([P, B, later, E]),
                                      start=False, stop=tt == TPB - 2)
                    return m
                ranks(eq)
                o = p_thr[:, 0:B * E].rearrange("p (b e) -> p b e", e=E)
                for tt in range(TPB):
                    m = t_.matmul(o, self.ones[:, :], gt[:, :, tt, :], start=tt == 0, stop=tt == TPB - 1)
                m.then_inc(s_pe, 1)
                t_.wait_ge(s_v, marks["sel"])
                ranks(sel).then_inc(s_pe, 1)
                for b in range(B):
                    t_.wait_ge(s_hot, 2 * b + 2)
                    t_.wait_ge(s_tok, b + 1)
                    for g in range(NG):
                        for tt in range(TPB):
                            c0 = tt * E + g * G
                            m = t_.matmul(p_tok[:, b, g, :, :], hot_hi[:, b, c0:c0 + G, :].rearrange("p c w -> p (c w)"),
                                          tok[:, b, :, c0 * WQ:(c0 + G) * WQ], start=tt == 0, stop=tt == TPB - 1)
                m.then_inc(s_pe, 1)
                t_.wait_ge(s_v, marks["own"])
                t_.matmul(p_own[:, :], self.spread, own[:, :, :, :, :].rearrange("p b n g w -> p (b n g w)"),
                          start=True, stop=True).then_inc(s_pe, 1)

    def experts(self, x, out, shared):
        nc, ALU, ACT, bass = self.nc, self.ALU, self.ACT, self.bass
        J = NQ if shared else E
        W = 4 * P
        with self.scope() as t, nc.Block() as blk:
            raw_g, raw_u = t.sb("raw_g", [P, DC, F]), t.sb("raw_u", [P, DC, F])
            raw_d = t.sb("raw_d", [P, FC, D])
            nw = 1 if shared else 2
            wg = [t.sb(f"wg{h}", [P, nw, DC, F], self.f32r) for h in range(2)]
            wu = [t.sb(f"wu{h}", [P, nw, DC, F], self.f32r) for h in range(2)]
            wd = [t.sb(f"wd{h}", [P, nw, FC, D], self.f32r) for h in range(2)]
            xr = t.sb("xr", [P, 2, 4, ROW])
            xT = [t.sb(f"xT{h}", [P, 2, DC, W], self.f32r) for h in range(2)]
            gl = t.sb("gl", [P, 2, W])
            hf = t.sb("hf", [P, 2, W])
            hT = [t.sb(f"hT{h}", [P, 2, FC, W], self.f32r) for h in range(2)]
            eo = t.sb("eo", [P, 2, 4, D])
            xres = t.sb("xres", [P, 2, 4, D]) if shared else None
            wt = t.sb("wt", [P, 2, 4])
            gidx = t.sb("gidx", [P, 2, 4], self.i32)
            sidx = t.sb("sidx", [P, 2, 4], self.i32)
            pG, pU = t.ps("pG", [P, 2, W]), t.ps("pU", [P, 2, W])
            pD = t.ps("pD", [P, 2, 2, D])
            pX = t.ps("pX", [P, W])
            p_cnt = t.ps("p_cnt", [P, 512]) if shared else None

            per = lambda *names: [(n, k) for k in range(2) for n in names]
            pe = t.steps("pe", per("G0", "U0", "G1", "U1", "T0", "D0", "D1", "T1", "G2", "U2", "G3", "U3"))
            a_own = () if shared else ("wgh", "wuh")
            act = t.steps("act", per("gelu0", "hh0", "gelu1", "hh1", "xh0", "xh1", *a_own, "gelu2", "hh2", "gelu3", "hh3",
                                     *(() if shared else ("wdh",))))
            dve = t.steps("dve", per("mul0", "mul1", "hl0", "hl1", "xl0", "ev0", "ev1", "xl1", "wt",
                                     *(() if shared else ("wgl",)), "mul2", "mul3", "hl2", "hl3"))
            pool = t.steps("pool", per(*(() if shared else ("wul", "si", "wdl"))) or ["none"])
            index = t.steps("index", per("gi"))
            s_rows = [t.sem(f"rows{k}") for k in range(2)]
            s_res = [t.sem(f"res{k}") for k in range(2)] if shared else None
            s_raw = [t.sem(n) for n in ("raw_g", "raw_u", "raw_d")]
            s_out = [t.sem(f"out{k}") for k in range(2)]
            s_wh, s_wl = (t.sem("wh"), t.sem("wl")) if shared else (None, None)
            if shared:
                assert 4 * J == NBITS
                GB = NT // 8 // B
                cand, keep = t.sb("cand", [P, B]), t.sb("keep", [P, B])
                ge = t.sb("ge", [P, S // 8], self.bf16)
                cnt = t.sb("cnt", [P, B], self.bf16)
                bit = t.steps("bit", ["cand", "cnt0", "cnt1", "keep", "best"])
                tot = t.steps("tot", ["tot"])
            rows_inc = 16 if shared else 64
            out_inc = 16 if shared else 64
            ob = lambda k: 0 if shared else k

            tv = self.table[:, 0:D].rearrange("(q t p) d -> q p t d", t=4, p=P)
            xv = x.rearrange("(q t p) d -> q p t d", t=4, p=P)
            ov = out.rearrange("(q t p) d -> q p t d", t=4, p=P)
            src = [self.ins[n] for n in (("WsgT", "WsuT", "WsdT") if shared else ("WgT", "WuT", "WdT"))]

            def other(k, d):
                return (k + d) % 2, (k + d) // 2

            class Pass:
                def __init__(p, i, k):
                    p.i, p.k, p.n = i, k, 1 - k
                    s = 2 * i + k if isinstance(i, int) else None
                    p.rows = s is None or s < J
                    p.up = s is None or 1 <= s <= J
                    p.down = s is None or s >= 2

            def stream(eng, body, tail=1):
                def both(i):
                    for k in range(2):
                        body(Pass(i, k))
                passes(eng, J // 2 + 1, both, tail)

            def split_weights(eng_op, eng, which, slot):
                raw = (raw_g, raw_u, raw_d)[which]
                hi, lo = (wg, wu, wd)[which]
                if eng_op == "hi":
                    return eng.activation(hi[:, slot, :, :], raw[:, :, :], ACT.Copy)
                return eng.tensor_tensor(lo[:, slot, :, :], raw[:, :, :], hi[:, slot, :, :].bitcast(self.f32), ALU.subtract)

            @blk.sync
            def _(sp):
                if shared:
                    for w, (dst, ch) in enumerate(((raw_g, P), (raw_u, P), (raw_d, P))):
                        sp.dma_start(dst[:, :, :], src[w].rearrange("(c p) f -> p c f", p=P)).then_inc(s_raw[w], 16)

                def body(p):
                    i, k = p.i, p.k
                    k1, d1 = other(k, 1)
                    if shared:
                        if p.rows:
                            pe.wait(sp, ("T1", k), i, -1)
                            sp.dma_start(xr[:, k, :, 0:D], tv[2 * i + k]).then_inc(s_rows[k], 16)
                        if p.down:
                            dve.wait(sp, ("ev1", k), i, -1)
                            sp.dma_start(xres[:, k, :, :], xv[2 * (i - 1) + k]).then_inc(s_res[k], 16)
                    elif p.rows:
                        for w, (dst, by, st) in enumerate(((raw_g, dve, "wgl"), (raw_u, pool, "wul"), (raw_d, pool, "wdl"))):
                            kb, db = other(k, -1)
                            by.wait(sp, (st, kb), i, db)
                            wsrc = src[w].rearrange("e (c p) f -> e p c f", p=P)
                            sp.dma_start(dst[:, :, :], wsrc[2 * i + k]).then_inc(s_raw[w], 16)
                stream(sp, body)

            @blk.tensor
            def _(t_):
                def gu(p, f):
                    i, k, n = p.i, p.k, p.n
                    b = f % 2
                    kb, db = (k, 0) if f >= 2 else other(k, -1)
                    fb = (f + 2) % 4
                    for name, ps, w, user, eng_u in (("G", pG, wg, "mul", dve), ("U", pU, wu, "mul", dve)):
                        if name == "G":
                            act.wait(t_, (f"gelu{fb}", kb), i, db)
                        dve.wait(t_, (f"mul{fb}", kb), i, db)
                        for c in range(DC):
                            m = self.product3(t_, ps[:, b, :], w[0][:, ob(n), c, f * P:(f + 1) * P],
                                              w[1][:, ob(n), c, f * P:(f + 1) * P],
                                              xT[0][:, n, c, :], xT[1][:, n, c, :], c == 0, c == DC - 1)
                        pe.done(m, (f"{name}{f}", k))

                def turn(p, c):
                    i, k = p.i, p.k
                    if not p.rows:
                        return pe.skip(t_, i, [(f"T{c}", k)])
                    if c == 0:
                        t_.wait_ge(s_rows[k], rows_inc * (i + 1))
                    cb, kc, dc = (0, k, 0) if c else (1, *other(k, -1))
                    dve.wait(t_, (f"xl{cb}", kc), i, dc)
                    for q in range(4):
                        m = t_.transpose(pX[:, q * P:(q + 1) * P], xr[:, k, q, c * P:(c + 1) * P], self.ident[:, :])
                    pe.done(m, (f"T{c}", k))

                def total(p, m):
                    if shared and p.rows:
                        n = 8 * p.i + (4 * p.k + m)
                        bit.wait(t_, "cnt1", n)
                        tot.done(t_.matmul(p_cnt[:, 0:B], self.same_expert[:, :], cnt[:, :], start=True, stop=True), "tot")

                def body(p):
                    i, k, n = p.i, p.k, p.n
                    kb, db = other(k, -1)
                    if p.up:
                        dve.wait(t_, ("xl1" if shared else "wgl", kb), i, db)
                        if not shared:
                            pool.wait(t_, ("wul", kb), i, db)
                        else:
                            t_.wait_ge(s_wl, 3)
                        gu(p, 0)
                        gu(p, 1)
                    else:
                        pe.skip(t_, i, [(x_, k) for x_ in ("G0", "U0", "G1", "U1")])
                    total(p, 0)
                    turn(p, 0)
                    if p.down:
                        dve.wait(t_, ("hl3", kb), i, db)
                        if not shared:
                            pool.wait(t_, ("wdl", k), i, -1)
                        for h in range(2):
                            dve.wait(t_, (f"ev{h}", kb), i, db)
                            for r in range(2):
                                for c in range(FC):
                                    q = 2 * h + r
                                    m = self.product3(t_, pD[:, h, r, :], hT[0][:, k, c, q * P:(q + 1) * P],
                                                      hT[1][:, k, c, q * P:(q + 1) * P], wd[0][:, ob(k), c, :],
                                                      wd[1][:, ob(k), c, :], c == 0, c == FC - 1)
                            pe.done(m, (f"D{h}", k))
                    else:
                        pe.skip(t_, i, [("D0", k), ("D1", k)])
                    total(p, 1)
                    turn(p, 1)
                    total(p, 2)
                    if p.up:
                        gu(p, 2)
                        total(p, 3)
                        gu(p, 3)
                    else:
                        total(p, 3)
                        pe.skip(t_, i, [(x_, k) for x_ in ("G2", "U2", "G3", "U3")])
                stream(t_, body)

            @blk.scalar
            def _(a):
                if shared:
                    for w in range(3):
                        a.wait_ge(s_raw[w], 16)
                        split_weights("hi", a, w, 0).then_inc(s_wh, 1)

                def hidden(p, f):
                    i, k, n = p.i, p.k, p.n
                    if not p.up:
                        act.skip(a, i, [(f"gelu{f}", k), (f"hh{f}", k)])
                        return
                    kb, db = (k, 0) if f >= 2 else other(k, -1)
                    pe.wait(a, (f"G{f}", k), i)
                    dve.wait(a, (f"mul{(f + 2) % 4}", kb), i, db)
                    act.done(a.activation(gl[:, f % 2, :], pG[:, f % 2, :], ACT.Gelu), (f"gelu{f}", k))
                    dve.wait(a, (f"mul{f}", k), i)
                    if f == 0:
                        kc, dc = other(k, -1)
                        pe.wait(a, ("D1", kc), i, dc)
                    act.done(a.activation(hT[0][:, n, f, :], hf[:, f % 2, :], ACT.Copy), (f"hh{f}", k))

                def body(p):
                    i, k = p.i, p.k
                    hidden(p, 0)
                    hidden(p, 1)
                    if p.rows:
                        kb, db = other(k, -1)
                        pe.wait(a, ("U3", kb), i, db)
                        for c in range(DC):
                            pe.wait(a, (f"T{c}", k), i)
                            act.done(a.activation(xT[0][:, k, c, :], pX[:, :], ACT.Copy), (f"xh{c}", k))
                        if not shared:
                            for w, nm in enumerate(("wgh", "wuh")):
                                a.wait_ge(s_raw[w], 16 * (2 * i + k + 1))
                                act.done(split_weights("hi", a, w, k), (nm, k))
                    else:
                        act.skip(a, i, [(x_, k) for x_ in ("xh0", "xh1", *a_own)])
                    hidden(p, 2)
                    hidden(p, 3)
                    if not shared:
                        if p.rows:
                            a.wait_ge(s_raw[2], 16 * (2 * i + k + 1))
                            pe.wait(a, ("D1", k), i)
                            act.done(split_weights("hi", a, 2, k), ("wdh", k))
                        else:
                            act.skip(a, i, [("wdh", k)])
                stream(a, body)

            @blk.vector
            def _(v):
                if shared:
                    for w in range(3):
                        v.wait_ge(s_wh, w + 1)
                        split_weights("lo", v, w, 0).then_inc(s_wl, 1)

                def mul(p, f):
                    i, k = p.i, p.k
                    act.wait(v, (f"gelu{f}", k), i)
                    pe.wait(v, (f"U{f}", k), i)
                    kb, db = (k, 0) if f >= 2 else other(k, -1)
                    act.wait(v, (f"hh{(f + 2) % 4}", kb), i, db)
                    dve.wait(v, (f"hl{(f + 2) % 4}", kb), i, db)
                    dve.done(v.tensor_tensor(hf[:, f % 2, :], gl[:, f % 2, :], pU[:, f % 2, :], ALU.mult), (f"mul{f}", k))

                def low(p, f):
                    i, k, n = p.i, p.k, p.n
                    act.wait(v, (f"hh{f}", k), i)
                    dve.done(v.tensor_tensor(hT[1][:, n, f, :], hf[:, f % 2, :], hT[0][:, n, f, :].bitcast(self.f32),
                                             ALU.subtract), (f"hl{f}", k))

                def xlow(p, c):
                    i, k = p.i, p.k
                    if not p.rows:
                        return dve.skip(v, i, [(f"xl{c}", k)])
                    act.wait(v, (f"xh{c}", k), i)
                    dve.done(v.tensor_tensor(xT[1][:, k, c, :], pX[:, :], xT[0][:, k, c, :].bitcast(self.f32),
                                             ALU.subtract), (f"xl{c}", k))

                def evacuate(p, h):
                    i, k = p.i, p.k
                    if not p.down:
                        return dve.skip(v, i, [(f"ev{h}", k)])
                    if h == 0:
                        if not isinstance(i, int) or 2 * i + k >= 4:
                            v.wait_ge(s_out[k], out_inc * (i - 1))
                        if shared:
                            v.wait_ge(s_res[k], 16 * i)
                    pe.wait(v, (f"D{h}", k), i)
                    for r in range(2):
                        q = 2 * h + r
                        if shared:
                            m = v.scalar_tensor_tensor(eo[:, k, q, :], pD[:, h, r, :], 0.5, xres[:, k, q, :],
                                                       ALU.mult, ALU.add)
                        else:
                            m = v.tensor_scalar(eo[:, k, q, :], pD[:, h, r, :], wt[:, k, q:q + 1], 0.5,
                                                ALU.mult, ALU.mult)
                    dve.done(m, (f"ev{h}", k))

                def decide(n):
                    tot.wait(v, "tot", n)
                    bit.done(v.scalar_tensor_tensor(keep[:, :], p_cnt[:, 0:B], float(CAP), cand[:, :],
                                                    ALU.is_ge, ALU.mult), "keep")
                    bit.wait(v, "keep", n)
                    bit.done(v.tensor_tensor(self.best[:, :], self.best[:, :], keep[:, :], ALU.max), "best")

                def search(p, m):
                    if not (shared and p.rows):
                        return
                    n = 8 * p.i + (4 * p.k + m)
                    if not (isinstance(n, int) and n == 0):
                        decide(n - 1)
                        bit.wait(v, "best", n, -1)
                    one = self.bits[:, bass.ds(n, 1)].to_broadcast([P, B])
                    bit.done(v.tensor_tensor(cand[:, :].bitcast(self.i32), self.best[:, :].bitcast(self.i32), one,
                                             ALU.bitwise_or), "cand")
                    bit.wait(v, "cand", n)
                    for b in range(B):
                        if b:
                            bit.wait(v, "cnt0", n)
                        c_ = v.tensor_scalar(ge[:, :], self.rows[:, b * GB:(b + 1) * GB, :].rearrange("p g k -> p (g k)"),
                                             cand[:, b:b + 1], None, ALU.is_ge, ALU.add, accum_out=cnt[:, b:b + 1])
                        bit.done(c_, f"cnt{b}")

                def body(p):
                    i, k = p.i, p.k
                    search(p, 0)
                    if p.up:
                        mul(p, 0)
                        mul(p, 1)
                        low(p, 0)
                        low(p, 1)
                    else:
                        dve.skip(v, i, [(x_, k) for x_ in ("mul0", "mul1", "hl0", "hl1")])
                    xlow(p, 0)
                    search(p, 1)
                    evacuate(p, 0)
                    search(p, 2)
                    evacuate(p, 1)
                    xlow(p, 1)
                    search(p, 3)
                    if p.rows and not shared:
                        dve.wait(v, ("ev1", k), i)
                        col = xr[:, k, :, :].rearrange("p q w -> p w q")[:, bass.ds(2 * i + (D + k), 1), :]
                        dve.done(v.tensor_copy(wt[:, k, :].unsqueeze(1), col), ("wt", k))
                    else:
                        dve.skip(v, i, [("wt", k)])
                    if p.rows and not shared:
                        act.wait(v, ("wgh", k), i)
                        dve.done(split_weights("lo", v, 0, k), ("wgl", k))
                    elif not shared:
                        dve.skip(v, i, [("wgl", k)])
                    if p.up:
                        mul(p, 2)
                        mul(p, 3)
                        low(p, 2)
                        low(p, 3)
                    else:
                        dve.skip(v, i, [(x_, k) for x_ in ("mul2", "mul3", "hl2", "hl3")])
                stream(v, body)
                if shared:
                    decide(4 * J - 1)
                    bit.wait(v, "best", 4 * J - 1)

            @blk.gpsimd
            def _(g):
                idx = self.idx

                def take_rows(i, k):
                    flat = idx[:, :, :, :].rearrange("p e b h -> p (e b h)")
                    m = g.tensor_copy(gidx[:, k, :], flat[:, bass.ds((2 * i + k) * 4, 4)])
                    return m

                def gather(k):
                    for q in range(4):
                        g.indirect_dma_start(xr[:, k, q, :], None, self.table[:, :],
                                             bass.IndirectOffsetOnAxis(gidx[:, k, q:q + 1], 0)).then_inc(s_rows[k], 16)

                if shared:
                    def body(p):
                        i, k = p.i, p.k
                        if p.down:
                            dve.wait(g, ("ev1", k), i)
                            g.dma_start(ov[2 * (i - 1) + k], eo[:, k, :, :]).then_inc(s_out[k], 16)
                    stream(g, body)
                    for k in range(2):
                        g.wait_ge(s_out[k], 16 * (J // 2))
                    return

                def fetch(i, k):
                    if not (isinstance(i, int) and i == 0):
                        g.wait_ge(s_rows[k], 64 * i)
                    index.done(take_rows(i, k), ("gi", k))
                    pe.wait(g, ("T1", k), i, -1)
                    dve.wait(g, ("wt", k), i, -1)
                    index.wait(g, ("gi", k), i)
                    self.settle(g)
                    gather(k)

                def body(p):
                    i, k = p.i, p.k
                    ki, di = other(k, 1)
                    if not isinstance(i, int) or 2 * i + k + 1 < J:
                        fetch(i + di, ki)
                    if p.rows:
                        act.wait(g, ("wuh", k), i)
                        pool.done(split_weights("lo", g, 1, k), ("wul", k))
                    else:
                        pool.skip(g, i, [("wul", k)])
                    if p.down:
                        if not isinstance(i, int) or 2 * i + k >= 3:
                            g.wait_ge(s_out[1 - k], 64 * (i - 1 + k))
                        flat = idx[:, :, :, :].rearrange("p e b h -> p (e b h)")
                        if not isinstance(i, int) or 2 * i + k >= 4:
                            g.wait_ge(s_out[k], 64 * (i - 1))
                        m = g.tensor_copy(sidx[:, k, :], flat[:, bass.ds((2 * i + k - 2) * 4, 4)])
                        pool.done(m, ("si", k))
                        pool.wait(g, ("si", k), i)
                        dve.wait(g, ("ev1", k), i)
                        self.settle(g)
                        for q in range(4):
                            g.indirect_dma_start(out, bass.IndirectOffsetOnAxis(sidx[:, k, q:q + 1], 0),
                                                 eo[:, k, q, :], None, compute_op=ALU.add).then_inc(s_out[k], 16)
                    else:
                        pool.skip(g, i, [("si", k)])
                    if p.rows:
                        act.wait(g, ("wdh", k), i)
                        pool.done(split_weights("lo", g, 2, k), ("wdl", k))
                    else:
                        pool.skip(g, i, [("wdl", k)])
                fetch(0, 0)
                stream(g, body, 2)
                for k in range(2):
                    g.wait_ge(s_out[k], 64 * (J // 2))

    def ffn(self, x, out):
        with self.scope() as st:
            self.scores = st.sb("scores", [P, NT, E])
            self.idx = st.sb("idx", [P, E, B, CAP // P], self.i32)
            self.rows = st.sb("rows", [P, NT // 8, P])
            self.best = st.sb("best", [P, B])
            self.ln_router(x)
            self.experts(x, out, True)
            self.route()
            self.experts(x, out, False)


    def projections(self, x):
        nc, ALU, ACT, bass, AX = self.nc, self.ALU, self.ACT, self.bass, self.AX
        HF = HD // 2
        LO = 32
        with self.scope() as t, nc.Block() as blk:
            raw = t.sb("raw", [P, DC, 3 * D])
            w = [t.sb(f"w{h}", [P, DC, 3 * D], self.f32r) for h in range(2)]
            bias_raw, bias_hi = t.sb("bias_raw", [LO + 1, 3 * D]), t.sb("bias_hi", [LO + 1, 3 * D], self.f32r)
            bias = t.sb("bias", [LO + 1, 3 * D], self.f32r)
            ones = t.sb("ones", [LO + 1, P], self.f32r)
            head_of = t.sb("head_of", [P, 32], self.bf16)
            rope = t.sb("rope", [P, NT, 2, HD])
            xq = t.sb("xq", [P, 2, 4, D])
            xn = t.sb("xn", [P, 2, 4, D])
            st6, mv = t.sb("st6", [P, 4, 6]), t.sb("mv", [P, 4, 2])
            std, rstd, shift = t.sb("std", [P, 4]), t.sb("rstd", [P, 4]), t.sb("shift", [P, 4])
            xT = [t.sb(f"xT{h}", [P, 2, DC, 4 * P], self.f32r) for h in range(2)]
            turned = t.sb("turned", [P, 2, 2 * D])
            scaled = t.sb("scaled", [P, 2, 2 * D])
            roped = t.sb("roped", [P, 2, 2 * D])
            half = [t.sb(f"half{h}", [P, 2, 4, 4 * P], self.f32r) for h in range(2)]
            squares = t.sb("squares", [P, 4, 4 * P], self.bf16)
            vt = t.sb("vt", [P, 2, 4, H, VW])
            norm, top = t.sb("norm", [P, 1]), t.sb("top", [P, 1])
            best, prod = t.sb("best", [1, 2]), t.sb("prod", [1, 1])
            zero = t.sb("zero", [B * H, 2 * S])
            pX = t.ps("pX", [P, DC, 4 * P])
            pQ = t.ps("pQ", [P, 2, 2 * D])
            pV = t.ps("pV", [P, 512])
            pR = t.ps("pR", [P, 2, 4, P])
            pN = t.ps("pN", [P, 4 * P])

            per = lambda *names: [(n, k) for k in range(2) for n in names]
            pe = t.steps("pe", per("A0", "V0", "N", "A1", "V1", "R0", "A2", "V2", "R1", "A3", "V3", "R2", "T0", "T1", "R3"))
            act = t.steps("act", per("v0", "v1", "rh0", "std", "v2", "rh1", "v3", "rh2", "xh0", "xh1", "rh3", "sq"))
            dve = t.steps("dve", per("cs0", "sn0", "cs1", "sn1", "rl0", "norm", "top",
                                     "stats", "mv", "rstd", "shift", "xn",
                                     "cs2", "sn2", "rl1", "cs3", "sn3", "rl2", "xl0", "xl1", "rl3"))
            pool = t.steps("pool", per(*(f"ad{j}" for j in range(4))))
            s_w, s_wh, s_wl, s_c, s_b = (t.sem(n) for n in ("w", "wh", "wl", "const", "bias"))
            s_x = [t.sem(f"x{k}") for k in range(2)]
            s_out = [t.sem(f"out{k}") for k in range(2)]
            s_zero, s_one, s_flag, s_tt = t.sem("zero"), t.sem("one"), t.sem("flag"), t.sem("top_t")
            J = NQ
            NOUT = 16 * 7
            xv = x.rearrange("(q t p) d -> q p t d", t=4, p=P)

            def stream(eng, body):
                def both(i):
                    for k in range(2):
                        s_ = 2 * i + k if isinstance(i, int) else None
                        body(i, k, s_ is None or s_ < J, s_ is None or 1 <= s_ <= J, s_ is None or s_ >= 2)
                passes(eng, J // 2 + 1, both)

            def back(k, d=1):
                return (k - d) % 2, (k - d) // 2

            def two_before(k, j):
                return (j - 2, k, 0) if j >= 2 else (j + 2, *back(k))

            @blk.sync
            def _(sp):
                sp.dma_start(raw[:, :, 0:2 * D], self.ins["WqkT"].rearrange("(c p) f -> p c f", p=P)).then_inc(s_w, 16)
                sp.dma_start(raw[:, :, 2 * D:], self.ins["WvT"].rearrange("(c p) f -> p c f", p=P)).then_inc(s_w, 16)
                for row in (0, LO):
                    sp.dma_start(bias_raw[row:row + 1, :], self.ins["b_qkvo"][0:1, 0:3 * D]).then_inc(s_b, 16)
                sp.dma_start(rope[:, :, :, :], self.ins["c_rope"]).then_inc(s_c, 16)
                sp.wait_ge(s_one, 3)
                sp.dma_start(self.shift.rearrange("h c s -> h (c s)"), zero[:, :]).then_inc(s_zero, 16)

                def body(i, k, rows, up, norms):
                    kb, db = back(k)
                    if rows:
                        dve.wait(sp, ("xn", k), i, -1)
                        sp.dma_start(xq[:, k, :, :], xv[2 * i + k]).then_inc(s_x[k], 16)
                    if up:
                        q = 2 * (i + db) + kb
                        dve.wait(sp, ("rl3", k), i)
                        bb, cc = q // (NQ // B), q % (NQ // B)
                        for a_ in range(2):
                            for r, part in enumerate(TRIPLE[a_]):
                                dst = self.qk[a_].rearrange("(b c p r) s -> b r p c s", b=B, p=P, r=3)[bb][r]
                                sp.dma_start(dst[:, :, bass.ds(cc * 4 * P, 4 * P)],
                                             half[part][:, kb, 2 * a_:2 * a_ + 2, :].bitcast(self.f32)).then_inc(s_out[kb], 16)
                        sp.dma_start(self.vals.rearrange("(q t p) w -> q p t w", t=4, p=P)[q],
                                     vt[:, kb, :, :, :].rearrange("p t h w -> p t (h w)")).then_inc(s_out[kb], 16)
                stream(sp, body)
                for k in range(2):
                    sp.wait_ge(s_out[k], NOUT * (J // 2))
                sp.wait_ge(s_zero, 16)

            @blk.tensor
            def _(t_):
                def product(o, kb, j, lo, hi):
                    t_.matmul(o, ones[:, :], bias[:, lo:hi], start=True, stop=False)
                    for c in range(DC):
                        x_hi, x_lo = (xT[h][:, kb, c, j * P:(j + 1) * P] for h in range(2))
                        t_.matmul(o, x_hi, w[0][:, c, lo:hi], start=False, stop=False)
                        t_.matmul(o, x_hi, w[1][:, c, lo:hi], start=False, stop=False)
                        m = t_.matmul(o, x_lo, w[0][:, c, lo:hi], start=False, stop=c == DC - 1)
                    return m

                def tile(i, k, j):
                    kb, db = back(k)
                    jb, kj, dj = two_before(k, j)
                    dve.wait(t_, (f"sn{jb}", kj), i, dj)
                    pe.done(product(pQ[:, j % 2, :], kb, j, 0, 2 * D), (f"A{j}", k))
                    act.wait(t_, (f"v{j - 1}", k) if j else ("v3", kb), i, 0 if j else db)
                    pe.done(product(pV[:, 0:D], kb, j, 2 * D, 3 * D), (f"V{j}", k))

                def turn(i, k, j):
                    jb, kj, dj = two_before(k, j)
                    pool.wait(t_, (f"ad{j}", k), i)
                    dve.wait(t_, (f"rl{jb}", kj), i, dj)
                    for c in range(4):
                        m = t_.transpose(pR[:, j % 2, c, :], roped[:, j % 2, c * P:(c + 1) * P], self.ident[:, :])
                    pe.done(m, (f"R{j}", k))

                def body(i, k, rows, up, norms):
                    kb, db = back(k)
                    if up:
                        dve.wait(t_, ("xl1", kb), i, db)
                        t_.wait_ge(s_wl, 2)
                        tile(i, k, 0)
                    else:
                        pe.skip(t_, i, [("A0", k), ("V0", k)])
                    if norms:
                        act.wait(t_, ("sq", kb), i, db)
                        dve.wait(t_, ("norm", kb), i, db)
                        for c in range(4):
                            m = t_.matmul(pN[32 * c:32 * c + 32, :], head_of[:, :], squares[:, c, :], start=True, stop=True)
                        pe.done(m, ("N", k))
                    else:
                        pe.skip(t_, i, [("N", k)])
                    if up:
                        tile(i, k, 1)
                        turn(i, k, 0)
                        tile(i, k, 2)
                        turn(i, k, 1)
                        tile(i, k, 3)
                        turn(i, k, 2)
                    else:
                        pe.skip(t_, i, [(n_, k) for n_ in ("A1", "V1", "R0", "A2", "V2", "R1", "A3", "V3", "R2")])
                    if rows:
                        dve.wait(t_, ("xn", k), i)
                        for c in range(DC):
                            dve.wait(t_, (f"xl{c}", kb), i, db)
                            for j in range(4):
                                m = t_.transpose(pX[:, c, j * P:(j + 1) * P], xn[:, k, j, c * P:(c + 1) * P], self.ident[:, :])
                            pe.done(m, (f"T{c}", k))
                    else:
                        pe.skip(t_, i, [("T0", k), ("T1", k)])
                    if up:
                        turn(i, k, 3)
                    else:
                        pe.skip(t_, i, [("R3", k)])
                stream(t_, body)
                t_.wait_ge(s_flag, 1)
                t_.transpose(pN[0:1, 0:P], top[:, :], self.ident[:, :]).then_inc(s_tt, 1)

            @blk.scalar
            def _(a):
                a.wait_ge(s_w, 32)
                a.activation(w[0][:, :, :], raw[:, :, :], ACT.Copy).then_inc(s_wh, 1)
                a.wait_ge(s_b, 32)
                a.wait_ge(s_one, 8)
                for row in (0, LO):
                    m = a.activation(bias_hi[row:row + 1, :], bias_raw[row:row + 1, :], ACT.Copy)
                a.activation(bias[0:1, :], bias_raw[0:1, :], ACT.Copy).then_inc(s_wh, 1)

                def value(i, k, j, up):
                    if not up:
                        return act.skip(a, i, [(f"v{j}", k)])
                    kb, db = back(k)
                    pe.wait(a, (f"V{j}", k), i)
                    a.wait_ge(s_one, 4)
                    if j == 0 and not (isinstance(i, int) and 2 * i + k < 3):
                        a.wait_ge(s_out[kb], NOUT * (i + db))
                    act.done(a.activation(vt[:, kb, j, :, 0:HD], pV[:, 0:D].rearrange("p (h w) -> p h w", w=HD), ACT.Copy),
                             (f"v{j}", k))

                def high(i, k, j, up):
                    if not up:
                        return act.skip(a, i, [(f"rh{j}", k)])
                    kb, db = back(k)
                    pe.wait(a, (f"R{j}", k), i)
                    if j == 0 and not (isinstance(i, int) and 2 * i + k < 3):
                        a.wait_ge(s_out[kb], NOUT * (i + db))
                        act.wait(a, ("sq", k), i, -1)
                    act.done(a.activation(half[0][:, kb, :, j * P:(j + 1) * P], pR[:, j % 2, :, :], ACT.Copy), (f"rh{j}", k))

                def body(i, k, rows, up, norms):
                    kb, db = back(k)
                    value(i, k, 0, up)
                    value(i, k, 1, up)
                    high(i, k, 0, up)
                    if rows:
                        dve.wait(a, ("mv", k), i)
                        act.done(a.activation(std[:, :], mv[:, :, 1], ACT.Sqrt, bias=self.eps[:, :]), ("std", k))
                    else:
                        act.skip(a, i, [("std", k)])
                    value(i, k, 2, up)
                    high(i, k, 1, up)
                    value(i, k, 3, up)
                    high(i, k, 2, up)
                    if rows:
                        for c in range(DC):
                            pe.wait(a, (f"T{c}", k), i)
                            pe.wait(a, ("V3", kb), i, db)
                            act.done(a.activation(xT[0][:, k, c, :], pX[:, c, :], ACT.Copy), (f"xh{c}", k))
                    else:
                        act.skip(a, i, [("xh0", k), ("xh1", k)])
                    high(i, k, 3, up)
                    if up:
                        act.wait(a, ("rh3", k), i)
                        pe.wait(a, ("N", k), i)
                        act.done(a.activation(squares[:, :, :], half[0][:, kb, :, :].bitcast(self.f32), ACT.Square), ("sq", k))
                    else:
                        act.skip(a, i, [("sq", k)])
                stream(a, body)

            @blk.vector
            def _(v):
                v.memset(top[:, :], 0.0).then_inc(s_one, 1)
                v.memset(zero[:, :], 0.0).then_inc(s_one, 1)
                v.memset(vt[:, :, :, :, :], 0.0).then_inc(s_one, 1)
                v.wait_ge(s_one, 3)
                v.memset(vt[:, :, :, :, HD:HD + 1], 1.0).then_inc(s_one, 1)
                v.memset(bias[:, :].bitcast(self.f32), 0.0).then_inc(s_one, 1)
                v.memset(ones[:, :].bitcast(self.f32), 1.0).then_inc(s_one, 1)
                v.memset(head_of[:, :], 0.0).then_inc(s_one, 1)
                v.wait_ge(s_one, 7)
                with nc.allow_low_precision(reason="zeros and ones"):
                    v.tensor_reduce(head_of[:, 0:P // HD], self.ident[:, :].rearrange("p (h w) -> p h w", w=HD),
                                    AX.X, ALU.add).then_inc(s_one, 1)
                v.wait_ge(s_one, 8)
                v.wait_ge(s_wh, 2)
                v.tensor_tensor(w[1][:, :, :], raw[:, :, :], w[0][:, :, :].bitcast(self.f32), ALU.subtract).then_inc(s_wl, 1)
                v.tensor_tensor(bias[LO:LO + 1, :], bias_raw[LO:LO + 1, :], bias_hi[LO:LO + 1, :].bitcast(self.f32),
                                ALU.subtract).then_inc(s_wl, 1)
                v.wait_ge(s_c, 16)

                def tile(i, k, j, up):
                    names = [(f"cs{j}", k), (f"sn{j}", k)]
                    if not up:
                        return dve.skip(v, i, names)
                    kb, db = back(k)
                    jb, kj, dj = two_before(k, j)
                    n = j % 2
                    tile_ = 4 * (2 * (i + db) + kb) + j
                    table = rope[:, :, :, :].rearrange("p t c w -> p (t c w)")
                    pe.wait(v, (f"A{j}", k), i)
                    pool.wait(v, (f"ad{jb}", kj), i, dj)
                    heads = lambda a_: a_.rearrange("p (h w) -> p h w", w=HD)
                    cs = table[:, bass.ds(tile_ * 2 * HD, HD)]
                    dve.done(v.tensor_tensor(heads(scaled[:, n, :]), heads(pQ[:, n, :]),
                                             cs.unsqueeze(1).to_broadcast([P, 2 * H, HD]), ALU.mult), names[0])
                    src = pQ[:, n, :].rearrange("p (h r w) -> p h r w", r=2, w=HF)
                    dst = turned[:, n, :].rearrange("p (h r w) -> p h r w", r=2, w=HF)
                    for r in range(2):
                        sn = table[:, bass.ds(tile_ * 2 * HD + HD + r * HF, HF)]
                        m = v.tensor_tensor(dst[:, :, r, :], src[:, :, 1 - r, :],
                                            sn.unsqueeze(1).to_broadcast([P, 2 * H, HF]), ALU.mult)
                    dve.done(m, names[1])

                def low(i, k, j, up):
                    if not up:
                        return dve.skip(v, i, [(f"rl{j}", k)])
                    kb, db = back(k)
                    act.wait(v, (f"rh{j}", k), i)
                    dve.done(v.tensor_tensor(half[1][:, kb, :, j * P:(j + 1) * P], pR[:, j % 2, :, :],
                                             half[0][:, kb, :, j * P:(j + 1) * P].bitcast(self.f32), ALU.subtract), (f"rl{j}", k))

                def body(i, k, rows, up, norms):
                    kb, db = back(k)
                    tile(i, k, 0, up)
                    tile(i, k, 1, up)
                    low(i, k, 0, up)
                    if norms:
                        pe.wait(v, ("N", k), i)
                        dve.wait(v, ("top", kb), i, db)
                        dve.done(v.tensor_reduce(norm[:, :], pN[:, :], AX.X, ALU.max), ("norm", k))
                        dve.wait(v, ("norm", k), i)
                        dve.done(v.tensor_tensor(top[:, :], top[:, :], norm[:, :], ALU.max), ("top", k))
                    else:
                        dve.skip(v, i, [("norm", k), ("top", k)])
                    if rows:
                        v.wait_ge(s_x[k], 16 * (i + 1))
                        dve.wait(v, ("mv", kb), i, db)
                        for j in range(4):
                            m = v.bn_stats(st6[:, j, :], xq[:, k, j, :])
                        dve.done(m, ("stats", k))
                        dve.wait(v, ("stats", k), i)
                        act.wait(v, ("std", kb), i, db)
                        dve.wait(v, ("shift", kb), i, db)
                        self.settle(v)
                        for j in range(4):
                            m = v.bn_aggr(mv[:, j, :], st6[:, j, :])
                        dve.done(m, ("mv", k))
                        act.wait(v, ("std", k), i)
                        dve.wait(v, ("xn", kb), i, db)
                        dve.done(v.reciprocal(rstd[:, :], std[:, :]), ("rstd", k))
                        dve.wait(v, ("rstd", k), i)
                        dve.done(v.scalar_tensor_tensor(shift[:, :], mv[:, :, 0], -1.0, rstd[:, :],
                                                        ALU.mult, ALU.mult), ("shift", k))
                        dve.wait(v, ("shift", k), i)
                        pe.wait(v, ("T1", k), i, -1)
                        for j in range(4):
                            m = v.tensor_scalar(xn[:, k, j, :], xq[:, k, j, :], rstd[:, j:j + 1],
                                                shift[:, j:j + 1], ALU.mult, ALU.add)
                        dve.done(m, ("xn", k))
                    else:
                        dve.skip(v, i, [(n_, k) for n_ in ("stats", "mv", "rstd", "shift", "xn")])
                    tile(i, k, 2, up)
                    low(i, k, 1, up)
                    tile(i, k, 3, up)
                    low(i, k, 2, up)
                    if rows:
                        for c in range(DC):
                            act.wait(v, (f"xh{c}", k), i)
                            dve.done(v.tensor_tensor(xT[1][:, k, c, :], pX[:, c, :], xT[0][:, k, c, :].bitcast(self.f32),
                                                     ALU.subtract), (f"xl{c}", k))
                    else:
                        dve.skip(v, i, [("xl0", k), ("xl1", k)])
                    low(i, k, 3, up)
                stream(v, body)
                dve.wait(v, ("top", 1), J // 2)
                v.engine_nop().then_inc(s_flag, 1)
                v.wait_ge(s_tt, 1)
                v.tensor_reduce(best[:, :], pN[0:1, 0:P].rearrange("p (a h) -> p a h", a=2), AX.X, ALU.max).then_inc(s_flag, 1)
                v.wait_ge(s_flag, 2)
                v.tensor_tensor(prod[:, :], best[:, 0:1], best[:, 1:2], ALU.mult).then_inc(s_flag, 1)
                v.wait_ge(s_flag, 3)
                v.tensor_scalar(self.unsafe[:, :], prod[:, :], SAFE_NORMS, None, ALU.is_gt).then_inc(s_flag, 1)
                v.wait_ge(s_flag, 4)

            @blk.gpsimd
            def _(g):
                def body(i, k, rows, up, norms):
                    if not up:
                        return pool.skip(g, i, [(f"ad{j}", k) for j in range(4)])
                    for j in range(4):
                        jb, kj, dj = two_before(k, j)
                        dve.wait(g, (f"sn{j}", k), i)
                        pe.wait(g, (f"R{jb}", kj), i, dj)
                        pool.done(g.tensor_tensor(roped[:, j % 2, :], scaled[:, j % 2, :], turned[:, j % 2, :], ALU.add),
                                  (f"ad{j}", k))
                stream(g, body)

    def exact_shift(self):
        nc, ALU, ACT, bass, AX = self.nc, self.ALU, self.ACT, self.bass, self.AX
        KR, NEG = 3 * HD, -1e30
        OFF = S - P
        with self.scope() as t, nc.Block() as blk:
            qa, ka = t.sb("qa", [KR, S], self.f32r), t.sb("ka", [KR, S], self.f32r)
            qc = t.sb("qc", [KR, P], self.f32r)
            mask = t.sb("mask", [P, OFF + S], self.bf16)
            ident = t.sb("ident", [P, P], self.bf16)
            mx = t.sb("mx", [P, TPB])
            halves = t.sb("halves", [TPB, 2, P], self.f32r)
            pS = t.ps("pS", [P, S])
            pM = t.ps("pM", [TPB, 512])
            dve_t = t.steps("dve_tile", ["query", "max"])
            pe_t = t.steps("pe_tile", ["scores"])
            dve_h = t.steps("dve_head", ["hi", "lo"])
            pe_h = t.steps("pe_head", ["turned"])
            s_ld, s_st, s_go = t.sem("load"), t.sem("store"), t.sem("go")
            s_mask, s_ident = t.sem("mask"), t.sem("ident")

            def guarded(eng, body):
                r = eng.value_load(self.unsafe[0:1, 0:1], min_val=0, max_val=1)
                with eng.If(r > 0):
                    body(eng)
                eng.end_ifs()

            def heads(eng, body):
                with eng.Fori(0, B * H) as h:
                    body(h)

            @blk.sync
            def _(sp):
                def run(sp):
                    def head(h):
                        sp.wait_ge(s_go, h + 1)
                        sp.dma_start(qa[:, :].bitcast(self.f32), self.qk[0][bass.ds(h * KR, KR), :]).then_inc(s_ld, 16)
                        sp.dma_start(ka[:, :].bitcast(self.f32), self.qk[1][bass.ds(h * KR, KR), :]).then_inc(s_ld, 16)
                        dve_h.wait(sp, "lo", h)
                        sp.dma_start(self.shift.rearrange("h c (t p) -> h t c p", p=P)[h],
                                     halves[:, :, :].bitcast(self.f32)).then_inc(s_st, 16)
                    heads(sp, head)
                    sp.wait_ge(s_st, 16 * B * H)
                guarded(sp, run)

            @blk.gpsimd
            def _(g):
                def run(g):
                    g.memset(mask[:, :], 0.0).then_inc(s_mask, 1)
                    g.wait_ge(s_mask, 1)
                    g.affine_select(out=mask[:, :], in_=mask[:, :], compare_op=ALU.is_ge, fill=NEG, base=OFF,
                                    pattern=[[-1, OFF + S]], channel_multiplier=1).then_inc(s_mask, 1)
                guarded(g, run)

            @blk.vector
            def _(v):
                def run(v):
                    v.tensor_copy(ident[:, :], self.ident[:, :]).then_inc(s_ident, 1)
                    v.sem_inc(s_go, 1)

                    def head(h):
                        v.wait_ge(s_ld, 32 * h + 32)

                        def tile(q):
                            n = h * TPB + q
                            dve_t.done(v.tensor_copy(qc[:, :], qa[:, bass.ds(q * P, P)].bitcast(self.f32)), "query")
                            pe_t.wait(v, "scores", n)
                            dve_t.done(v.tensor_reduce(mx[:, bass.ds(q, 1)], pS[:, :], AX.X, ALU.max), "max")
                            dve_t.wait(v, "max", n)
                        self.settle(v)
                        with v.Fori(0, TPB) as q:
                            tile(q)
                        pe_h.wait(v, "turned", h)
                        dve_h.done(v.tensor_scalar(halves[:, 0, :], pM[:, 0:P], -1.0, None, ALU.mult), "hi")
                        dve_h.wait(v, "hi", h)
                        dve_h.done(v.scalar_tensor_tensor(halves[:, 1, :], pM[:, 0:P], -1.0,
                                                          halves[:, 0, :].bitcast(self.f32), ALU.mult, ALU.subtract), "lo")
                        v.wait_ge(s_st, 16 * h + 16)
                        v.sem_inc(s_go, 1)
                    heads(v, head)
                guarded(v, run)

            @blk.tensor
            def _(t_):
                def run(t_):
                    t_.wait_ge(s_mask, 2)
                    t_.wait_ge(s_ident, 1)

                    def head(h):
                        with t_.Fori(0, TPB) as q:
                            dve_t.wait(t_, "query", h * TPB + q)
                            for c in range(S // 512):
                                o = pS[:, c * 512:(c + 1) * 512]
                                t_.matmul(o, qc[:, :], ka[:, c * 512:(c + 1) * 512], start=True, stop=False)
                                m = t_.matmul(o, ident[:, :], mask[:, bass.ds(q * -P + (OFF + c * 512), 512)],
                                              start=False, stop=True)
                            pe_t.done(m, "scores")
                        dve_t.wait(t_, "max", h * TPB + (TPB - 1))
                        pe_h.done(t_.transpose(pM[:, 0:P], mx[:, :], self.ident[:, :]), "turned")
                    heads(t_, head)
                guarded(t_, run)

    def attention(self):
        nc, ALU, ACT, bass = self.nc, self.ALU, self.ACT, self.bass
        NG, GH = B * H // 4, 4
        QB = S // 512
        KR = 3 * HD + 2
        with self.scope() as t, nc.Block() as blk:
            sq = t.sb("sq", [P, 2, GH, S], self.f32r)
            sk = t.sb("sk", [P, 2, 2, S], self.f32r)
            vg = t.sb("vg", [P, 2, TPB, GH * VW])
            NP = 4
            pr = t.sb("pr", [P, NP, GH, 512])
            oT = t.sb("oT", [P, 2, 512])
            rs = t.sb("rs", [P, 2, 4, GH])
            yo = t.sb("yo", [P, 2, 4, GH, HD])
            pS = t.ps("pS", [P, 3, 2, 512])
            pO = t.ps("pO", [P, 512])
            pT = t.ps("pT", [P, 4, P])

            work = [(k, qb, kt) for k in range(2) for qb in range(QB) for kt in range(4 * qb + 4)]
            NS = len(work)
            last = [n for n, (k, qb, kt) in enumerate(work) if kt == 4 * qb + 3]
            diag = lambda n: work[n][2] - 4 * work[n][1] >= 0

            def span(n):
                k, qb, kt = work[n]
                lo = max(qb * 512, kt * P)
                return lo, (qb + 1) * 512 - lo

            pe_names = [("S", 0, 0), ("S", 0, 1), ("S", 1, 0)]
            for n in range(NS + 3):
                if n + 1 < NS:
                    pe_names.append(("S", n + 1, 1))
                if 1 <= n <= NS:
                    pe_names.append(("O", n - 1))
                if n + 2 < NS:
                    pe_names.append(("S", n + 2, 0))
                if n - 3 in last:
                    pe_names.append(("T", n - 3))
            pe = t.steps("pe", pe_names)
            act = t.steps("act", [("exp", n, h) for n in range(NS) for h in range(2)])
            pool = t.steps("pool", [("mask", n) for n in range(NS) if diag(n)])
            dve = t.steps("dve", [(a_, n) for n in last for a_ in ("copy", "rs", "y")])
            s_ld = [t.sem(f"ld{k}") for k in range(2)]
            s_y = [t.sem(f"y{k}") for k in range(2)]
            s_init = t.sem("init")
            loads = 3 * GH + 1

            @blk.sync
            def _(sp):
                sp.wait_ge(s_init, 2)

                def body(i):
                    for k in range(2):
                        lastk = max(n for n in range(NS) if work[n][0] == k)
                        pe.wait(sp, ("O", lastk), i, -1)
                        g = 2 * i + k
                        for hh in range(GH):
                            pair, base = hh // 2, 64 * (hh % 2)
                            for dst, tab in ((sq[:, k, hh, :], 0), (sk[:, k, pair, :], 1)):
                                sp.dma_start(dst[base:base + 3 * HD, :].bitcast(self.f32),
                                             self.qk[tab][bass.ds((g * GH + hh) * 3 * HD, 3 * HD), :]).then_inc(s_ld[k], 16)
                            sp.dma_start(sq[base + 3 * HD:base + KR, k, hh, :].bitcast(self.f32),
                                         self.shift.rearrange("h c s -> (h c) s")[bass.ds((g * GH + hh) * 2, 2), :]
                                         ).then_inc(s_ld[k], 16)
                        vv = self.vals.rearrange("(b t p) w -> b p t w", b=B, p=P)[g // (NG // B)]
                        sp.dma_start(vg[:, k, :, :], vv[:, :, bass.ds((g % (NG // B)) * (GH * VW), GH * VW)]).then_inc(s_ld[k], 16)
                passes(sp, NG // 2, body)

            @blk.tensor
            def _(t_):
                def scores(i, n, h):
                    k, qb, kt = work[n]
                    u = 2 * n + h
                    if u >= 3:
                        act.wait(t_, ("exp", (u - 3) // 2, (u - 3) % 2), i)
                    else:
                        lb = max(x_ for x_ in range(2 * NS) if x_ % 3 == u % 3)
                        act.wait(t_, ("exp", lb // 2, lb % 2), i, -1)
                    lo, wd = span(n)
                    for e in range(2):
                        m = t_.matmul(pS[:, u % 3, e, 0:wd], sk[:, k, h, kt * P:(kt + 1) * P],
                                      sq[:, k, 2 * h + e, lo:lo + wd], start=True, stop=True)
                    pe.done(m, ("S", n, h))

                def values(i, n):
                    k, qb, kt = work[n]
                    act.wait(t_, ("exp", n, 1), i)
                    if diag(n):
                        pool.wait(t_, ("mask", n), i)
                    if kt == 0:
                        j = last.index(next(x_ for x_ in last if x_ >= n))
                        dve.wait(t_, ("copy", last[j - 1]), i, 0 if j else -1)
                    lo, wd = span(n)
                    off = lo - qb * 512
                    for e in range(GH):
                        m = t_.matmul(pO[e * VW:(e + 1) * VW, off:off + wd], vg[:, k, kt, e * VW:(e + 1) * VW],
                                      pr[:, n % NP, e, 0:wd], start=kt == 0, stop=kt == 4 * qb + 3)
                    pe.done(m, ("O", n))

                def turn(i, n):
                    j = last.index(n)
                    dve.wait(t_, ("copy", n), i)
                    dve.wait(t_, ("y", last[j - 1]), i, 0 if j else -1)
                    for q in range(4):
                        m = t_.transpose(pT[:, q, :], oT[:, j % 2, q * P:(q + 1) * P], self.ident[:, :])
                    pe.done(m, ("T", n))

                def body(i):
                    t_.wait_ge(s_ld[0], 16 * loads * (i + 1))
                    for name, n, *h in pe_names:
                        if name == "S":
                            if h[0] == 0 and n and work[n][0] != work[n - 1][0]:
                                t_.wait_ge(s_ld[1], 16 * loads * (i + 1))
                            scores(i, n, h[0])
                        else:
                            {"O": values, "T": turn}[name](i, n)
                passes(t_, NG // 2, body)

            @blk.scalar
            def _(a):
                def body(i):
                    for n in range(NS):
                        lo, wd = span(n)
                        for h in range(2):
                            u = 2 * n + h
                            pe.wait(a, ("S", n, h), i)
                            if h == 0:
                                pe.wait(a, ("O", (n - NP) % NS), i, 0 if n >= NP else -1)
                            act.done(a.activation(pr[:, n % NP, 2 * h:2 * h + 2, 0:wd], pS[:, u % 3, :, 0:wd], ACT.Exp,
                                                  scale=HD ** -0.5), ("exp", n, h))
                passes(a, NG // 2, body)

            yv = self.y.rearrange("(b q t p) d -> b q p t d", b=B, q=QB, p=P)

            def store(eng, i, n):
                k, qb, kt = work[n]
                dve.wait(eng, ("y", n), i)
                g, jj = 2 * i + k, last.index(n) % 2
                dst = yv[g // (NG // B)][qb][:, :, bass.ds((g % (NG // B)) * GH * HD, GH * HD)]
                eng.dma_start(dst, yo[:, jj, :, :, :].rearrange("p t h w -> p t (h w)")).then_inc(s_y[jj], 16)

            @blk.gpsimd
            def _(g):
                def body(i):
                    for n in range(NS):
                        if n - 7 in last:
                            store(g, i, n - 7)
                        if diag(n):
                            act.wait(g, ("exp", n, 1), i)
                            self.settle(g)
                            blk_ = pr[:, n % NP, :, 0:P]
                            pool.done(g.affine_select(out=blk_, in_=blk_, compare_op=ALU.is_ge, fill=0.0, base=0,
                                                      pattern=[[0, GH], [1, P]], channel_multiplier=-1), ("mask", n))
                    store(g, i, NS - 1)
                passes(g, NG // 2, body)
                for k in range(2):
                    g.wait_ge(s_y[k], 16 * (NG // 2) * len(last) // 2)

            @blk.vector
            def _(v):
                v.memset(sq[:, :, :, :].bitcast(self.f32), 0.0).then_inc(s_init, 1)
                v.memset(sk[:, :, :, :].bitcast(self.f32), 1.0).then_inc(s_init, 1)

                def body(i):
                    for j, n in enumerate(last):
                        k, qb, kt = work[n]
                        jj = j % 2
                        pe.wait(v, ("O", n), i)
                        pe.wait(v, ("T", last[j - 2]), i, 0 if j >= 2 else -1)
                        dve.done(v.tensor_copy(oT[:, jj, :], pO[:, :]), ("copy", n))
                        pe.wait(v, ("T", n), i)
                        heads = pT[:, :, :].rearrange("p t (h w) -> p t h w", w=VW)
                        dve.wait(v, ("y", last[j - 2]), i, 0 if j >= 2 else -1)
                        dve.done(v.reciprocal(rs[:, jj, :, :], heads[:, :, :, HD]), ("rs", n))
                        dve.wait(v, ("rs", n), i)
                        cnt = i * (len(last) // 2) + j // 2
                        if not (isinstance(cnt, int) and cnt == 0):
                            v.wait_ge(s_y[jj], 16 * cnt)
                        dve.done(v.tensor_tensor(yo[:, jj, :, :, :], heads[:, :, :, 0:HD],
                                                 rs[:, jj, :, :].unsqueeze(3).to_broadcast([P, 4, GH, HD]), ALU.mult), ("y", n))
                passes(v, NG // 2, body)


    def output(self, x, out):
        nc, ALU, ACT = self.nc, self.ALU, self.ACT
        with self.scope() as t, nc.Block() as blk:
            raw = t.sb("raw", [P, DC, D])
            w = [t.sb(f"w{h}", [P, DC, D], self.f32r) for h in range(2)]
            bias = t.sb("bias", [P, D])
            yq, xq, xb, ob = (t.sb(n_, [P, 2, 4, D]) for n_ in ("yq", "xq", "xb", "ob"))
            yT = [t.sb(f"yT{h}", [P, 2, DC, 4 * P], self.f32r) for h in range(2)]
            pX = t.ps("pX", [P, DC, 4 * P])
            pO = t.ps("pO", [P, 4, 512])
            per = lambda *names: [(n, k) for k in range(2) for n in names]
            pe = t.steps("pe", per("T0", "T1", "O0", "O1", "O2", "O3"))
            act = t.steps("act", per("yh0", "yh1"))
            dve = t.steps("dve", per("yl0", "yl1", "o0", "o1", "o2", "o3"))
            pool = t.steps("pool", per("xb"))
            s_w, s_wh, s_wl = t.sem("w"), t.sem("wh"), t.sem("wl")
            s_y = [t.sem(f"y{k}") for k in range(2)]
            s_x = [t.sem(f"x{k}") for k in range(2)]
            s_out = [t.sem(f"out{k}") for k in range(2)]
            J = NQ
            quads = lambda a_: a_.rearrange("(q t p) d -> q p t d", t=4, p=P)

            @blk.sync
            def _(sp):
                sp.dma_start(raw[:, :, :], self.ins["WoT"].rearrange("(c p) f -> p c f", p=P)).then_inc(s_w, 16)
                sp.dma_start(bias[:, :], self.ins["b_qkvo"][0:1, 3 * D:4 * D].partition_broadcast(P)).then_inc(s_w, 16)

                def body(i):
                    for k in range(2):
                        pe.wait(sp, ("T1", k), i, -1)
                        sp.dma_start(yq[:, k, :, :], quads(self.y)[2 * i + k]).then_inc(s_y[k], 16)
                        pool.wait(sp, ("xb", k), i, -1)
                        sp.dma_start(xq[:, k, :, :], quads(x)[2 * i + k]).then_inc(s_x[k], 16)
                passes(sp, J // 2, body)

            @blk.tensor
            def _(t_):
                t_.wait_ge(s_wl, 1)

                def body(i):
                    for k in range(2):
                        kb, db = (k - 1) % 2, (k - 1) // 2
                        t_.wait_ge(s_y[k], 16 * (i + 1))
                        for c in range(DC):
                            dve.wait(t_, (f"yl{c}", kb), i, db)
                            for j in range(4):
                                m = t_.transpose(pX[:, c, j * P:(j + 1) * P], yq[:, k, j, c * P:(c + 1) * P], self.ident[:, :])
                            pe.done(m, (f"T{c}", k))
                        dve.wait(t_, ("yl1", k), i)
                        for j in range(4):
                            dve.wait(t_, (f"o{j}", kb), i, db)
                            o = pO[:, j, 0:D]
                            for c in range(DC):
                                y_hi, y_lo = (yT[h][:, k, c, j * P:(j + 1) * P] for h in range(2))
                                t_.matmul(o, y_hi, w[0][:, c, :], start=c == 0, stop=False)
                                t_.matmul(o, y_hi, w[1][:, c, :], start=False, stop=False)
                                m = t_.matmul(o, y_lo, w[0][:, c, :], start=False, stop=c == DC - 1)
                            pe.done(m, (f"O{j}", k))
                passes(t_, J // 2, body)

            @blk.scalar
            def _(a):
                a.wait_ge(s_w, 32)
                a.activation(w[0][:, :, :], raw[:, :, :], ACT.Copy).then_inc(s_wh, 1)

                def body(i):
                    for k in range(2):
                        for c in range(DC):
                            pe.wait(a, (f"T{c}", k), i)
                            pe.wait(a, ("O3", k), i, -1)
                            act.done(a.activation(yT[0][:, k, c, :], pX[:, c, :], ACT.Copy), (f"yh{c}", k))
                passes(a, J // 2, body)

            @blk.gpsimd
            def _(g):
                g.wait_ge(s_w, 32)

                def body(i):
                    for k in range(2):
                        g.wait_ge(s_x[k], 16 * (i + 1))
                        dve.wait(g, ("o3", k), i, -1)
                        pool.done(g.tensor_tensor(xb[:, k, :, :], xq[:, k, :, :],
                                                  bias[:, :].unsqueeze(1).to_broadcast([P, 4, D]), ALU.add), ("xb", k))
                        dve.wait(g, ("o3", k), i)
                        g.dma_start(quads(out)[2 * i + k], ob[:, k, :, :]).then_inc(s_out[k], 16)
                passes(g, J // 2, body)
                for k in range(2):
                    g.wait_ge(s_out[k], 16 * (J // 2))

            @blk.vector
            def _(v):
                v.wait_ge(s_wh, 1)
                v.tensor_tensor(w[1][:, :, :], raw[:, :, :], w[0][:, :, :].bitcast(self.f32), ALU.subtract).then_inc(s_wl, 1)

                def body(i):
                    for k in range(2):
                        for c in range(DC):
                            act.wait(v, (f"yh{c}", k), i)
                            dve.done(v.tensor_tensor(yT[1][:, k, c, :], pX[:, c, :], yT[0][:, k, c, :].bitcast(self.f32),
                                                     ALU.subtract), (f"yl{c}", k))
                        pool.wait(v, ("xb", k), i)
                        if not (isinstance(i, int) and i == 0):
                            v.wait_ge(s_out[k], 16 * i)
                        for j in range(4):
                            pe.wait(v, (f"O{j}", k), i)
                            dve.done(v.tensor_tensor(ob[:, k, j, :], pO[:, j, 0:D], xb[:, k, j, :], ALU.add), (f"o{j}", k))
                passes(v, J // 2, body)

    def attn(self, x, out):
        with self.scope() as st:
            self.unsafe = st.sb("unsafe", [1, 1], self.i32)
            self.projections(x)
            self.exact_shift()
            self.attention()
            self.output(x, out)


def build(nc, ins, out):
    prog = Program(nc, ins, out)
    with prog.scope() as st:
        prog.load_constants(st)
        prog.ffn(ins["x"], prog.x1)
        prog.attn(prog.x1, prog.x2)
        prog.ffn(prog.x2, out)


def layout(inputs):
    a = {k: np.asarray(v) for k, v in inputs.items()}
    p = np.arange(P)
    same = (p[:, None] % E == p[None, :] % E)
    masks = np.concatenate([p[:, None] <= p[None, :], np.ones((P, P)), same,
                            np.broadcast_to(np.arange(WQ), (P, WQ))], 1).astype(np.float32)
    route = np.concatenate([p[:, None] % WQ == p[None, :] // 8, p[:, None] // WQ == np.arange(P // WQ)[None, :],
                            p[:, None] % 8 == np.arange(8)[None, :], p[:, None]], 1).astype(np.float32)
    theta = (np.float32(1.0) / np.power(np.float32(10000.0), np.arange(0, HD, 2, dtype=np.float32) / np.float32(HD))).astype(np.float32)
    ang = np.arange(1, S + 1, dtype=np.float32)[:, None] * theta[None, :]
    ang = np.concatenate([ang, ang], 1).astype(np.float64)
    sign = np.where(np.arange(HD) < HD // 2, -1.0, 1.0)
    rope = np.stack([np.cos(ang), np.sin(ang) * sign], 1).astype(np.float32)
    t = lambda w: np.ascontiguousarray(w.T)
    te = lambda w: np.ascontiguousarray(np.transpose(w, (0, 2, 1)))
    return {
        "x": a["L0_attn_x"].reshape(N, D),
        "WqkT": np.ascontiguousarray(np.concatenate([a["L0_attn_Wq"], a["L0_attn_Wk"]], 0).T),
        "WvT": t(a["L0_attn_Wv"]), "WoT": t(a["L0_attn_Wo"]),
        "b_qkvo": np.concatenate([a["L0_attn_bq"], a["L0_attn_bk"], a["L0_attn_bv"], a["L0_attn_bo"]]).reshape(1, 4 * D),
        "gate_wT": t(a["L0_ffn_gate_w"]),
        "WgT": te(a["L0_ffn_Wg"]), "WuT": te(a["L0_ffn_Wu"]), "WdT": te(a["L0_ffn_Wd"]),
        "WsgT": t(a["L0_ffn_Ws_g"]), "WsuT": t(a["L0_ffn_Ws_u"]), "WsdT": t(a["L0_ffn_Ws_d"]),
        "c_ident": np.eye(P, dtype=np.float32),
        "c_masks": masks, "c_route": route,
        "c_bits": np.ascontiguousarray(np.broadcast_to(np.r_[0, 0, 1 << np.arange(NBITS - 3, -1, -1)], (P, NBITS))).astype(np.int32),
        "c_rope": np.ascontiguousarray(np.tile(rope.reshape(TPB, P, 2, HD).transpose(1, 0, 2, 3), (1, B, 1, 1))),
    }


def kernel(**inputs):
    import concourse.bacc as bacc
    from concourse import mybir
    from concourse.bass_utils import run_bass_kernel_spmd

    nc = bacc.Bacc("TRN2", target_bir_lowering=False, num_devices=1)
    arrays = layout(inputs)
    ins = {n: nc.dram_tensor(n, a.shape, mybir.dt.from_np(a.dtype), kind="ExternalInput").ap()
           for n, a in arrays.items()}
    out = nc.dram_tensor("out", [N, D], mybir.dt.float32, kind="ExternalOutput").ap()
    build(nc, ins, out)
    r = run_bass_kernel_spmd(nc, [arrays], core_ids=[0])
    return r.results[0]["out"].reshape(B, S, D)
```

```python
from contextlib import ExitStack

import numpy as np

B, S, D = 2, 2048, 256
N = B * S
P = 128
NT = N // P
TPB = S // P
NQ = NT // 4
E, F = 16, 512
CAP = S * 2 // E
H, HD = 16, 16
DC = D // P
FC = F // P
ROW = D + E
WQ = 16
VW = 32
EPS = 1e-5
SAFE_NORMS = 14000.0
NBITS = 30


class Steps:

    def __init__(self, sem, names):
        self.sem, self.names, self.K = sem, names, len(names)
        self.at = {n: k for k, n in enumerate(names)}
        assert len(self.at) == self.K
        self.next = 0

    def value(self, name, i, d=0):
        c = self.at[name] + 1 + d * self.K
        return i * self.K + c

    def wait(self, eng, name, i, d=0):
        v = self.value(name, i, d)
        if isinstance(v, int) and v <= 0:
            return
        eng.wait_ge(self.sem, v)

    def done(self, ins, name):
        assert self.names[self.next] == name, (self.names[self.next], name)
        self.next = (self.next + 1) % self.K
        ins.then_inc(self.sem, 1)

    def skip(self, eng, i, names):
        first = self.at[names[0]]
        v = i * self.K + first
        if v > 0:
            eng.wait_ge(self.sem, v)
        for n in names:
            assert self.names[self.next] == n, (self.names[self.next], n)
            self.next = (self.next + 1) % self.K
        eng.sem_inc(self.sem, len(names))


def passes(eng, n, body, tail=1):
    body(0)
    if n > tail + 1:
        with eng.Fori(1, n - tail) as i:
            body(i)
    for i in range(max(1, n - tail), n):
        body(i)


class Program:
    def __init__(self, nc, ins, out):
        import concourse.bass as bass
        from concourse import mybir
        self.nc, self.bass, self.ins, self.out = nc, bass, ins, out
        self.f32, self.f32r = mybir.dt.float32, mybir.dt.float32r
        self.bf16, self.i32 = mybir.dt.bfloat16, mybir.dt.int32
        self.ACT, self.ALU, self.AX = mybir.ActivationFunctionType, mybir.AluOpType, mybir.AxisListType

        def dram(name, shape):
            return nc.dram_tensor(name, shape, self.f32, kind="Internal").ap()

        self.x1 = dram("x_after_ffn1", [N, D])
        self.x2 = dram("x_after_attn", [N, D])
        self.table = dram("token_table", [N, ROW])
        self.qk = [dram(n, [B * H * 2 * HD, S]) for n in ("q_rows", "k_rows")]
        self.shift = dram("shift", [B * H, 2, S])
        self.vals = dram("values", [N, H * VW])
        self.y = dram("attn_heads", [N, D])

    def settle(self, eng):
        eng.sem_inc(self.settled, 1)

    def scope(self):
        st = ExitStack()
        nc = self.nc
        tag = f"{nc.next_id()}_"
        st.sb = lambda name, shape, dt=self.f32: st.enter_context(nc.sbuf_tensor(tag + name, shape, dt))
        st.ps = lambda name, shape, dt=self.f32: st.enter_context(nc.psum_tensor(tag + name, shape, dt))
        st.sem = lambda name: st.enter_context(nc.semaphore(tag + name))
        st.steps = lambda name, names: Steps(st.sem(name), names)
        return st

    def load_stack(self, eng, dst, a, head, sem):
        tab, ds = self.qk[a], self.bass.ds
        for lo, n in ((0, 2 * HD), (2 * HD, HD)) if a == 0 else ((0, HD), (HD, 2 * HD)):
            eng.dma_start(dst[lo:lo + n, :].bitcast(self.f32), tab[ds(head * (2 * HD), n), :]).then_inc(sem, 16)

    def product3(self, pe, out, w_hi, w_lo, x_hi, x_lo, start, stop):
        pe.matmul(out, w_hi, x_hi, start=start, stop=False)
        pe.matmul(out, w_hi, x_lo, start=False, stop=False)
        return pe.matmul(out, w_lo, x_hi, start=False, stop=stop)

    def load_constants(self, st):
        nc, ALU = self.nc, self.ALU
        self.ident = st.sb("ident", [P, P])
        self.tri = st.sb("tri", [P, P], self.bf16)
        self.ones = st.sb("ones", [P, P], self.bf16)
        self.same_expert = st.sb("same_expert", [P, P], self.bf16)
        route = st.sb("route", [P, P + P // WQ + 8 + 1])
        self.spread = route[:, 0:P]
        self.own_expert = route[:, P:P + P // WQ]
        self.own_column = route[:, P + P // WQ:P + P // WQ + 8]
        self.place = route[:, P + P // WQ + 8:]
        self.bits = st.sb("bits", [P, NBITS], self.i32)
        self.ones32 = st.sb("ones32", [E, P])
        self.gate = st.sb("gate", [P, DC, E])
        self.eps = st.sb("eps", [P, 1])
        self.settled = st.sem("settled")
        with self.scope() as t, nc.Block() as blk:
            raw = t.sb("raw", [P, 3 * P])
            s_in, s_id, s_cast = t.sem("in"), t.sem("ident"), t.sem("cast")

            @blk.sync
            def _(sp):
                sp.dma_start(self.ident[:, :], self.ins["c_ident"]).then_inc(s_id, 16)
                sp.dma_start(raw[:, :], self.ins["c_masks"]).then_inc(s_in, 16)
                sp.dma_start(self.bits[:, :], self.ins["c_bits"]).then_inc(s_id, 16)
                sp.dma_start(self.gate[:, :, :], self.ins["gate_wT"].rearrange("(c p) e -> p c e", p=P)).then_inc(s_id, 16)
                sp.dma_start(route[:, :], self.ins["c_route"]).then_inc(s_id, 16)
                sp.wait_ge(s_id, 64)

            @blk.vector
            def _(dve):
                dve.memset(self.ones32[:, :], 1.0)
                dve.memset(self.eps[:, :], EPS)
                dve.wait_ge(s_in, 16)
                for k, m in enumerate((self.tri, self.ones, self.same_expert)):
                    c = dve.tensor_copy(m[:, :], raw[:, k * P:(k + 1) * P])
                c.then_inc(s_cast, 1)
                dve.wait_ge(s_cast, 1)

    def ln_router(self, x):
        nc, ALU, ACT, AX = self.nc, self.ALU, self.ACT, self.AX
        scores = self.scores
        with self.scope() as t, nc.Block() as blk:
            xq = t.sb("xq", [P, 2, 4, D])
            xn = t.sb("xn", [P, 2, 4, D])
            st6 = t.sb("st6", [P, 2, 4, 6])
            mv = t.sb("mv", [P, 2, 4, 2])
            std = t.sb("std", [P, 2, 4])
            rstd = t.sb("rstd", [P, 2, 4])
            shift = t.sb("shift", [P, 2, 4])
            xT = t.sb("xT", [P, 2, DC, 4 * P])
            mx = t.sb("mx", [P, NT])
            dif = t.sb("dif", [P, NT, E])
            ex = t.sb("ex", [P, NT, E])
            pT = t.ps("pT", [P, 2, DC, 4 * P])
            pL = t.ps("pL", [P, NT * E])
            s_x = [t.sem(f"x{k}") for k in range(2)]
            s_w = [t.sem(f"w{k}") for k in range(2)]
            s_raw, s_hi = t.sem("raw"), t.sem("hi")
            raw = [t.sb("raw_g", [P, DC, F]), t.sb("raw_u", [P, DC, F]), t.sb("raw_d", [P, FC, D])]
            per = lambda *names: [(n, k) for k in range(2) for n in names]
            dve = t.steps("dve", per("stats", "mv", "rstd", "shift", "xn", "xT1"))
            act = t.steps("act", per("std", "xT0"))
            pe = t.steps("pe", per("T", "L"))
            s_sm = t.sem("softmax_dve")
            s_ex = t.sem("softmax_act")
            s_rows, s_turned = t.sem("rows"), t.sem("turned")
            xv = x.rearrange("(q t p) d -> q p t d", t=4, p=P)
            tv = self.table[:, 0:D].rearrange("(q t p) d -> q p t d", t=4, p=P)

            def stream(eng, body):
                def both(i):
                    for k in range(2):
                        s_ = 2 * i + k if isinstance(i, int) else None
                        body(i, k, s_ is None or s_ < NQ, s_ is None or 1 <= s_ <= NQ)
                passes(eng, NQ // 2 + 1, both)

            @blk.sync
            def _(sp):
                def body(i):
                    for k in range(2):
                        dve.wait(sp, ("xn", k), i, -1)
                        sp.dma_start(xq[:, k, :, :], xv[2 * i + k]).then_inc(s_x[k], 16)
                passes(sp, NQ // 2, body)
                for dst, name in zip(raw, ("WsgT", "WsuT", "WsdT")):
                    sp.dma_start(dst[:, :, :], self.ins[name].rearrange("(c p) f -> p c f", p=P)).then_inc(s_raw, 16)
                for k in range(2):
                    sp.wait_ge(s_w[k], 16)
                    sp.dma_start(self.xr[:, k, :, 0:D], tv[k]).then_inc(self.s_quads[k], 16)
                sp.wait_ge(s_sm, 6)
                with nc.allow_non_contiguous_dma(reason="64-byte rows"):
                    sp.dma_start(self.table[:, D:ROW].rearrange("(t p) e -> p t e", p=P),
                                 scores[:, :, :]).then_inc(self.s_scores, 16)

            @blk.gpsimd
            def _(pool):
                def body(i):
                    for k in range(2):
                        dve.wait(pool, ("xn", k), i)
                        pool.dma_start(tv[2 * i + k], xn[:, k, :, :]).then_inc(s_w[k], 16)
                passes(pool, NQ // 2, body)
                for w, (hi, lo) in enumerate(self.shared_halves):
                    pool.wait_ge(s_hi, w + 1)
                    m = pool.tensor_tensor(lo[:, 0, :, :], raw[w][:, :, :], hi[:, 0, :, :].bitcast(self.f32), ALU.subtract)
                for k in range(2):
                    pool.wait_ge(s_w[k], 16 * (NQ // 2))

            @blk.vector
            def _(v):
                def body(i, k, rows, up):
                    kb, db = 1 - k, k - 1
                    if rows:
                        v.wait_ge(s_x[k], 16 * (i + 1))
                        for j in range(4):
                            m = v.bn_stats(st6[:, k, j, :], xq[:, k, j, :])
                        dve.done(m, ("stats", k))
                        dve.wait(v, ("stats", k), i)
                        self.settle(v)
                        for j in range(4):
                            m = v.bn_aggr(mv[:, k, j, :], st6[:, k, j, :])
                        dve.done(m, ("mv", k))
                    else:
                        dve.skip(v, i, [("stats", k), ("mv", k)])
                    if rows:
                        act.wait(v, ("std", k), i)
                        dve.done(v.reciprocal(rstd[:, k, :], std[:, k, :]), ("rstd", k))
                        dve.wait(v, ("rstd", k), i)
                        dve.done(v.scalar_tensor_tensor(shift[:, k, :], mv[:, k, :, 0], -1.0, rstd[:, k, :],
                                                        ALU.mult, ALU.mult), ("shift", k))
                        dve.wait(v, ("shift", k), i)
                        pe.wait(v, ("T", k), i, -1)
                        if not (isinstance(i, int) and i == 0):
                            v.wait_ge(s_w[k], 16 * i)
                        for j in range(4):
                            m = v.tensor_scalar(xn[:, k, j, :], xq[:, k, j, :], rstd[:, k, j:j + 1],
                                                shift[:, k, j:j + 1], ALU.mult, ALU.add)
                        dve.done(m, ("xn", k))
                    else:
                        dve.skip(v, i, [(n_, k) for n_ in ("rstd", "shift", "xn")])
                    if up:
                        pe.wait(v, ("T", kb), i, db)
                        pe.wait(v, ("L", k), i, -1)
                        dve.done(v.tensor_copy(xT[:, kb, 1, :], pT[:, kb, 1, :]), ("xT1", k))
                    else:
                        dve.skip(v, i, [("xT1", k)])
                stream(v, body)
                pe.wait(v, ("L", 0), NQ // 2)
                lg = pL[:, :].rearrange("p (t e) -> p t e", e=E)
                bc = lambda a: a[:, :].unsqueeze(2).to_broadcast([P, NT, E])
                v.tensor_reduce(mx[:, :], lg, AX.X, ALU.max).then_inc(s_sm, 1)
                v.wait_ge(s_sm, 1)
                v.tensor_tensor(dif[:, :, :], lg, bc(mx), ALU.subtract).then_inc(s_sm, 1)
                v.wait_ge(s_ex, 1)
                v.wait_ge(s_sm, 2)
                v.tensor_reduce(mx[:, :], ex[:, :, :], AX.X, ALU.add).then_inc(s_sm, 1)
                v.wait_ge(s_sm, 3)
                v.reciprocal(mx[:, :], mx[:, :]).then_inc(s_sm, 1)
                v.wait_ge(s_sm, 4)
                v.tensor_tensor(scores[:, :, :], ex[:, :, :], bc(mx), ALU.mult).then_inc(s_sm, 2)
                v.memset(self.best[:, :], 0.0).then_inc(s_rows, 1)
                v.wait_ge(s_turned, 1)
                v.tensor_copy(self.rows[:, :, :], pT[:, 0, 0, :].rearrange("p (g k) -> p g k", k=P)).then_inc(s_rows, 1)
                v.wait_ge(s_rows, 2)

            @blk.scalar
            def _(a):
                def body(i, k, rows, up):
                    kb, db = 1 - k, k - 1
                    if rows:
                        dve.wait(a, ("mv", k), i)
                        dve.wait(a, ("rstd", k), i, -1)
                        act.done(a.activation(std[:, k, :], mv[:, k, :, 1], ACT.Sqrt, bias=self.eps[:, :]), ("std", k))
                    else:
                        act.skip(a, i, [("std", k)])
                    if up:
                        pe.wait(a, ("T", kb), i, db)
                        pe.wait(a, ("L", k), i, -1)
                        act.done(a.activation(xT[:, kb, 0, :], pT[:, kb, 0, :], ACT.Copy), ("xT0", k))
                    else:
                        act.skip(a, i, [("xT0", k)])
                stream(a, body)
                a.wait_ge(s_raw, 48)
                for w, (hi, lo) in enumerate(self.shared_halves):
                    a.activation(hi[:, 0, :, :], raw[w][:, :, :], ACT.Copy).then_inc(s_hi, 1)
                a.wait_ge(s_sm, 2)
                a.activation(ex[:, :, :], dif[:, :, :], ACT.Exp).then_inc(s_ex, 1)

            @blk.tensor
            def _(t_):
                def body(i, k, rows, up):
                    kb, db = 1 - k, k - 1
                    if rows:
                        dve.wait(t_, ("xn", k), i)
                        dve.wait(t_, ("xT1", kb), i, db)
                        act.wait(t_, ("xT0", kb), i, db)
                        for j in range(4):
                            for c in range(DC):
                                m = t_.transpose(pT[:, k, c, j * P:(j + 1) * P], xn[:, k, j, c * P:(c + 1) * P],
                                                 self.ident[:, :])
                        pe.done(m, ("T", k))
                    else:
                        pe.skip(t_, i, [("T", k)])
                    if up:
                        dve.wait(t_, ("xT1", k), i)
                        act.wait(t_, ("xT0", k), i)
                        for j in range(4):
                            o = pL[:, self.bass.ds((2 * (i + db) + kb) * 4 * E + j * E, E)]
                            for c in range(DC):
                                m = t_.matmul(o, xT[:, kb, c, j * P:(j + 1) * P], self.gate[:, c, :],
                                              start=c == 0, stop=c == DC - 1)
                        pe.done(m, ("L", k))
                    else:
                        pe.skip(t_, i, [("L", k)])
                stream(t_, body)
                t_.wait_ge(s_sm, 6)
                for g in range(NT // 8):
                    m = t_.transpose(pT[:, 0, 0, g * P:(g + 1) * P],
                                     scores[:, 8 * g:8 * g + 8, :].rearrange("p t e -> p (t e)"), self.ident[:, :])
                m.then_inc(s_turned, 1)

    def routing(self, t, bank):
        nc, ALU, ACT, AX, f32, bf16 = self.nc, self.ALU, self.ACT, self.AX, self.f32, self.bf16
        scores, idx = self.scores, self.idx
        TE = TPB * E
        G = P // WQ
        NG = E // G
        FAR = 4096.0
        ROUND = float(3 << 22)
        diag = t.sb("diag", [E, B, E])
        thr = t.sb("thr", [P, B, E])
        gt, eq, sel = (t.sb(n, [P, B, TPB, E], bf16) for n in ("gt", "eq", "sel"))
        need = t.sb("need", [P, B, E])
        fits = t.sb("fits", [P, B, TPB, E])
        rank, quot = t.sb("rank", [P, B * TE]), t.sb("quot", [P, B * TE])
        hi, lo = t.sb("hi", [P, B * TE], bf16), t.sb("lo", [P, B * TE], bf16)
        hot_hi = t.sb("hot_hi", [P, TPB * NG, WQ, G], bf16)
        hot_lo = t.sb("hot_lo", [P, WQ, TE], bf16)
        tok = t.sb("tok", [P, 2, WQ, TE], bf16)
        own, mine = t.sb("own", [P, B, NG, WQ, G]), t.sb("mine", [P, B * NG * 2, 8, G])
        found = t.sb("found", [P, B, NG, 2, G])
        s_v = t.sem("route_dve")
        s_go = t.sem("route_go")
        s_pe = t.sem("route_pe")
        s_hot, s_tok = t.sem("hot"), t.sem("tok")
        flat = lambda a: a[:, :, :, :].rearrange("p b t e -> p (b t e)")
        by_expert = bank[:, 0:B * E].rearrange("p (b e) -> p b e", e=E)
        p_rank = bank[:, :].rearrange("p (b t e) -> p b t e", b=B, e=E)
        p_tok = bank[:, :].rearrange("p (n c w) -> p n c w", n=NG, c=2)
        n = [0]

        def link(v, m):
            n[0] += 1
            m.then_inc(s_v, 1)
            v.wait_ge(s_v, n[0])

        def go(v):
            v.sem_inc(s_go, 1)

        def thresholds(v):
            for b in range(B):
                m = v.tensor_scalar(diag[:, b, :], self.ident[0:E, 0:E], self.best[0:E, b:b + 1], None, ALU.mult)
            link(v, m)
            go(v)

        def masks(v):
            v.wait_ge(s_pe, 1)
            link(v, v.tensor_copy(thr[:, :, :], by_expert))
            sc = scores[:, :, :].rearrange("p (b t) e -> p b t e", b=B)
            for b in range(B):
                tb = thr[:, b, :].unsqueeze(1).to_broadcast([P, TPB, E])
                v.tensor_tensor(gt[:, b, :, :], sc[:, b, :, :], tb, ALU.is_gt)
                m = v.tensor_tensor(eq[:, b, :, :], sc[:, b, :, :], tb, ALU.is_equal)
            link(v, m)
            go(v)

        def needed(v):
            v.wait_ge(s_pe, 2)
            link(v, v.tensor_scalar(need[:, :, :], by_expert, -1.0, float(CAP), ALU.mult, ALU.add))
            go(v)

        def select(v):
            v.wait_ge(s_pe, 3)
            for b in range(B):
                nb = need[:, b, :].unsqueeze(1).to_broadcast([P, TPB, E])
                m = v.tensor_tensor(fits[:, b, :, :], p_rank[:, b, :, :], nb, ALU.is_le)
            link(v, m)
            link(v, v.tensor_tensor(flat(fits), flat(fits), flat(eq), ALU.mult))
            link(v, v.tensor_tensor(flat(sel), flat(fits), flat(gt), ALU.add))
            go(v)

        def slots(v):
            v.wait_ge(s_pe, 4)
            link(v, v.scalar_tensor_tensor(rank[:, :], flat(sel), -FAR, bank[:, :], ALU.mult, ALU.add))
            link(v, v.tensor_scalar(rank[:, :], rank[:, :], FAR - 1.0, None, ALU.add))
            link(v, v.tensor_scalar(quot[:, :], rank[:, :], 1.0 / WQ, 0.5 / WQ - 0.5, ALU.mult, ALU.add))
            link(v, v.tensor_scalar(quot[:, :], quot[:, :], ROUND, None, ALU.add))
            link(v, v.tensor_scalar(quot[:, :], quot[:, :], ROUND, None, ALU.subtract))
            v.tensor_copy(hi[:, :], quot[:, :])
            link(v, v.scalar_tensor_tensor(lo[:, :], quot[:, :], -float(WQ), rank[:, :], ALU.mult, ALU.add))

        def one_hot(v, hot, part, b):
            for w_ in range(WQ):
                src = part[:, b * TE:(b + 1) * TE]
                m = v.tensor_scalar(hot(w_), src.rearrange("p (c g) -> p c g", g=G), float(w_), None, ALU.is_equal)
            return m

        def low(v, b):
            v.wait_ge(s_pe, 4 + b)
            link(v, one_hot(v, lambda w_: hot_lo[:, w_, :].rearrange("p (c g) -> p c g", g=G), lo, b))
            v.sem_inc(s_hot, 1)

        def high(v, b):
            one_hot(v, lambda w_: hot_hi[:, :, w_, :], hi, b)
            link(v, v.tensor_scalar(tok[:, 0, :, :], hot_lo[:, :, :], self.place, None, ALU.mult))
            go(v)

        def columns(v, b):
            v.wait_ge(s_pe, 5 + b)
            mine_ = own[:, b, :, :, :].rearrange("p n w g -> p n (w g)")
            link(v, v.tensor_copy(mine_, p_tok[:, :, 0, :]))
            link(v, v.scalar_tensor_tensor(mine_, p_tok[:, :, 1, :], float(P), mine_, ALU.mult, ALU.add))
            cols = own[:, b, :, :, :].rearrange("p n w g -> p (n w) g")
            link(v, v.tensor_tensor(cols, cols, self.own_expert.unsqueeze(1).to_broadcast([P, NG * WQ, G]), ALU.mult))
            if b == B - 1:
                go(v)

        def rows_of(v):
            v.wait_ge(s_pe, 7)
            link(v, v.tensor_tensor(mine[:, :, :, :], bank[:, :].rearrange("p (c w g) -> p c w g", w=8, g=G),
                                    self.own_column.unsqueeze(1).unsqueeze(3).to_broadcast([P, B * NG * 2, 8, G]), ALU.mult))
            link(v, v.tensor_reduce(found[:, :, :, :, :].rearrange("p b n h g -> p (b n h) g"),
                                    mine[:, :, :, :].rearrange("p c w g -> p c g w"), AX.X, ALU.add))
            for b in range(B):
                m = v.tensor_scalar(idx[:, :, b, :].rearrange("p (n g) h -> p n h g", g=G), found[:, b, :, :, :],
                                    float(b * S), None, ALU.add)
            link(v, m)

        dve = {(6, 0): [thresholds], (6, 1): [masks], (6, 2): [needed], (6, 3): [select], (6, 4): [slots],
               (7, 0): [lambda v: low(v, 0)], (7, 2): [lambda v: high(v, 0)],
               (8, 0): [lambda v: columns(v, 0), lambda v: low(v, 1)], (8, 2): [lambda v: high(v, 1)],
               (9, 1): [lambda v: columns(v, 1)], (9, 2): [rows_of]}

        def times_tile(a, b, quarter):
            a.wait_ge(s_hot, b + 1)
            for tt in range(quarter * TPB // 4, (quarter + 1) * TPB // 4):
                cols = slice(tt * E, (tt + 1) * E)
                m = a.activation(tok[:, 1, :, cols], hot_lo[:, :, cols], ACT.Copy, scale=float(tt))
            m.then_inc(s_tok, 1)

        act = {(7 + b, q): (lambda a, b=b, q=q: times_tile(a, b, q)) for b in range(B) for q in range(4)}

        def spread_thresholds(t_):
            t_.wait_ge(s_go, 1)
            t_.matmul(bank[:, 0:B * E], self.ones32[:, :], diag[:, :, :].rearrange("p b e -> p (b e)"),
                      start=True, stop=True).then_inc(s_pe, 1)

        def counts(t_):
            t_.wait_ge(s_go, 2)
            for tt in range(TPB):
                m = t_.matmul(by_expert, self.ones[:, :], gt[:, :, tt, :], start=tt == 0, stop=tt == TPB - 1)
            m.then_inc(s_pe, 1)

        def ranks(t_, mask, v_go):
            t_.wait_ge(s_go, v_go)
            t_.matmul(bank[:, :], self.tri[:, :], flat(mask), start=True, stop=False)
            for tt in range(TPB - 1):
                m = t_.matmul(p_rank[:, :, tt + 1:, :], self.ones[:, :],
                              mask[:, :, tt, :].unsqueeze(2).to_broadcast([P, B, TPB - 1 - tt, E]),
                              start=False, stop=tt == TPB - 2)
            m.then_inc(s_pe, 1)

        def tokens(t_, b):
            t_.wait_ge(s_go, 5 + b)
            t_.wait_ge(s_tok, 4 * (b + 1))
            for g in range(NG):
                for tt in range(TPB):
                    c0 = tt * E + g * G
                    m = t_.matmul(bank[:, g * 2 * WQ * G:(g + 1) * 2 * WQ * G].rearrange("p (c w g) -> p c w g", c=2, g=G),
                                  hot_hi[:, tt * NG + g, :, :].rearrange("p w g -> p (w g)"), tok[:, :, :, c0:c0 + G],
                                  start=tt == 0, stop=tt == TPB - 1)
            m.then_inc(s_pe, 1)

        def spread_rows(t_):
            t_.wait_ge(s_go, 7)
            t_.matmul(bank[:, :], self.spread, own[:, :, :, :, :].rearrange("p b n w g -> p (b n w g)"),
                      start=True, stop=True).then_inc(s_pe, 1)

        pe = {(6, 0): spread_thresholds, (6, 1): counts, (6, 2): lambda t_: ranks(t_, eq, 3),
              (6, 3): lambda t_: ranks(t_, sel, 4), (7, 3): lambda t_: tokens(t_, 0),
              (8, 4): lambda t_: tokens(t_, 1), (9, 1): spread_rows}
        self.routed = lambda: (s_v, n[0])
        return dve, act, pe

    def experts(self, x, out, shared):
        nc, ALU, ACT, bass = self.nc, self.ALU, self.ACT, self.bass
        J = NQ if shared else E
        W = 4 * P
        with self.scope() as t, nc.Block() as blk:
            if shared:
                wg, wu, wd = self.shared_halves
            else:
                wg = [t.sb(f"wg{h}", [P, 2, DC, F], self.f32r) for h in range(2)]
                wu = [t.sb(f"wu{h}", [P, 2, DC, F], self.f32r) for h in range(2)]
                wd = [t.sb(f"wd{h}", [P, 2, FC, D], self.f32r) for h in range(2)]
            xr, (raw_g, raw_u, raw_d) = self.xr, self.raw_weights
            xT = [t.sb(f"xT{h}", [P, 2, DC, W], self.f32r) for h in range(2)]
            gl = t.sb("gl", [P, 2, W])
            hf = t.sb("hf", [P, 2, W])
            hT = [t.sb(f"hT{h}", [P, 2, FC, W], self.f32r) for h in range(2)]
            eo = t.sb("eo", [P, 2, 4, D])
            xres = t.sb("xres", [P, 2, 4, D]) if shared else None
            wt = t.sb("wt", [P, 2, 4])
            gidx = self.gidx
            sidx = t.sb("sidx", [P, 2, 4], self.i32)
            pG, pU = t.ps("pG", [P, 2, W]), t.ps("pU", [P, 2, W])
            pD = t.ps("pD", [P, 2, 2, D])
            pX = t.ps("pX", [P, W])
            p_cnt = t.ps("p_cnt", [P, 512]) if shared else None

            per = lambda *names: [(n, k) for k in range(2) for n in names]
            pe = t.steps("pe", per("G0", "U0", "G1", "U1", "T0", "D0", "D1", "T1", "G2", "U2", "G3", "U3"))
            a_own = () if shared else ("wgh", "wuh")
            act = t.steps("act", per(*a_own, "gelu0", "hh0", "gelu1", "hh1", "xh0", "xh1", "gelu2", "hh2", "gelu3", "hh3",
                                     *(() if shared else ("wdh",))))
            dve = t.steps("dve", per(*(() if shared else ("wgl",)), "mul0", "mul1", "hl0", "hl1", "xl0", "ev0", "ev1",
                                     "xl1", "wt", "mul2", "mul3", "hl2", "hl3"))
            pool = t.steps("pool", per(*(() if shared else ("wul", "si", "wdl"))) or ["none"])
            index = self.index
            s_rows = self.s_quads if shared else self.s_gathered
            s_res = [t.sem(f"res{k}") for k in range(2)] if shared else None
            s_raw = self.s_raw
            s_last = t.sem("last")
            s_out = [t.sem(f"out{k}") for k in range(2)]
            if shared:
                BITS, FIRST = 5, 6
                assert BITS * FIRST == NBITS
                GB = NT // 8 // B
                cand, keep = t.sb("cand", [P, B]), t.sb("keep", [P, B])
                ge = t.sb("ge", [P, S // 8], self.bf16)
                cnt = t.sb("cnt", [P, B], self.bf16)
                bit = t.steps("bit", ["cand", "cnt0", "cnt1", "keep", "best"])
                tot = t.steps("tot", ["tot"])
                route_dve, route_act, route_pe = self.routing(t, p_cnt)
            rows_inc = 16 if shared else 64
            out_inc = 16 if shared else 64
            ob = lambda k: 0 if shared else k
            tail = 2 if shared else 1

            tv = self.table[:, 0:D].rearrange("(q t p) d -> q p t d", t=4, p=P)
            xv = x.rearrange("(q t p) d -> q p t d", t=4, p=P)
            ov = out.rearrange("(q t p) d -> q p t d", t=4, p=P)
            src = [self.ins[n] for n in ("WgT", "WuT", "WdT")]

            def other(k, d):
                return (k + d) % 2, (k + d) // 2

            class Pass:
                def __init__(p, i, k):
                    p.i, p.k, p.n = i, k, 1 - k
                    s = 2 * i + k if isinstance(i, int) else None
                    p.rows = s is None or s < J
                    p.up = s is None or 1 <= s <= J
                    p.down = s is None or s >= 2
                    p.s = s
                    p.searches = shared and (s is None or s < FIRST)

            def stream(eng, body, tail=1):
                def both(i):
                    for k in range(2):
                        body(Pass(i, k))
                passes(eng, J // 2 + 1, both, tail)

            def split_weights(eng_op, eng, which, slot):
                raw = (raw_g, raw_u, raw_d)[which]
                hi, lo = (wg, wu, wd)[which]
                if eng_op == "hi":
                    return eng.activation(hi[:, slot, :, :], raw[:, :, :], ACT.Copy)
                return eng.tensor_tensor(lo[:, slot, :, :], raw[:, :, :], hi[:, slot, :, :].bitcast(self.f32), ALU.subtract)

            @blk.sync
            def _(sp):
                def weight(w, i, k):
                    wsrc = src[w].rearrange("e (c p) f -> e p c f", p=P)
                    sp.dma_start((raw_g, raw_u, raw_d)[w][:, :, :], wsrc[2 * i + k]).then_inc(s_raw[w], 16)

                def weights(i, k):
                    for w in range(3):
                        weight(w, i, k)

                def body(p):
                    i, k = p.i, p.k
                    if shared:
                        if p.rows and p.s not in (0, 1):
                            pe.wait(sp, ("T1", k), i, -1)
                            sp.dma_start(xr[:, k, :, 0:D], tv[2 * i + k]).then_inc(s_rows[k], 16)
                        if p.down:
                            dve.wait(sp, ("ev1", k), i, -1)
                            sp.dma_start(xres[:, k, :, :], xv[2 * (i - 1) + k]).then_inc(s_res[k], 16)
                        if p.s == J + 1:
                            weights(0, 0)
                            dve.wait(sp, ("ev1", k), i)
                            sp.dma_start(ov[2 * (i - 1) + k], eo[:, k, :, :]).then_inc(s_last, 16)
                            sp.wait_ge(s_last, 16)
                    elif p.rows and p.s != 0:
                        for w, (dst, by, st) in enumerate(((raw_g, dve, "wgl"), (raw_u, pool, "wul"), (raw_d, pool, "wdl"))):
                            kb, db = other(k, -1)
                            by.wait(sp, (st, kb), i, db)
                            weight(w, i, k)
                stream(sp, body)

            @blk.tensor
            def _(t_):
                def gu(p, f):
                    i, k, n = p.i, p.k, p.n
                    b = f % 2
                    kb, db = (k, 0) if f >= 2 else other(k, -1)
                    fb = (f + 2) % 4
                    for name, ps, w, user, eng_u in (("G", pG, wg, "mul", dve), ("U", pU, wu, "mul", dve)):
                        if name == "G":
                            act.wait(t_, (f"gelu{fb}", kb), i, db)
                        dve.wait(t_, (f"mul{fb}", kb), i, db)
                        for c in range(DC):
                            m = self.product3(t_, ps[:, b, :], w[0][:, ob(n), c, f * P:(f + 1) * P],
                                              w[1][:, ob(n), c, f * P:(f + 1) * P],
                                              xT[0][:, n, c, :], xT[1][:, n, c, :], c == 0, c == DC - 1)
                        pe.done(m, (f"{name}{f}", k))
                        if name == "G" and f == 1:
                            side(p, 0)

                def turn(p, c):
                    i, k = p.i, p.k
                    if not p.rows:
                        return pe.skip(t_, i, [(f"T{c}", k)])
                    if c == 0:
                        t_.wait_ge(s_rows[k], rows_inc * (i + 1))
                    cb, kc, dc = (0, k, 0) if c else (1, *other(k, -1))
                    dve.wait(t_, (f"xl{cb}", kc), i, dc)
                    for q in range(4):
                        m = t_.transpose(pX[:, q * P:(q + 1) * P], xr[:, k, q, c * P:(c + 1) * P], self.ident[:, :])
                    pe.done(m, (f"T{c}", k))

                def side(p, m):
                    if p.searches:
                        n = 2 * BITS * p.i + (BITS * p.k + m)
                        bit.wait(t_, "cnt1", n)
                        tot.done(t_.matmul(p_cnt[:, 0:B], self.same_expert[:, :], cnt[:, :], start=True, stop=True), "tot")
                    elif shared and (p.s, m) in route_pe:
                        route_pe[p.s, m](t_)

                def body(p):
                    i, k, n = p.i, p.k, p.n
                    kb, db = other(k, -1)
                    if p.up:
                        dve.wait(t_, ("xl1", kb), i, db)
                        if not shared:
                            pool.wait(t_, ("wul", kb), i, db)
                        gu(p, 0)
                        gu(p, 1)
                    else:
                        side(p, 0)
                        pe.skip(t_, i, [(x_, k) for x_ in ("G0", "U0", "G1", "U1")])
                    turn(p, 0)
                    if p.down:
                        dve.wait(t_, ("hl3", kb), i, db)
                        if not shared:
                            pool.wait(t_, ("wdl", k), i, -1)
                        for h in range(2):
                            dve.wait(t_, (f"ev{h}", kb), i, db)
                            for r in range(2):
                                for c in range(FC):
                                    q = 2 * h + r
                                    m = self.product3(t_, pD[:, h, r, :], hT[0][:, k, c, q * P:(q + 1) * P],
                                                      hT[1][:, k, c, q * P:(q + 1) * P], wd[0][:, ob(k), c, :],
                                                      wd[1][:, ob(k), c, :], c == 0, c == FC - 1)
                                if (h, r) == (1, 0):
                                    side(p, 1)
                            pe.done(m, (f"D{h}", k))
                    else:
                        side(p, 1)
                        pe.skip(t_, i, [("D0", k), ("D1", k)])
                    turn(p, 1)
                    side(p, 2)
                    if p.up:
                        gu(p, 2)
                        side(p, 3)
                        gu(p, 3)
                        side(p, 4)
                    else:
                        side(p, 3)
                        side(p, 4)
                        pe.skip(t_, i, [(x_, k) for x_ in ("G2", "U2", "G3", "U3")])
                stream(t_, body, tail)

            @blk.scalar
            def _(a):
                def hidden(p, f):
                    i, k, n = p.i, p.k, p.n
                    if not p.up:
                        act.skip(a, i, [(f"gelu{f}", k), (f"hh{f}", k)])
                        return
                    kb, db = (k, 0) if f >= 2 else other(k, -1)
                    pe.wait(a, (f"G{f}", k), i)
                    dve.wait(a, (f"mul{(f + 2) % 4}", kb), i, db)
                    act.done(a.activation(gl[:, f % 2, :], pG[:, f % 2, :], ACT.Gelu), (f"gelu{f}", k))
                    dve.wait(a, (f"mul{f}", k), i)
                    if f == 0:
                        kc, dc = other(k, -1)
                        pe.wait(a, ("D1", kc), i, dc)
                    act.done(a.activation(hT[0][:, n, f, :], hf[:, f % 2, :], ACT.Copy), (f"hh{f}", k))

                def tiles(p, m):
                    if shared and (p.s, m) in route_act:
                        route_act[p.s, m](a)

                def body(p):
                    i, k = p.i, p.k
                    kb, db = other(k, -1)
                    if not shared and p.rows:
                        pe.wait(a, ("U3", kb), i, db)
                        for w, nm in enumerate(("wgh", "wuh")):
                            a.wait_ge(s_raw[w], 16 * (2 * i + k + 1))
                            act.done(split_weights("hi", a, w, k), (nm, k))
                    elif not shared:
                        act.skip(a, i, [("wgh", k), ("wuh", k)])
                    hidden(p, 0)
                    tiles(p, 0)
                    hidden(p, 1)
                    tiles(p, 1)
                    if p.rows:
                        pe.wait(a, ("U3", kb), i, db)
                        for c in range(DC):
                            pe.wait(a, (f"T{c}", k), i)
                            act.done(a.activation(xT[0][:, k, c, :], pX[:, :], ACT.Copy), (f"xh{c}", k))
                            if c == 0:
                                tiles(p, 2)
                    else:
                        tiles(p, 2)
                        act.skip(a, i, [(x_, k) for x_ in ("xh0", "xh1")])
                    tiles(p, 3)
                    hidden(p, 2)
                    hidden(p, 3)
                    if not shared:
                        if p.rows:
                            a.wait_ge(s_raw[2], 16 * (2 * i + k + 1))
                            pe.wait(a, ("D1", k), i)
                            act.done(split_weights("hi", a, 2, k), ("wdh", k))
                        else:
                            act.skip(a, i, [("wdh", k)])
                stream(a, body, tail)

            @blk.vector
            def _(v):
                def mul(p, f):
                    i, k = p.i, p.k
                    act.wait(v, (f"gelu{f}", k), i)
                    pe.wait(v, (f"U{f}", k), i)
                    kb, db = (k, 0) if f >= 2 else other(k, -1)
                    act.wait(v, (f"hh{(f + 2) % 4}", kb), i, db)
                    dve.wait(v, (f"hl{(f + 2) % 4}", kb), i, db)
                    dve.done(v.tensor_tensor(hf[:, f % 2, :], gl[:, f % 2, :], pU[:, f % 2, :], ALU.mult), (f"mul{f}", k))

                def low(p, f):
                    i, k, n = p.i, p.k, p.n
                    act.wait(v, (f"hh{f}", k), i)
                    dve.done(v.tensor_tensor(hT[1][:, n, f, :], hf[:, f % 2, :], hT[0][:, n, f, :].bitcast(self.f32),
                                             ALU.subtract), (f"hl{f}", k))

                def xlow(p, c):
                    i, k = p.i, p.k
                    if not p.rows:
                        return dve.skip(v, i, [(f"xl{c}", k)])
                    act.wait(v, (f"xh{c}", k), i)
                    dve.done(v.tensor_tensor(xT[1][:, k, c, :], pX[:, :], xT[0][:, k, c, :].bitcast(self.f32),
                                             ALU.subtract), (f"xl{c}", k))

                def evacuate(p, h):
                    i, k = p.i, p.k
                    if not p.down:
                        return dve.skip(v, i, [(f"ev{h}", k)])
                    if h == 0:
                        if not isinstance(i, int) or 2 * i + k >= 4:
                            v.wait_ge(s_out[k], out_inc * (i - 1))
                        if shared:
                            v.wait_ge(s_res[k], 16 * i)
                    pe.wait(v, (f"D{h}", k), i)
                    for r in range(2):
                        q = 2 * h + r
                        if shared:
                            m = v.scalar_tensor_tensor(eo[:, k, q, :], pD[:, h, r, :], 0.5, xres[:, k, q, :],
                                                       ALU.mult, ALU.add)
                        else:
                            m = v.tensor_scalar(eo[:, k, q, :], pD[:, h, r, :], wt[:, k, q:q + 1], 0.5,
                                                ALU.mult, ALU.mult)
                    dve.done(m, (f"ev{h}", k))

                def decide(n):
                    tot.wait(v, "tot", n)
                    bit.done(v.scalar_tensor_tensor(keep[:, :], p_cnt[:, 0:B], float(CAP), cand[:, :],
                                                    ALU.is_ge, ALU.mult), "keep")
                    bit.wait(v, "keep", n)
                    bit.done(v.tensor_tensor(self.best[:, :], self.best[:, :], keep[:, :], ALU.max), "best")

                def side(p, m):
                    if not p.searches:
                        if shared:
                            if (p.s, m) == (FIRST, 0):
                                decide(NBITS - 1)
                                bit.wait(v, "best", NBITS - 1)
                            for step in route_dve.get((p.s, m), []):
                                step(v)
                        return
                    n = 2 * BITS * p.i + (BITS * p.k + m)
                    if not (isinstance(n, int) and n == 0):
                        decide(n - 1)
                        bit.wait(v, "best", n, -1)
                    one = self.bits[:, bass.ds(n, 1)].to_broadcast([P, B])
                    bit.done(v.tensor_tensor(cand[:, :].bitcast(self.i32), self.best[:, :].bitcast(self.i32), one,
                                             ALU.bitwise_or), "cand")
                    bit.wait(v, "cand", n)
                    for b in range(B):
                        if b:
                            bit.wait(v, "cnt0", n)
                        c_ = v.tensor_scalar(ge[:, :], self.rows[:, b * GB:(b + 1) * GB, :].rearrange("p g k -> p (g k)"),
                                             cand[:, b:b + 1], None, ALU.is_ge, ALU.add, accum_out=cnt[:, b:b + 1])
                        bit.done(c_, f"cnt{b}")

                def body(p):
                    i, k = p.i, p.k
                    if p.rows and not shared:
                        act.wait(v, ("wgh", k), i)
                        dve.done(split_weights("lo", v, 0, k), ("wgl", k))
                    elif not shared:
                        dve.skip(v, i, [("wgl", k)])
                    side(p, 0)
                    if p.up:
                        mul(p, 0)
                        mul(p, 1)
                        side(p, 1)
                        low(p, 0)
                        low(p, 1)
                    else:
                        side(p, 1)
                        dve.skip(v, i, [(x_, k) for x_ in ("mul0", "mul1", "hl0", "hl1")])
                    xlow(p, 0)
                    evacuate(p, 0)
                    side(p, 2)
                    evacuate(p, 1)
                    side(p, 3)
                    xlow(p, 1)
                    if p.rows and not shared:
                        dve.wait(v, ("ev1", k), i)
                        col = xr[:, k, :, :].rearrange("p q w -> p w q")[:, bass.ds(2 * i + (D + k), 1), :]
                        dve.done(v.tensor_copy(wt[:, k, :].unsqueeze(1), col), ("wt", k))
                    else:
                        dve.skip(v, i, [("wt", k)])
                    if p.up:
                        mul(p, 2)
                        side(p, 4)
                        mul(p, 3)
                        low(p, 2)
                        low(p, 3)
                    else:
                        side(p, 4)
                        dve.skip(v, i, [(x_, k) for x_ in ("mul2", "mul3", "hl2", "hl3")])
                stream(v, body, tail)

            @blk.gpsimd
            def _(g):
                idx = self.idx

                def take_rows(i, k):
                    flat = idx[:, :, :, :].rearrange("p e b h -> p (e b h)")
                    m = g.tensor_copy(gidx[:, k, :], flat[:, bass.ds((2 * i + k) * 4, 4)])
                    return m

                def gather(k):
                    for q in range(4):
                        g.indirect_dma_start(xr[:, k, q, :], None, self.table[:, :],
                                             bass.IndirectOffsetOnAxis(gidx[:, k, q:q + 1], 0)).then_inc(self.s_gathered[k], 16)

                if shared:
                    def body(p):
                        i, k = p.i, p.k
                        if p.s == J + 1:
                            g.wait_ge(*self.routed())
                            g.wait_ge(self.s_scores, 16)
                            pe.wait(g, ("T1", 0), J // 2 - 1)
                            index.done(take_rows(0, 0), ("gi", 0))
                            index.wait(g, ("gi", 0), 0)
                            self.settle(g)
                            gather(0)
                        elif p.down:
                            dve.wait(g, ("ev1", k), i)
                            g.dma_start(ov[2 * (i - 1) + k], eo[:, k, :, :]).then_inc(s_out[k], 16)
                    stream(g, body)
                    for k in range(2):
                        g.wait_ge(s_out[k], 16 * (J // 2 - k))
                    return

                def fetch(i, k):
                    if not (isinstance(i, int) and i == 0):
                        g.wait_ge(s_rows[k], 64 * i)
                    index.done(take_rows(i, k), ("gi", k))
                    pe.wait(g, ("T1", k), i, -1)
                    dve.wait(g, ("wt", k), i, -1)
                    index.wait(g, ("gi", k), i)
                    self.settle(g)
                    gather(k)

                def body(p):
                    i, k = p.i, p.k
                    if p.rows:
                        act.wait(g, ("wuh", k), i)
                        pool.done(split_weights("lo", g, 1, k), ("wul", k))
                    else:
                        pool.skip(g, i, [("wul", k)])
                    ki, di = other(k, 1)
                    if not isinstance(i, int) or 2 * i + k + 1 < J:
                        fetch(i + di, ki)
                    if p.down:
                        if not isinstance(i, int) or 2 * i + k >= 3:
                            g.wait_ge(s_out[1 - k], 64 * (i - 1 + k))
                        flat = idx[:, :, :, :].rearrange("p e b h -> p (e b h)")
                        if not isinstance(i, int) or 2 * i + k >= 4:
                            g.wait_ge(s_out[k], 64 * (i - 1))
                        m = g.tensor_copy(sidx[:, k, :], flat[:, bass.ds((2 * i + k - 2) * 4, 4)])
                        pool.done(m, ("si", k))
                        pool.wait(g, ("si", k), i)
                        dve.wait(g, ("ev1", k), i)
                        self.settle(g)
                        for q in range(4):
                            g.indirect_dma_start(out, bass.IndirectOffsetOnAxis(sidx[:, k, q:q + 1], 0),
                                                 eo[:, k, q, :], None, compute_op=ALU.add).then_inc(s_out[k], 16)
                    else:
                        pool.skip(g, i, [("si", k)])
                    if p.rows:
                        act.wait(g, ("wdh", k), i)
                        pool.done(split_weights("lo", g, 2, k), ("wdl", k))
                    else:
                        pool.skip(g, i, [("wdl", k)])
                stream(g, body, 2)
                for k in range(2):
                    g.wait_ge(s_out[k], 64 * (J // 2))

    def ffn(self, x, out):
        with self.scope() as st:
            self.scores = st.sb("scores", [P, NT, E])
            self.idx = st.sb("idx", [P, E, B, CAP // P], self.i32)
            self.rows = st.sb("rows", [P, NT // 8, P])
            self.best = st.sb("best", [P, B])
            self.s_scores = st.sem("scores_stored")
            self.xr = st.sb("xr", [P, 2, 4, ROW])
            self.gidx = st.sb("gidx", [P, 2, 4], self.i32)
            self.index = st.steps("index", [("gi", 0), ("gi", 1)])
            self.s_quads = [st.sem(f"quads{k}") for k in range(2)]
            self.s_gathered = [st.sem(f"gathered{k}") for k in range(2)]
            self.raw_weights = [st.sb("raw_g", [P, DC, F]), st.sb("raw_u", [P, DC, F]), st.sb("raw_d", [P, FC, D])]
            self.s_raw = [st.sem(n) for n in ("raw_g", "raw_u", "raw_d")]
            with self.scope() as ws:
                self.shared_halves = [[ws.sb(f"shared_{n}{h}", [P, 1, *sh], self.f32r) for h in range(2)]
                                      for n, sh in (("gate", (DC, F)), ("up", (DC, F)), ("down", (FC, D)))]
                self.ln_router(x)
                self.experts(x, out, True)
            self.experts(x, out, False)


    def projections(self, x):
        nc, ALU, ACT, bass, AX = self.nc, self.ALU, self.ACT, self.bass, self.AX
        HF = HD // 2
        LO = 32
        with self.scope() as t, nc.Block() as blk:
            raw = t.sb("raw", [P, DC, 3 * D])
            w = [t.sb(f"w{h}", [P, DC, 3 * D], self.f32r) for h in range(2)]
            bias_raw, bias_hi = t.sb("bias_raw", [LO + 1, 3 * D]), t.sb("bias_hi", [LO + 1, 3 * D], self.f32r)
            bias = t.sb("bias", [LO + 1, 3 * D], self.f32r)
            ones = t.sb("ones", [LO + 1, P], self.f32r)
            head_of = t.sb("head_of", [P, 32], self.bf16)
            rope = t.sb("rope", [P, NT, 2, HD])
            xq = t.sb("xq", [P, 2, 4, D])
            xn = t.sb("xn", [P, 2, 4, D])
            st6, mv = t.sb("st6", [P, 4, 6]), t.sb("mv", [P, 4, 2])
            std, rstd, shift = t.sb("std", [P, 4]), t.sb("rstd", [P, 4]), t.sb("shift", [P, 4])
            xT = [t.sb(f"xT{h}", [P, 2, DC, 4 * P], self.f32r) for h in range(2)]
            turned = t.sb("turned", [P, 2, 2 * D])
            scaled = t.sb("scaled", [P, 2, 2 * D])
            roped = t.sb("roped", [P, 2, 2 * D])
            half = [t.sb(f"half{h}", [P, 2, 4, 4 * P], self.f32r) for h in range(2)]
            squares = t.sb("squares", [P, 4, 4 * P], self.bf16)
            vt = t.sb("vt", [P, 2, 4, H, VW])
            norm, top = t.sb("norm", [P, 1]), t.sb("top", [P, 1])
            best, prod = t.sb("best", [1, 2]), t.sb("prod", [1, 1])
            zero = t.sb("zero", [B * H, 2 * S])
            pX = t.ps("pX", [P, DC, 4 * P])
            pQ = t.ps("pQ", [P, 2, 2 * D])
            pV = t.ps("pV", [P, 512])
            pR = t.ps("pR", [P, 2, 4, P])
            pN = t.ps("pN", [P, 4 * P])

            per = lambda *names: [(n, k) for k in range(2) for n in names]
            pe = t.steps("pe", per("A0", "V0", "A1", "V1", "R0", "A2", "V2", "R1", "A3", "V3", "N", "T0", "T1", "R2", "R3"))
            act = t.steps("act", per("std", "v0", "v1", "rh0", "v2", "rh1", "v3", "xh0", "xh1", "rh2", "rh3", "sq"))
            dve = t.steps("dve", per("stats", "mv", "cs0", "sn0", "cs1", "sn1", "rstd", "shift", "xn", "rl0",
                                     "cs2", "sn2", "rl1", "cs3", "sn3", "norm", "top", "xl0", "xl1", "rl2", "rl3"))
            pool = t.steps("pool", per(*(f"ad{j}" for j in range(4))))
            s_w, s_wh, s_wl, s_c, s_b = (t.sem(n) for n in ("w", "wh", "wl", "const", "bias"))
            s_x = [t.sem(f"x{k}") for k in range(2)]
            s_out = [t.sem(f"out{k}") for k in range(2)]
            s_set = t.sem("set")
            s_zero, s_one, s_flag, s_tt = t.sem("zero"), t.sem("one"), t.sem("flag"), t.sem("top_t")
            J = NQ
            NOUT = 16 * 9
            xv = x.rearrange("(q t p) d -> q p t d", t=4, p=P)

            def stream(eng, body, tail=1):
                def both(i):
                    for k in range(2):
                        s_ = 2 * i + k if isinstance(i, int) else None
                        body(i, k, s_ is None or s_ < J, s_ is None or 1 <= s_ <= J, s_ is None or s_ >= 2)
                passes(eng, J // 2 + 1, both, tail)

            def back(k, d=1):
                return (k - d) % 2, (k - d) // 2

            def two_before(k, j):
                return (j - 2, k, 0) if j >= 2 else (j + 2, *back(k))

            @blk.sync
            def _(sp):
                sp.dma_start(xq[:, 0, :, :], xv[0]).then_inc(s_x[0], 16)
                sp.dma_start(raw[:, :, 0:2 * D], self.ins["WqkT"].rearrange("(c p) f -> p c f", p=P)).then_inc(s_w, 16)
                sp.dma_start(raw[:, :, 2 * D:], self.ins["WvT"].rearrange("(c p) f -> p c f", p=P)).then_inc(s_w, 16)
                for row in (0, LO):
                    sp.dma_start(bias_raw[row:row + 1, :], self.ins["b_qkvo"][0:1, 0:3 * D]).then_inc(s_b, 16)
                sp.dma_start(rope[:, :, :, :], self.ins["c_rope"]).then_inc(s_c, 16)
                sp.wait_ge(s_set, 1)
                sp.dma_start(self.shift.rearrange("h c s -> h (c s)"), zero[:, :]).then_inc(s_zero, 16)

                def load(i, k):
                    dve.wait(sp, ("xn", k), i, -1)
                    sp.dma_start(xq[:, k, :, :], xv[2 * i + k]).then_inc(s_x[k], 16)

                def body(i, k, rows, up, norms):
                    kb, db = back(k)
                    if not isinstance(i, int) or 2 * i + k + 1 < J:
                        load(i + k, 1 - k)
                    if up:
                        q = 2 * (i + db) + kb
                        dve.wait(sp, ("rl3", k), i)
                        bb, cc = q // (NQ // B), q % (NQ // B)
                        for a_ in range(2):
                            for part in range(2):
                                for c in range(DC):
                                    dst = self.qk[a_].rearrange("(b c h u f) s -> c u b h f s", b=B, c=DC, u=2, f=HD)[c][part][bb]
                                    sp.dma_start(dst[:, :, bass.ds(cc * 4 * P, 4 * P)],
                                                 half[part][:, kb, 2 * a_ + c, :].bitcast(self.f32)).then_inc(s_out[kb], 16)
                        sp.dma_start(self.vals.rearrange("(q t p) w -> q p t w", t=4, p=P)[q],
                                     vt[:, kb, :, :, :].rearrange("p t h w -> p t (h w)")).then_inc(s_out[kb], 16)
                stream(sp, body, 2)
                for k in range(2):
                    sp.wait_ge(s_out[k], NOUT * (J // 2))
                sp.wait_ge(s_zero, 16)

            @blk.tensor
            def _(t_):
                def product(o, kb, j, lo, hi):
                    t_.matmul(o, ones[:, :], bias[:, lo:hi], start=True, stop=False)
                    for c in range(DC):
                        x_hi, x_lo = (xT[h][:, kb, c, j * P:(j + 1) * P] for h in range(2))
                        t_.matmul(o, x_hi, w[0][:, c, lo:hi], start=False, stop=False)
                        t_.matmul(o, x_hi, w[1][:, c, lo:hi], start=False, stop=False)
                        m = t_.matmul(o, x_lo, w[0][:, c, lo:hi], start=False, stop=c == DC - 1)
                    return m

                def tile(i, k, j):
                    kb, db = back(k)
                    jb, kj, dj = two_before(k, j)
                    dve.wait(t_, (f"sn{jb}", kj), i, dj)
                    pe.done(product(pQ[:, j % 2, :], kb, j, 0, 2 * D), (f"A{j}", k))
                    act.wait(t_, (f"v{j - 1}", k) if j else ("v3", kb), i, 0 if j else db)
                    pe.done(product(pV[:, 0:D], kb, j, 2 * D, 3 * D), (f"V{j}", k))

                def turn(i, k, j):
                    jb, kj, dj = two_before(k, j)
                    pool.wait(t_, (f"ad{j}", k), i)
                    dve.wait(t_, (f"rl{jb}", kj), i, dj)
                    for c in range(4):
                        m = t_.transpose(pR[:, j % 2, c, :], roped[:, j % 2, c * P:(c + 1) * P], self.ident[:, :])
                    pe.done(m, (f"R{j}", k))

                def body(i, k, rows, up, norms):
                    kb, db = back(k)
                    if up:
                        dve.wait(t_, ("xl1", kb), i, db)
                        t_.wait_ge(s_wl, 2)
                        tile(i, k, 0)
                    else:
                        pe.skip(t_, i, [("A0", k), ("V0", k)])
                    if up:
                        tile(i, k, 1)
                        turn(i, k, 0)
                        tile(i, k, 2)
                        turn(i, k, 1)
                        tile(i, k, 3)
                    else:
                        pe.skip(t_, i, [(n_, k) for n_ in ("A1", "V1", "R0", "A2", "V2", "R1", "A3", "V3")])
                    if norms:
                        act.wait(t_, ("sq", kb), i, db)
                        dve.wait(t_, ("norm", kb), i, db)
                        for c in range(4):
                            m = t_.matmul(pN[32 * c:32 * c + 32, :], head_of[:, :], squares[:, c, :], start=True, stop=True)
                        pe.done(m, ("N", k))
                    else:
                        pe.skip(t_, i, [("N", k)])
                    if rows:
                        dve.wait(t_, ("xn", k), i)
                        for c in range(DC):
                            dve.wait(t_, (f"xl{c}", kb), i, db)
                            for j in range(4):
                                m = t_.transpose(pX[:, c, j * P:(j + 1) * P], xn[:, k, j, c * P:(c + 1) * P], self.ident[:, :])
                            pe.done(m, (f"T{c}", k))
                    else:
                        pe.skip(t_, i, [("T0", k), ("T1", k)])
                    if up:
                        turn(i, k, 2)
                        turn(i, k, 3)
                    else:
                        pe.skip(t_, i, [("R2", k), ("R3", k)])
                stream(t_, body)
                t_.wait_ge(s_flag, 1)
                t_.transpose(pN[0:1, 0:P], top[:, :], self.ident[:, :]).then_inc(s_tt, 1)

            @blk.scalar
            def _(a):
                a.wait_ge(s_w, 32)
                a.activation(w[0][:, :, :], raw[:, :, :], ACT.Copy).then_inc(s_wh, 1)
                a.wait_ge(s_b, 32)
                a.wait_ge(s_one, 5)
                for row in (0, LO):
                    m = a.activation(bias_hi[row:row + 1, :], bias_raw[row:row + 1, :], ACT.Copy)
                a.activation(bias[0:1, :], bias_raw[0:1, :], ACT.Copy).then_inc(s_wh, 1)

                def value(i, k, j, up):
                    if not up:
                        return act.skip(a, i, [(f"v{j}", k)])
                    kb, db = back(k)
                    pe.wait(a, (f"V{j}", k), i)
                    a.wait_ge(s_set, 3)
                    if j == 0 and not (isinstance(i, int) and 2 * i + k < 3):
                        a.wait_ge(s_out[kb], NOUT * (i + db))
                    act.done(a.activation(vt[:, kb, j, :, 0:HD], pV[:, 0:D].rearrange("p (h w) -> p h w", w=HD), ACT.Copy),
                             (f"v{j}", k))

                def high(i, k, j, up):
                    if not up:
                        return act.skip(a, i, [(f"rh{j}", k)])
                    kb, db = back(k)
                    pe.wait(a, (f"R{j}", k), i)
                    if j == 0 and not (isinstance(i, int) and 2 * i + k < 3):
                        a.wait_ge(s_out[kb], NOUT * (i + db))
                        act.wait(a, ("sq", k), i, -1)
                    act.done(a.activation(half[0][:, kb, :, j * P:(j + 1) * P], pR[:, j % 2, :, :], ACT.Copy), (f"rh{j}", k))

                def body(i, k, rows, up, norms):
                    kb, db = back(k)
                    if rows:
                        dve.wait(a, ("mv", k), i)
                        act.done(a.activation(std[:, :], mv[:, :, 1], ACT.Sqrt, bias=self.eps[:, :]), ("std", k))
                    else:
                        act.skip(a, i, [("std", k)])
                    value(i, k, 0, up)
                    value(i, k, 1, up)
                    high(i, k, 0, up)
                    value(i, k, 2, up)
                    high(i, k, 1, up)
                    value(i, k, 3, up)
                    if rows:
                        for c in range(DC):
                            pe.wait(a, (f"T{c}", k), i)
                            pe.wait(a, ("V3", kb), i, db)
                            act.done(a.activation(xT[0][:, k, c, :], pX[:, c, :], ACT.Copy), (f"xh{c}", k))
                    else:
                        act.skip(a, i, [("xh0", k), ("xh1", k)])
                    high(i, k, 2, up)
                    high(i, k, 3, up)
                    if up:
                        act.wait(a, ("rh3", k), i)
                        pe.wait(a, ("N", k), i)
                        act.done(a.activation(squares[:, :, :], half[0][:, kb, :, :].bitcast(self.f32), ACT.Square), ("sq", k))
                    else:
                        act.skip(a, i, [("sq", k)])
                stream(a, body)

            @blk.vector
            def _(v):
                v.memset(top[:, :], 0.0).then_inc(s_one, 1)
                v.memset(bias[:, :].bitcast(self.f32), 0.0).then_inc(s_one, 1)
                v.memset(ones[:, :].bitcast(self.f32), 1.0).then_inc(s_one, 1)
                v.memset(head_of[:, :], 0.0).then_inc(s_one, 1)
                v.wait_ge(s_one, 4)
                with nc.allow_low_precision(reason="zeros and ones"):
                    v.tensor_reduce(head_of[:, 0:P // HD], self.ident[:, :].rearrange("p (h w) -> p h w", w=HD),
                                    AX.X, ALU.add).then_inc(s_one, 1)
                v.wait_ge(s_one, 5)
                v.wait_ge(s_c, 16)

                def tile(i, k, j, up):
                    names = [(f"cs{j}", k), (f"sn{j}", k)]
                    if not up:
                        return dve.skip(v, i, names)
                    kb, db = back(k)
                    jb, kj, dj = two_before(k, j)
                    n = j % 2
                    tile_ = 4 * (2 * (i + db) + kb) + j
                    table = rope[:, :, :, :].rearrange("p t c w -> p (t c w)")
                    pe.wait(v, (f"A{j}", k), i)
                    pool.wait(v, (f"ad{jb}", kj), i, dj)
                    heads = lambda a_: a_.rearrange("p (h w) -> p h w", w=HD)
                    cs = table[:, bass.ds(tile_ * 2 * HD, HD)]
                    dve.done(v.tensor_tensor(heads(scaled[:, n, :]), heads(pQ[:, n, :]),
                                             cs.unsqueeze(1).to_broadcast([P, 2 * H, HD]), ALU.mult), names[0])
                    swapped = pQ[:, n, :].rearrange("p (h u f) -> p h u f", u=2, f=HF)
                    out_ = turned[:, n, :].rearrange("p (h u f) -> p h u f", u=2, f=HF)
                    for r in range(2):
                        sn = table[:, bass.ds(tile_ * 2 * HD + HD + r * HF, HF)]
                        m = v.tensor_tensor(out_[:, :, r, :], swapped[:, :, 1 - r, :],
                                            sn.unsqueeze(1).to_broadcast([P, 2 * H, HF]), ALU.mult)
                    dve.done(m, names[1])

                def low(i, k, j, up):
                    if not up:
                        return dve.skip(v, i, [(f"rl{j}", k)])
                    kb, db = back(k)
                    act.wait(v, (f"rh{j}", k), i)
                    dve.done(v.tensor_tensor(half[1][:, kb, :, j * P:(j + 1) * P], pR[:, j % 2, :, :],
                                             half[0][:, kb, :, j * P:(j + 1) * P].bitcast(self.f32), ALU.subtract), (f"rl{j}", k))

                def body(i, k, rows, up, norms):
                    kb, db = back(k)
                    if rows:
                        v.wait_ge(s_x[k], 16 * (i + 1))
                        dve.wait(v, ("mv", kb), i, db)
                        for j in range(4):
                            m = v.bn_stats(st6[:, j, :], xq[:, k, j, :])
                        dve.done(m, ("stats", k))
                        dve.wait(v, ("stats", k), i)
                        act.wait(v, ("std", kb), i, db)
                        dve.wait(v, ("shift", kb), i, db)
                        self.settle(v)
                        for j in range(4):
                            m = v.bn_aggr(mv[:, j, :], st6[:, j, :])
                        dve.done(m, ("mv", k))
                    else:
                        dve.skip(v, i, [("stats", k), ("mv", k)])
                    tile(i, k, 0, up)
                    tile(i, k, 1, up)
                    if rows:
                        act.wait(v, ("std", k), i)
                        dve.wait(v, ("xn", kb), i, db)
                        dve.done(v.reciprocal(rstd[:, :], std[:, :]), ("rstd", k))
                        dve.wait(v, ("rstd", k), i)
                        dve.done(v.scalar_tensor_tensor(shift[:, :], mv[:, :, 0], -1.0, rstd[:, :],
                                                        ALU.mult, ALU.mult), ("shift", k))
                        dve.wait(v, ("shift", k), i)
                        pe.wait(v, ("T1", k), i, -1)
                        for j in range(4):
                            m = v.tensor_scalar(xn[:, k, j, :], xq[:, k, j, :], rstd[:, j:j + 1],
                                                shift[:, j:j + 1], ALU.mult, ALU.add)
                        dve.done(m, ("xn", k))
                    else:
                        dve.skip(v, i, [(n_, k) for n_ in ("rstd", "shift", "xn")])
                    low(i, k, 0, up)
                    tile(i, k, 2, up)
                    low(i, k, 1, up)
                    tile(i, k, 3, up)
                    if norms:
                        pe.wait(v, ("N", k), i)
                        dve.wait(v, ("top", kb), i, db)
                        dve.done(v.tensor_reduce(norm[:, :], pN[:, :], AX.X, ALU.max), ("norm", k))
                        dve.wait(v, ("norm", k), i)
                        dve.done(v.tensor_tensor(top[:, :], top[:, :], norm[:, :], ALU.max), ("top", k))
                    else:
                        dve.skip(v, i, [("norm", k), ("top", k)])
                    if rows:
                        for c in range(DC):
                            act.wait(v, (f"xh{c}", k), i)
                            dve.done(v.tensor_tensor(xT[1][:, k, c, :], pX[:, c, :], xT[0][:, k, c, :].bitcast(self.f32),
                                                     ALU.subtract), (f"xl{c}", k))
                    else:
                        dve.skip(v, i, [("xl0", k), ("xl1", k)])
                    low(i, k, 2, up)
                    low(i, k, 3, up)
                stream(v, body)
                dve.wait(v, ("top", 1), J // 2)
                v.engine_nop().then_inc(s_flag, 1)
                v.wait_ge(s_tt, 1)
                v.tensor_reduce(best[:, :], pN[0:1, 0:P].rearrange("p (a h) -> p a h", a=2), AX.X, ALU.max).then_inc(s_flag, 1)
                v.wait_ge(s_flag, 2)
                v.tensor_tensor(prod[:, :], best[:, 0:1], best[:, 1:2], ALU.mult).then_inc(s_flag, 1)
                v.wait_ge(s_flag, 3)
                v.tensor_scalar(self.unsafe[:, :], prod[:, :], SAFE_NORMS, None, ALU.is_gt).then_inc(s_flag, 1)
                v.wait_ge(s_flag, 4)

            @blk.gpsimd
            def _(g):
                g.memset(zero[:, :], 0.0).then_inc(s_set, 1)
                g.memset(vt[:, :, :, :, :], 0.0).then_inc(s_set, 1)
                g.wait_ge(s_set, 2)
                g.memset(vt[:, :, :, :, HD:HD + 1], 1.0).then_inc(s_set, 1)
                g.wait_ge(s_wh, 1)
                g.tensor_tensor(w[1][:, :, :], raw[:, :, :], w[0][:, :, :].bitcast(self.f32), ALU.subtract).then_inc(s_wl, 1)
                g.wait_ge(s_wl, 1)
                g.wait_ge(s_wh, 2)
                g.wait_ge(s_one, 5)
                g.tensor_tensor(bias[LO:LO + 1, :], bias_raw[LO:LO + 1, :], bias_hi[LO:LO + 1, :].bitcast(self.f32),
                                ALU.subtract).then_inc(s_wl, 1)
                g.wait_ge(s_wl, 2)

                def body(i, k, rows, up, norms):
                    if not up:
                        return pool.skip(g, i, [(f"ad{j}", k) for j in range(4)])
                    for j in range(4):
                        jb, kj, dj = two_before(k, j)
                        dve.wait(g, (f"sn{j}", k), i)
                        pe.wait(g, (f"R{jb}", kj), i, dj)
                        pool.done(g.tensor_tensor(roped[:, j % 2, :], scaled[:, j % 2, :], turned[:, j % 2, :], ALU.add),
                                  (f"ad{j}", k))
                stream(g, body)

    def exact_shift(self):
        nc, ALU, ACT, bass, AX = self.nc, self.ALU, self.ACT, self.bass, self.AX
        KR, NEG = 3 * HD, -1e30
        OFF = S - P
        with self.scope() as t, nc.Block() as blk:
            qa, ka = t.sb("qa", [KR, S], self.f32r), t.sb("ka", [KR, S], self.f32r)
            qc = t.sb("qc", [KR, P], self.f32r)
            mask = t.sb("mask", [P, OFF + S], self.bf16)
            ident = t.sb("ident", [P, P], self.bf16)
            mx = t.sb("mx", [P, TPB])
            halves = t.sb("halves", [TPB, 2, P], self.f32r)
            pS = t.ps("pS", [P, S])
            pM = t.ps("pM", [TPB, 512])
            dve_t = t.steps("dve_tile", ["query", "max"])
            pe_t = t.steps("pe_tile", ["scores"])
            dve_h = t.steps("dve_head", ["hi", "lo"])
            pe_h = t.steps("pe_head", ["turned"])
            s_ld, s_st, s_go = t.sem("load"), t.sem("store"), t.sem("go")
            s_mask, s_ident = t.sem("mask"), t.sem("ident")

            def guarded(eng, body):
                r = eng.value_load(self.unsafe[0:1, 0:1], min_val=0, max_val=1)
                with eng.If(r > 0):
                    body(eng)
                eng.end_ifs()

            def heads(eng, body):
                with eng.Fori(0, B * H) as h:
                    body(h)

            @blk.sync
            def _(sp):
                def run(sp):
                    def head(h):
                        sp.wait_ge(s_go, h + 1)
                        self.load_stack(sp, qa, 0, h, s_ld)
                        self.load_stack(sp, ka, 1, h, s_ld)
                        dve_h.wait(sp, "lo", h)
                        sp.dma_start(self.shift.rearrange("h c (t p) -> h t c p", p=P)[h],
                                     halves[:, :, :].bitcast(self.f32)).then_inc(s_st, 16)
                    heads(sp, head)
                    sp.wait_ge(s_st, 16 * B * H)
                guarded(sp, run)

            @blk.gpsimd
            def _(g):
                def run(g):
                    g.memset(mask[:, :], 0.0).then_inc(s_mask, 1)
                    g.wait_ge(s_mask, 1)
                    g.affine_select(out=mask[:, :], in_=mask[:, :], compare_op=ALU.is_ge, fill=NEG, base=OFF,
                                    pattern=[[-1, OFF + S]], channel_multiplier=1).then_inc(s_mask, 1)
                guarded(g, run)

            @blk.vector
            def _(v):
                def run(v):
                    v.tensor_copy(ident[:, :], self.ident[:, :]).then_inc(s_ident, 1)
                    v.sem_inc(s_go, 1)

                    def head(h):
                        v.wait_ge(s_ld, 64 * h + 64)

                        def tile(q):
                            n = h * TPB + q
                            dve_t.done(v.tensor_copy(qc[:, :], qa[:, bass.ds(q * P, P)].bitcast(self.f32)), "query")
                            pe_t.wait(v, "scores", n)
                            dve_t.done(v.tensor_reduce(mx[:, bass.ds(q, 1)], pS[:, :], AX.X, ALU.max), "max")
                            dve_t.wait(v, "max", n)
                        self.settle(v)
                        with v.Fori(0, TPB) as q:
                            tile(q)
                        pe_h.wait(v, "turned", h)
                        dve_h.done(v.tensor_scalar(halves[:, 0, :], pM[:, 0:P], -1.0, None, ALU.mult), "hi")
                        dve_h.wait(v, "hi", h)
                        dve_h.done(v.scalar_tensor_tensor(halves[:, 1, :], pM[:, 0:P], -1.0,
                                                          halves[:, 0, :].bitcast(self.f32), ALU.mult, ALU.subtract), "lo")
                        v.wait_ge(s_st, 16 * h + 16)
                        v.sem_inc(s_go, 1)
                    heads(v, head)
                guarded(v, run)

            @blk.tensor
            def _(t_):
                def run(t_):
                    t_.wait_ge(s_mask, 2)
                    t_.wait_ge(s_ident, 1)

                    def head(h):
                        with t_.Fori(0, TPB) as q:
                            dve_t.wait(t_, "query", h * TPB + q)
                            for c in range(S // 512):
                                o = pS[:, c * 512:(c + 1) * 512]
                                t_.matmul(o, qc[:, :], ka[:, c * 512:(c + 1) * 512], start=True, stop=False)
                                m = t_.matmul(o, ident[:, :], mask[:, bass.ds(q * -P + (OFF + c * 512), 512)],
                                              start=False, stop=True)
                            pe_t.done(m, "scores")
                        dve_t.wait(t_, "max", h * TPB + (TPB - 1))
                        pe_h.done(t_.transpose(pM[:, 0:P], mx[:, :], self.ident[:, :]), "turned")
                    heads(t_, head)
                guarded(t_, run)

    def attention(self):
        nc, ALU, ACT, bass = self.nc, self.ALU, self.ACT, self.bass
        NG, GH = B * H // 4, 4
        QB = S // 512
        KR = 3 * HD + 2
        with self.scope() as t, nc.Block() as blk:
            sq = t.sb("sq", [P, 2, GH, S], self.f32r)
            sk = t.sb("sk", [P, 2, 2, S], self.f32r)
            vg = t.sb("vg", [P, 2, TPB, GH * VW])
            NP = 4
            pr = t.sb("pr", [P, NP, GH, 512])
            oT = t.sb("oT", [P, 2, 512])
            rs = t.sb("rs", [P, 2, 4, GH])
            yo = t.sb("yo", [P, 2, 4, GH, HD])
            pS = t.ps("pS", [P, 3, 2, 512])
            pO = t.ps("pO", [P, 512])
            pT = t.ps("pT", [P, 4, P])

            work = [(k, qb, kt) for k in range(2) for qb in range(QB) for kt in range(4 * qb + 4)]
            NS = len(work)
            last = [n for n, (k, qb, kt) in enumerate(work) if kt == 4 * qb + 3]
            first = [n for n in range(NS) if n == 0 or work[n][0] != work[n - 1][0]]
            diag = lambda n: work[n][2] - 4 * work[n][1] >= 0

            def span(n):
                k, qb, kt = work[n]
                lo = max(qb * 512, kt * P)
                return lo, (qb + 1) * 512 - lo

            pe_names = [("S", 0, 0), ("S", 0, 1), ("S", 1, 0)]
            for n in range(NS + 3):
                if n + 1 < NS:
                    pe_names.append(("S", n + 1, 1))
                if 1 <= n <= NS:
                    pe_names.append(("O", n - 1))
                if n + 2 < NS:
                    pe_names.append(("S", n + 2, 0))
                if n - 3 in last:
                    pe_names.append(("T", n - 3))
            pe = t.steps("pe", pe_names)
            act = t.steps("act", [("exp", n, h) for n in range(NS) for h in range(2)])
            pool = t.steps("pool", [("mask", n) for n in range(NS) if diag(n)])
            dve = t.steps("dve", [(a_, n) for n in last for a_ in ("copy", "rs", "y")])
            s_ld = [[t.sem(f"ld{k}{pair}") for pair in range(2)] for k in range(2)]
            s_vals = [t.sem(f"vals{k}") for k in range(2)]
            s_y = [t.sem(f"y{k}") for k in range(2)]
            s_zero, s_one = t.sem("zero"), t.sem("one")
            loads = 5 * GH // 2

            @blk.sync
            def _(sp):
                def body(i):
                    for k in range(2):
                        lastk = max(n for n in range(NS) if work[n][0] == k)
                        pe.wait(sp, ("O", lastk), i, -1)
                        g = 2 * i + k
                        for hh in range(GH):
                            pair, base = hh // 2, 64 * (hh % 2)
                            if isinstance(i, int) and i == 0:
                                sp.wait_ge(s_zero, GH * k + hh + 1)
                                sp.wait_ge(s_one, 2 * k + pair + 1)
                            self.load_stack(sp, sq[base:base + 3 * HD, k, hh, :], 0, g * GH + hh, s_ld[k][pair])
                            self.load_stack(sp, sk[base:base + 3 * HD, k, pair, :], 1, g * GH + hh, s_ld[k][pair])
                            sp.dma_start(sq[base + 3 * HD:base + KR, k, hh, :].bitcast(self.f32),
                                         self.shift.rearrange("h c s -> (h c) s")[bass.ds((g * GH + hh) * 2, 2), :]
                                         ).then_inc(s_ld[k][pair], 16)
                        vv = self.vals.rearrange("(b t p) w -> b p t w", b=B, p=P)[g // (NG // B)]
                        sp.dma_start(vg[:, k, :, :], vv[:, :, bass.ds((g % (NG // B)) * (GH * VW), GH * VW)]).then_inc(s_vals[k], 16)
                passes(sp, NG // 2, body)

            @blk.tensor
            def _(t_):
                def scores(i, n, h):
                    k, qb, kt = work[n]
                    u = 2 * n + h
                    if u >= 3:
                        act.wait(t_, ("exp", (u - 3) // 2, (u - 3) % 2), i)
                    else:
                        lb = max(x_ for x_ in range(2 * NS) if x_ % 3 == u % 3)
                        act.wait(t_, ("exp", lb // 2, lb % 2), i, -1)
                    lo, wd = span(n)
                    for e in range(2):
                        m = t_.matmul(pS[:, u % 3, e, 0:wd], sk[:, k, h, kt * P:(kt + 1) * P],
                                      sq[:, k, 2 * h + e, lo:lo + wd], start=True, stop=True)
                    pe.done(m, ("S", n, h))

                def values(i, n):
                    k, qb, kt = work[n]
                    act.wait(t_, ("exp", n, 1), i)
                    if diag(n):
                        pool.wait(t_, ("mask", n), i)
                    if kt == 0:
                        j = last.index(next(x_ for x_ in last if x_ >= n))
                        dve.wait(t_, ("copy", last[j - 1]), i, 0 if j else -1)
                    lo, wd = span(n)
                    off = lo - qb * 512
                    for e in range(GH):
                        m = t_.matmul(pO[e * VW:(e + 1) * VW, off:off + wd], vg[:, k, kt, e * VW:(e + 1) * VW],
                                      pr[:, n % NP, e, 0:wd], start=kt == 0, stop=kt == 4 * qb + 3)
                    pe.done(m, ("O", n))

                def turn(i, n):
                    j = last.index(n)
                    dve.wait(t_, ("copy", n), i)
                    dve.wait(t_, ("y", last[j - 1]), i, 0 if j else -1)
                    for q in range(4):
                        m = t_.transpose(pT[:, q, :], oT[:, j % 2, q * P:(q + 1) * P], self.ident[:, :])
                    pe.done(m, ("T", n))

                def body(i):
                    for name, n, *h in pe_names:
                        if name == "S":
                            if n in first:
                                t_.wait_ge(s_ld[work[n][0]][h[0]], 16 * loads * (i + 1))
                            scores(i, n, h[0])
                        else:
                            if name == "O" and n in first:
                                t_.wait_ge(s_vals[work[n][0]], 16 * (i + 1))
                            {"O": values, "T": turn}[name](i, n)
                passes(t_, NG // 2, body)

            @blk.scalar
            def _(a):
                def body(i):
                    for n in range(NS):
                        lo, wd = span(n)
                        for h in range(2):
                            u = 2 * n + h
                            pe.wait(a, ("S", n, h), i)
                            if h == 0:
                                pe.wait(a, ("O", (n - NP) % NS), i, 0 if n >= NP else -1)
                            act.done(a.activation(pr[:, n % NP, 2 * h:2 * h + 2, 0:wd], pS[:, u % 3, :, 0:wd], ACT.Exp,
                                                  scale=HD ** -0.5), ("exp", n, h))
                passes(a, NG // 2, body)

            yv = self.y.rearrange("(b q t p) d -> b q p t d", b=B, q=QB, p=P)

            def store(eng, i, n):
                k, qb, kt = work[n]
                dve.wait(eng, ("y", n), i)
                g, jj = 2 * i + k, last.index(n) % 2
                dst = yv[g // (NG // B)][qb][:, :, bass.ds((g % (NG // B)) * GH * HD, GH * HD)]
                eng.dma_start(dst, yo[:, jj, :, :, :].rearrange("p t h w -> p t (h w)")).then_inc(s_y[jj], 16)

            @blk.gpsimd
            def _(g):
                for k in range(2):
                    for pair in range(2):
                        g.memset(sk[:, k, pair, :].bitcast(self.f32), 1.0).then_inc(s_one, 1)

                def body(i):
                    for n in range(NS):
                        if n - 7 in last:
                            store(g, i, n - 7)
                        if diag(n):
                            act.wait(g, ("exp", n, 1), i)
                            self.settle(g)
                            blk_ = pr[:, n % NP, :, 0:P]
                            pool.done(g.affine_select(out=blk_, in_=blk_, compare_op=ALU.is_ge, fill=0.0, base=0,
                                                      pattern=[[0, GH], [1, P]], channel_multiplier=-1), ("mask", n))
                    store(g, i, NS - 1)
                passes(g, NG // 2, body)
                for k in range(2):
                    g.wait_ge(s_y[k], 16 * (NG // 2) * len(last) // 2)

            @blk.vector
            def _(v):
                for k in range(2):
                    for hh in range(GH):
                        v.memset(sq[:, k, hh, :].bitcast(self.f32), 0.0).then_inc(s_zero, 1)

                def body(i):
                    for j, n in enumerate(last):
                        k, qb, kt = work[n]
                        jj = j % 2
                        pe.wait(v, ("O", n), i)
                        pe.wait(v, ("T", last[j - 2]), i, 0 if j >= 2 else -1)
                        dve.done(v.tensor_copy(oT[:, jj, :], pO[:, :]), ("copy", n))
                        pe.wait(v, ("T", n), i)
                        heads = pT[:, :, :].rearrange("p t (h w) -> p t h w", w=VW)
                        dve.wait(v, ("y", last[j - 2]), i, 0 if j >= 2 else -1)
                        dve.done(v.reciprocal(rs[:, jj, :, :], heads[:, :, :, HD]), ("rs", n))
                        dve.wait(v, ("rs", n), i)
                        cnt = i * (len(last) // 2) + j // 2
                        if not (isinstance(cnt, int) and cnt == 0):
                            v.wait_ge(s_y[jj], 16 * cnt)
                        dve.done(v.tensor_tensor(yo[:, jj, :, :, :], heads[:, :, :, 0:HD],
                                                 rs[:, jj, :, :].unsqueeze(3).to_broadcast([P, 4, GH, HD]), ALU.mult), ("y", n))
                passes(v, NG // 2, body)


    def output(self, x, out):
        nc, ALU, ACT = self.nc, self.ALU, self.ACT
        with self.scope() as t, nc.Block() as blk:
            raw = t.sb("raw", [P, DC, D])
            w = [t.sb(f"w{h}", [P, DC, D], self.f32r) for h in range(2)]
            bias = t.sb("bias", [P, D])
            yq, xq, xb, ob = (t.sb(n_, [P, 2, 4, D]) for n_ in ("yq", "xq", "xb", "ob"))
            yT = [t.sb(f"yT{h}", [P, 2, DC, 4 * P], self.f32r) for h in range(2)]
            pX = t.ps("pX", [P, 2, DC, 4 * P])
            pO = t.ps("pO", [P, 4, 512])
            per = lambda *names: [(n, k) for k in range(2) for n in names]
            pe = t.steps("pe", per("T0", "T1", "O0", "O1", "O2", "O3"))
            act = t.steps("act", per("yh0", "yh1"))
            dve = t.steps("dve", per("yl0", "yl1", "o0", "o1", "o2", "o3"))
            pool = t.steps("pool", per("xb"))
            s_w, s_wh, s_wl = t.sem("w"), t.sem("wh"), t.sem("wl")
            s_y = [t.sem(f"y{k}") for k in range(2)]
            s_x = [t.sem(f"x{k}") for k in range(2)]
            s_out = [t.sem(f"out{k}") for k in range(2)]
            J = NQ
            def stream(eng, body):
                def both(i):
                    for k in range(2):
                        s_ = 2 * i + k if isinstance(i, int) else None
                        body(i, k, s_ is None or s_ < J, s_ is None or 1 <= s_ <= J)
                passes(eng, J // 2 + 1, both)

            quads = lambda a_: a_.rearrange("(q t p) d -> q p t d", t=4, p=P)

            @blk.sync
            def _(sp):
                sp.dma_start(raw[:, :, :], self.ins["WoT"].rearrange("(c p) f -> p c f", p=P)).then_inc(s_w, 16)
                sp.dma_start(bias[:, :], self.ins["b_qkvo"][0:1, 3 * D:4 * D].partition_broadcast(P)).then_inc(s_w, 16)

                def body(i):
                    for k in range(2):
                        pe.wait(sp, ("T1", k), i, -1)
                        sp.dma_start(yq[:, k, :, :], quads(self.y)[2 * i + k]).then_inc(s_y[k], 16)
                        pool.wait(sp, ("xb", k), i, -1)
                        sp.dma_start(xq[:, k, :, :], quads(x)[2 * i + k]).then_inc(s_x[k], 16)
                passes(sp, J // 2, body)

            @blk.tensor
            def _(t_):
                t_.wait_ge(s_wl, 1)

                def body(i, k, rows, up):
                    kb, db = 1 - k, k - 1
                    if rows:
                        t_.wait_ge(s_y[k], 16 * (i + 1))
                        for c in range(DC):
                            dve.wait(t_, (f"yl{c}", k), i, -1)
                            for j in range(4):
                                m = t_.transpose(pX[:, k, c, j * P:(j + 1) * P], yq[:, k, j, c * P:(c + 1) * P], self.ident[:, :])
                            pe.done(m, (f"T{c}", k))
                    else:
                        pe.skip(t_, i, [("T0", k), ("T1", k)])
                    if not up:
                        return pe.skip(t_, i, [(f"O{j}", k) for j in range(4)])
                    dve.wait(t_, ("yl1", kb), i, db)
                    for j in range(4):
                        dve.wait(t_, (f"o{j}", kb), i, db)
                        o = pO[:, j, 0:D]
                        for c in range(DC):
                            y_hi, y_lo = (yT[h][:, kb, c, j * P:(j + 1) * P] for h in range(2))
                            t_.matmul(o, y_hi, w[0][:, c, :], start=c == 0, stop=False)
                            t_.matmul(o, y_hi, w[1][:, c, :], start=False, stop=False)
                            m = t_.matmul(o, y_lo, w[0][:, c, :], start=False, stop=c == DC - 1)
                        pe.done(m, (f"O{j}", k))
                stream(t_, body)

            @blk.scalar
            def _(a):
                a.wait_ge(s_w, 32)
                a.activation(w[0][:, :, :], raw[:, :, :], ACT.Copy).then_inc(s_wh, 1)

                def body(i, k, rows, up):
                    kb, db = 1 - k, k - 1
                    if not rows:
                        return act.skip(a, i, [("yh0", k), ("yh1", k)])
                    for c in range(DC):
                        pe.wait(a, (f"T{c}", k), i)
                        pe.wait(a, ("O3", kb), i, db)
                        act.done(a.activation(yT[0][:, k, c, :], pX[:, k, c, :], ACT.Copy), (f"yh{c}", k))
                stream(a, body)

            @blk.gpsimd
            def _(g):
                g.wait_ge(s_w, 32)

                def body(i, k, rows, up):
                    kb, db = 1 - k, k - 1
                    if rows:
                        g.wait_ge(s_x[k], 16 * (i + 1))
                        dve.wait(g, ("o3", kb), i, db)
                        pool.done(g.tensor_tensor(xb[:, k, :, :], xq[:, k, :, :],
                                                  bias[:, :].unsqueeze(1).to_broadcast([P, 4, D]), ALU.add), ("xb", k))
                    else:
                        pool.skip(g, i, [("xb", k)])
                    if up:
                        dve.wait(g, ("o3", k), i)
                        g.dma_start(quads(out)[2 * (i + db) + kb], ob[:, kb, :, :]).then_inc(s_out[kb], 16)
                stream(g, body)
                for k in range(2):
                    g.wait_ge(s_out[k], 16 * (J // 2))

            @blk.vector
            def _(v):
                v.wait_ge(s_wh, 1)
                v.tensor_tensor(w[1][:, :, :], raw[:, :, :], w[0][:, :, :].bitcast(self.f32), ALU.subtract).then_inc(s_wl, 1)

                def body(i, k, rows, up):
                    kb, db = 1 - k, k - 1
                    if rows:
                        for c in range(DC):
                            act.wait(v, (f"yh{c}", k), i)
                            dve.done(v.tensor_tensor(yT[1][:, k, c, :], pX[:, k, c, :], yT[0][:, k, c, :].bitcast(self.f32),
                                                     ALU.subtract), (f"yl{c}", k))
                    else:
                        dve.skip(v, i, [("yl0", k), ("yl1", k)])
                    if not up:
                        return dve.skip(v, i, [(f"o{j}", k) for j in range(4)])
                    pool.wait(v, ("xb", kb), i, db)
                    if not isinstance(i, int) or 2 * i + k >= 3:
                        v.wait_ge(s_out[kb], 16 * (i + db))
                    for j in range(4):
                        pe.wait(v, (f"O{j}", k), i)
                        dve.done(v.tensor_tensor(ob[:, kb, j, :], pO[:, j, 0:D], xb[:, kb, j, :], ALU.add), (f"o{j}", k))
                stream(v, body)

    def attn(self, x, out):
        with self.scope() as st:
            self.unsafe = st.sb("unsafe", [1, 1], self.i32)
            self.projections(x)
            self.exact_shift()
            self.attention()
            self.output(x, out)


def build(nc, ins, out):
    prog = Program(nc, ins, out)
    with prog.scope() as st:
        prog.load_constants(st)
        prog.ffn(ins["x"], prog.x1)
        prog.attn(prog.x1, prog.x2)
        prog.ffn(prog.x2, out)


def layout(inputs):
    a = {k: np.asarray(v) for k, v in inputs.items()}
    p = np.arange(P)
    same = (p[:, None] % E == p[None, :] % E)
    masks = np.concatenate([p[:, None] <= p[None, :], np.ones((P, P)), same], 1).astype(np.float32)
    route = np.concatenate([p[:, None] // 8 == p[None, :] // 8, p[:, None] % 8 == np.arange(P // WQ)[None, :],
                            p[:, None] % 8 == np.arange(8)[None, :], p[:, None]], 1).astype(np.float32)
    theta = (np.float32(1.0) / np.power(np.float32(10000.0), np.arange(0, HD, 2, dtype=np.float32) / np.float32(HD))).astype(np.float32)
    ang = np.arange(1, S + 1, dtype=np.float32)[:, None] * theta[None, :]
    ang = np.concatenate([ang, ang], 1).astype(np.float64)
    sign = np.where(np.arange(HD) < HD // 2, -1.0, 1.0)
    rope = np.stack([np.cos(ang), np.sin(ang) * sign], 1).astype(np.float32)
    t = lambda w: np.ascontiguousarray(w.T)
    te = lambda w: np.ascontiguousarray(np.transpose(w, (0, 2, 1)))
    return {
        "x": a["L0_attn_x"].reshape(N, D),
        "WqkT": np.ascontiguousarray(np.concatenate([a["L0_attn_Wq"], a["L0_attn_Wk"]], 0).T),
        "WvT": t(a["L0_attn_Wv"]), "WoT": t(a["L0_attn_Wo"]),
        "b_qkvo": np.concatenate([a["L0_attn_bq"], a["L0_attn_bk"], a["L0_attn_bv"], a["L0_attn_bo"]]).reshape(1, 4 * D),
        "gate_wT": t(a["L0_ffn_gate_w"]),
        "WgT": te(a["L0_ffn_Wg"]), "WuT": te(a["L0_ffn_Wu"]), "WdT": te(a["L0_ffn_Wd"]),
        "WsgT": t(a["L0_ffn_Ws_g"]), "WsuT": t(a["L0_ffn_Ws_u"]), "WsdT": t(a["L0_ffn_Ws_d"]),
        "c_ident": np.eye(P, dtype=np.float32),
        "c_masks": masks, "c_route": route,
        "c_bits": np.ascontiguousarray(np.broadcast_to(1 << np.arange(NBITS - 1, -1, -1), (P, NBITS))).astype(np.int32),
        "c_rope": np.ascontiguousarray(np.tile(rope.reshape(TPB, P, 2, HD).transpose(1, 0, 2, 3), (1, B, 1, 1))),
    }


def kernel(**inputs):
    import concourse.bacc as bacc
    from concourse import mybir
    from concourse.bass_utils import run_bass_kernel_spmd

    nc = bacc.Bacc("TRN2", target_bir_lowering=False, num_devices=1)
    arrays = layout(inputs)
    ins = {n: nc.dram_tensor(n, a.shape, mybir.dt.from_np(a.dtype), kind="ExternalInput").ap()
           for n, a in arrays.items()}
    out = nc.dram_tensor("out", [N, D], mybir.dt.float32, kind="ExternalOutput").ap()
    build(nc, ins, out)
    r = run_bass_kernel_spmd(nc, [arrays], core_ids=[0])
    return r.results[0]["out"].reshape(B, S, D)
```
